# Optimizing a Trainium2 kernel written in Bass

```python
import numpy as np
import jax
import jax.numpy as jnp

def _softmax(x, axis=-1):
    return jax.nn.softmax(x, axis=axis)

def _gelu(x):
    return jax.nn.gelu(x, approximate=True)

def _silu(x):
    return jax.nn.silu(x)

def _sigmoid(x):
    return jax.nn.sigmoid(x)

def _layernorm(x, axis=-1, eps=1e-05):
    m = jnp.mean(x, axis=axis, keepdims=True)
    v = jnp.var(x, axis=axis, keepdims=True)
    return (x - m) / jnp.sqrt(v + eps)

def _scatter_add(tgt, idx, src, axis=0):
    return tgt.at[idx].add(src)

def _segment_sum(src, seg, n):
    return jax.ops.segment_sum(src, seg, n)
kernel_name = 'mk_hybrid_d1_jaxref_r8_df8f11'

def setup_inputs(seed: int=0):
    np.random.seed(seed)
    _w = jnp.asarray

    def _L0_attn_a_setup():
        import jax, jax.numpy as jnp
        import numpy as np
        B, S, D, H = (4, 256, 128, 16)
        HD = D // H
        LN_EPS = 1e-05
        KERN_EPS = 1e-06

        def kernel_func(q, k):
            scores = jnp.einsum('bhqd,bhkd->bhqk', q, k) / jnp.sqrt(jnp.asarray(HD, q.dtype))
            w = jax.nn.relu(scores)
            return w / (jnp.sum(w, axis=-1, keepdims=True) + KERN_EPS)
        key = jax.random.key(seed)
        k1, k2, k3 = jax.random.split(key, 3)
        scale = 1.0 / np.sqrt(D)
        return {'x': jax.random.normal(k1, (B, S, D), dtype=jnp.float32), 'w_qkv': jax.random.normal(k2, (D, 3 * D), dtype=jnp.float32) * scale, 'w_out': jax.random.normal(k3, (D, D), dtype=jnp.float32) * scale, 'b_out': jnp.zeros((D,), dtype=jnp.float32), 'gamma': jnp.ones((D,), dtype=jnp.float32), 'beta': jnp.zeros((D,), dtype=jnp.float32)}
    _L0_attn_a_in = _L0_attn_a_setup()

    def _L0_attn_b_setup():
        import jax, jax.numpy as jnp
        import numpy as np
        from jax import lax
        B, L, D = (2, 256, 128)
        E, N, D_DELTA, D_CONV = (256, 16, 64, 4)
        EPS = 1e-05
        key = jax.random.key(seed)
        ks = jax.random.split(key, 16)
        s = lambda fan_in: 1.0 / np.sqrt(fan_in)
        return {'resid': jax.random.normal(ks[0], (B, L, D), jnp.float32), 'norm_w': jnp.ones((D,), jnp.float32), 'skip_w': jax.random.normal(ks[1], (E, D), jnp.float32) * s(D), 'in_w': jax.random.normal(ks[2], (E, D), jnp.float32) * s(D), 'conv_w': jax.random.normal(ks[3], (E, 1, D_CONV), jnp.float32) * s(D_CONV), 'conv_b': jnp.zeros((E,), jnp.float32), 'wd1': jax.random.normal(ks[4], (D_DELTA, E), jnp.float32) * s(E), 'wd2': jax.random.normal(ks[5], (E, D_DELTA), jnp.float32) * s(D_DELTA), 'wd2_b': jnp.zeros((E,), jnp.float32), 'wb': jax.random.normal(ks[6], (N, E), jnp.float32) * s(E), 'wc': jax.random.normal(ks[7], (N, E), jnp.float32) * s(E), 'A_log': jnp.log(jax.random.uniform(ks[8], (E, N), jnp.float32, 0.5, 1.5)), 'W_D': jnp.ones((E,), jnp.float32), 'out_w': jax.random.normal(ks[9], (D, E), jnp.float32) * s(E)}
    _L0_attn_b_in = _L0_attn_b_setup()

    def _L0_ffn_setup():
        import jax, jax.numpy as jnp
        import numpy as np
        E = 8
        TOPK = 2
        H = 128
        I = 128
        ISH = I * 2
        B, S = (2, 128)
        key = jax.random.key(seed)
        ks = jax.random.split(key, 7)
        s = 0.02
        return {'hidden_states': jax.random.normal(ks[0], (B, S, H), jnp.float32), 'w_router': jax.random.normal(ks[1], (H, E), jnp.float32) * s, 'fc1_w': jax.random.normal(ks[2], (E, H, 2 * I), jnp.float32) * s, 'fc2_w': jax.random.normal(ks[3], (E, I, H), jnp.float32) * s, 'gate_w': jax.random.normal(ks[4], (H, ISH), jnp.float32) * s, 'up_w': jax.random.normal(ks[5], (H, ISH), jnp.float32) * s, 'down_w': jax.random.normal(ks[6], (ISH, H), jnp.float32) * s}
    _L0_ffn_in = _L0_ffn_setup()
    _d = {'L0_attn_a_x': _L0_attn_a_in['x'], 'L0_attn_a_w_qkv': _L0_attn_a_in['w_qkv'], 'L0_attn_a_w_out': _L0_attn_a_in['w_out'], 'L0_attn_a_b_out': _L0_attn_a_in['b_out'], 'L0_attn_a_gamma': _L0_attn_a_in['gamma'], 'L0_attn_a_beta': _L0_attn_a_in['beta'], 'L0_attn_b_norm_w': _L0_attn_b_in['norm_w'], 'L0_attn_b_skip_w': _L0_attn_b_in['skip_w'], 'L0_attn_b_in_w': _L0_attn_b_in['in_w'], 'L0_attn_b_conv_w': _L0_attn_b_in['conv_w'], 'L0_attn_b_conv_b': _L0_attn_b_in['conv_b'], 'L0_attn_b_wd1': _L0_attn_b_in['wd1'], 'L0_attn_b_wd2': _L0_attn_b_in['wd2'], 'L0_attn_b_wd2_b': _L0_attn_b_in['wd2_b'], 'L0_attn_b_wb': _L0_attn_b_in['wb'], 'L0_attn_b_wc': _L0_attn_b_in['wc'], 'L0_attn_b_A_log': _L0_attn_b_in['A_log'], 'L0_attn_b_W_D': _L0_attn_b_in['W_D'], 'L0_attn_b_out_w': _L0_attn_b_in['out_w'], 'L0_ffn_w_router': _L0_ffn_in['w_router'], 'L0_ffn_fc1_w': _L0_ffn_in['fc1_w'], 'L0_ffn_fc2_w': _L0_ffn_in['fc2_w'], 'L0_ffn_gate_w': _L0_ffn_in['gate_w'], 'L0_ffn_up_w': _L0_ffn_in['up_w'], 'L0_ffn_down_w': _L0_ffn_in['down_w']}
    _x0 = _d['L0_attn_a_x']
    _d['L0_attn_a_x'] = jax.random.normal(jax.random.fold_in(jax.random.key(seed), 1), (4, 1024, 128), dtype=_x0.dtype)
    del _x0
    return _d

def reference(L0_attn_a_x, L0_attn_a_w_qkv, L0_attn_a_w_out, L0_attn_a_b_out, L0_attn_a_gamma, L0_attn_a_beta, L0_attn_b_norm_w, L0_attn_b_skip_w, L0_attn_b_in_w, L0_attn_b_conv_w, L0_attn_b_conv_b, L0_attn_b_wd1, L0_attn_b_wd2, L0_attn_b_wd2_b, L0_attn_b_wb, L0_attn_b_wc, L0_attn_b_A_log, L0_attn_b_W_D, L0_attn_b_out_w, L0_ffn_w_router, L0_ffn_fc1_w, L0_ffn_fc2_w, L0_ffn_gate_w, L0_ffn_up_w, L0_ffn_down_w):

    def _L0_attn_a_ref(x, w_qkv, w_out, b_out, gamma, beta):
        import jax, jax.numpy as jnp
        import numpy as np
        B, S, D, H = (4, 256, 128, 16)
        HD = D // H
        LN_EPS = 1e-05
        KERN_EPS = 1e-06

        def kernel_func(q, k):
            scores = jnp.einsum('bhqd,bhkd->bhqk', q, k) / jnp.sqrt(jnp.asarray(HD, q.dtype))
            w = jax.nn.relu(scores)
            return w / (jnp.sum(w, axis=-1, keepdims=True) + KERN_EPS)
        Bx, Sx, _ = x.shape
        qkv = (x @ w_qkv).reshape(Bx, Sx, H, 3 * HD)
        q, k, v = jnp.split(qkv, 3, axis=-1)
        q = q.transpose(0, 2, 1, 3)
        k = k.transpose(0, 2, 1, 3)
        v = v.transpose(0, 2, 1, 3)
        attn = kernel_func(q, k)
        out = jnp.einsum('bhqk,bhkd->bhqd', attn, v)
        out = out.transpose(0, 2, 1, 3).reshape(Bx, Sx, D)
        out = out @ w_out + b_out
        y = x + out
        mu = jnp.mean(y, axis=-1, keepdims=True)
        var = jnp.var(y, axis=-1, keepdims=True)
        return (y - mu) * jax.lax.rsqrt(var + LN_EPS) * gamma + beta

    def _L0_attn_b_ref(resid, norm_w, skip_w, in_w, conv_w, conv_b, wd1, wd2, wd2_b, wb, wc, A_log, W_D, out_w):
        import jax, jax.numpy as jnp
        import numpy as np
        from jax import lax
        B, L, D = (2, 256, 128)
        E, N, D_DELTA, D_CONV = (256, 16, 64, 4)
        EPS = 1e-05
        Bt, Lt, Dt = resid.shape
        x = resid * lax.rsqrt(jnp.mean(resid * resid, -1, keepdims=True) + EPS) * norm_w
        skip = x @ skip_w.T
        xe = x @ in_w.T
        xt = xe.transpose(0, 2, 1)
        xc = lax.conv_general_dilated(xt, conv_w, window_strides=(1,), padding=[(D_CONV - 1, 0)], feature_group_count=conv_w.shape[0])
        xc = xc + conv_b[None, :, None]
        xs = jax.nn.silu(xc.transpose(0, 2, 1))
        delta = jax.nn.softplus(xs @ wd1.T @ wd2.T + wd2_b)
        A = -jnp.exp(A_log)
        Bm = xs @ wb.T
        Cm = xs @ wc.T

        def step(h, inp):
            d_l, b_l, c_l, x_l = inp
            h = jnp.exp(d_l[:, :, None] * A) * h + (d_l * x_l)[:, :, None] * b_l[:, None, :]
            y_l = jnp.einsum('ben,bn->be', h, c_l)
            return (h, y_l)
        h0 = jnp.zeros((Bt, xs.shape[-1], A.shape[-1]), xs.dtype)
        _, ys = lax.scan(step, h0, (delta.transpose(1, 0, 2), Bm.transpose(1, 0, 2), Cm.transpose(1, 0, 2), xs.transpose(1, 0, 2)))
        y = ys.transpose(1, 0, 2)
        y = y + xs * W_D
        y = y * jax.nn.silu(skip)
        y = y @ out_w.T
        return resid + y

    def _L0_ffn_ref(hidden_states, w_router, fc1_w, fc2_w, gate_w, up_w, down_w):
        import jax, jax.numpy as jnp
        import numpy as np
        E = 8
        TOPK = 2
        H = 128
        I = 128
        ISH = I * 2
        B, S = (2, 128)
        orig_shape = hidden_states.shape
        x = hidden_states.reshape(-1, orig_shape[-1])
        logits = x @ w_router
        top_logits, top_idx = jax.lax.top_k(logits, TOPK)
        scores = jax.nn.softmax(top_logits, axis=-1)
        flat_idx = top_idx.reshape(-1)
        sorted_idx = jnp.argsort(flat_idx)
        permuted = x[sorted_idx // TOPK]
        eid = flat_idx[sorted_idx]
        out_perm = jnp.zeros((permuted.shape[0], orig_shape[-1]), x.dtype)
        for e in range(E):
            m = (eid == e).astype(x.dtype)[:, None]
            h1 = permuted * m @ fc1_w[e]
            proj, gate = jnp.split(h1, 2, axis=-1)
            out_perm = out_perm + jax.nn.silu(proj) * gate @ fc2_w[e]
        unperm = jnp.zeros_like(out_perm).at[sorted_idx].set(out_perm)
        moe_out = (unperm.reshape(-1, TOPK, orig_shape[-1]) * scores[:, :, None]).sum(axis=1)
        moe_out = moe_out.reshape(orig_shape)
        shared = jax.nn.silu(hidden_states @ gate_w) * (hidden_states @ up_w) @ down_w
        return moe_out + shared
    x = L0_attn_a_x
    x = x + _L0_attn_a_ref(_layernorm(x, axis=-1), L0_attn_a_w_qkv, L0_attn_a_w_out, L0_attn_a_b_out, L0_attn_a_gamma, L0_attn_a_beta)
    x = x + _L0_ffn_ref(_layernorm(x, axis=-1), L0_ffn_w_router, L0_ffn_fc1_w, L0_ffn_fc2_w, L0_ffn_gate_w, L0_ffn_up_w, L0_ffn_down_w)
    x = x + _L0_attn_b_ref(_layernorm(x, axis=-1), L0_attn_b_norm_w, L0_attn_b_skip_w, L0_attn_b_in_w, L0_attn_b_conv_w, L0_attn_b_conv_b, L0_attn_b_wd1, L0_attn_b_wd2, L0_attn_b_wd2_b, L0_attn_b_wb, L0_attn_b_wc, L0_attn_b_A_log, L0_attn_b_W_D, L0_attn_b_out_w)
    x = x + _L0_ffn_ref(_layernorm(x, axis=-1), L0_ffn_w_router, L0_ffn_fc1_w, L0_ffn_fc2_w, L0_ffn_gate_w, L0_ffn_up_w, L0_ffn_down_w)
    return x

_drawn_inputs = setup_inputs


def setup_inputs(seed=0):
    import zlib

    import numpy as np

    out = dict(_drawn_inputs(seed))
    spreads = {'L0_attn_a_b_out': (0.0, 0.1),
     'L0_attn_a_gamma': (1.0, 0.2),
     'L0_attn_a_beta': (0.0, 0.1),
     'L0_attn_b_norm_w': (1.0, 0.2),
     'L0_attn_b_conv_b': (0.0, 0.1),
     'L0_attn_b_wd2_b': (0.0, 0.696),
     'L0_attn_b_W_D': (1.0, 0.6)}
    factors = {'L0_ffn_w_router': 8.0,
     'L0_ffn_fc1_w': 8.0,
     'L0_ffn_fc2_w': 8.0,
     'L0_ffn_gate_w': 8.0,
     'L0_ffn_up_w': 8.0,
     'L0_ffn_down_w': 8.0}
    for name, (base, spread) in spreads.items():
        noise = np.random.default_rng([zlib.crc32(name.encode()), seed]).standard_normal(out[name].shape)
        drawn = base * np.exp(spread * noise) if base else spread * noise
        out[name] = jnp.asarray(drawn.astype(out[name].dtype))
    for name, factor in factors.items():
        out[name] = (out[name] * factor).astype(out[name].dtype)
    return out
```

```python
from contextlib import ExitStack

import concourse.bass as bass
from concourse import mybir

F32 = mybir.dt.float32
BF16 = mybir.dt.bfloat16
ALU = mybir.AluOpType
ACT = mybir.ActivationFunctionType
AX_X = mybir.AxisListType.X
ds = bass.ds

P = 128
B, S, D = 4, 1024, 128
H, HD = 16, 8
TB = S // P
HG = 4
GB = H // HG
NG = B * GB
STRIP = 32
GW = HG * HD
PARTS = 3
Q_TERM = (0, 0, 0, 1, 1, 2)
K_TERM = (0, 1, 2, 0, 1, 0)
NT = len(Q_TERM)
HALF = 512
STEPS = 2 * TB
CH = 512
NCH = B * S // CH
CT = CH // P
E, TOPK, I = 8, 2, 128
NE = E + 2
ME, MN, MR, MC = 256, 16, 64, 4
MT = ME // P
UNITS = MN * MT
LN_EPS = 1e-5
KERN_EPS = 1e-6


class Names:
    pass


class Chain:

    def __init__(self, eng, sem, per, turn):
        self.eng, self.sem, self.per, self.turn, self.n = eng, sem, per, turn, 0

    def did(self, ins):
        ins.then_inc(self.sem, 1)
        self.n += 1

    def wait(self):
        self.eng.wait_ge(self.sem, self.turn * self.per + self.n)

    def end(self):
        assert self.n == self.per, self.n


NORM_STEPS = 5


def gather_stats(dve, step, stats, moments, mean, var_eps):
    even, odd = stats[:, :, 0:3], stats[:, :, 3:6]
    step.did(dve.tensor_tensor(moments[:, :, 0:3], even, odd, ALU.add))
    step.did(dve.tensor_tensor(moments[:, :, 3:4], even[:, :, 1:2], odd[:, :, 1:2], ALU.subtract))
    step.wait()
    step.did(dve.tensor_scalar(mean[:, :], moments[:, :, 1], 0.5, None, ALU.mult))
    step.did(dve.tensor_tensor(moments[:, :, 4:5], moments[:, :, 3:4], moments[:, :, 3:4], ALU.mult))
    step.did(dve.tensor_scalar(moments[:, :, 5:6], moments[:, :, 2:3], 1.0 / D, LN_EPS, ALU.mult, ALU.add))
    step.wait()
    return dve.scalar_tensor_tensor(out=var_eps, in0=moments[:, :, 4], scalar=0.25, in1=moments[:, :, 5],
                                    op0=ALU.mult, op1=ALU.add)


def project_qkv(nc, k):
    with ExitStack() as ctx:
        sb = lambda n, s, d=F32: ctx.enter_context(nc.sbuf_tensor("qkv_" + n, s, d))
        pb = lambda n: ctx.enter_context(nc.psum_tensor("qkv_" + n, [P, S], F32))
        sem = lambda n: ctx.enter_context(nc.semaphore("qkv_" + n))
        stats = sb("stats", [P, TB, 6])
        moments = sb("moments", [P, TB, 8])
        mean = sb("mean", [P, TB])
        var_eps = sb("var_eps", [P, TB])
        rstd = sb("rstd", [P, TB])
        xn = sb("xn", [P, 2, TB, D])
        xnT = sb("xnT", [P, S])
        q_part = sb("q_part", [P, PARTS, S], BF16)
        k_part = sb("k_part", [P, PARTS, S], BF16)
        q_rest = sb("q_rest", [P, S])
        k_rest = sb("k_rest", [P, S])
        psT, psQ, psK, psV = pb("psT"), pb("psQ"), pb("psK"), pb("psV")
        dve_steps = sem("dve_steps")
        var_ready, rstd_ready = sem("var_ready"), sem("rstd_ready")
        xn_ready, xn_copied, xn_turned = sem("xn_ready"), sem("xn_copied"), sem("xn_turned")
        xnT_ready = sem("xnT_ready")
        q_ready, k_ready, v_ready = sem("q_ready"), sem("k_ready"), sem("v_ready")
        qk_taken, v_copied = sem("qk_taken"), sem("v_copied")
        first_ready, second_ready, third_ready = sem("first_ready"), sem("second_ready"), sem("third_ready")
        stored = sem("stored")
        block = ctx.enter_context(nc.Block())
        scale = float(HD) ** -0.5
        STORES = 2 * NT * 16

        @block.sync
        def _(sp):
            sp.sem_inc(stored, STORES)
            with sp.Fori(0, B) as b:
                for part, ready in enumerate((first_ready, second_ready, third_ready)):
                    sp.wait_ge(ready, b * 2 + 2)
                    for src, terms, dst in ((q_part, Q_TERM, k.q_terms), (k_part, K_TERM, k.k_terms)):
                        for t in range(NT):
                            if terms[t] == part:
                                out = dst[ds(b, 1), :, t].rearrange("o h d s -> (o h) d s")
                                sp.dma_start(out, src[:, part, :]).then_inc(stored, 16)
            sp.wait_ge(stored, (B + 1) * STORES)

        @block.gpsimd
        def _(pool):
            pool.wait_ge(k.consts_loaded, k.consts_total)
            with pool.Fori(0, B // 2) as i:
                for par in range(2):
                    b = i * 2 + par
                    pool.wait_ge(var_ready, b + 1)
                    pool.tensor_tensor(rstd[:, :], var_eps[:, :], k.minus_half[:, 0:TB], ALU.pow).then_inc(rstd_ready, 1)
                    pool.wait_ge(xn_ready, (b + 1) * TB)
                    bias = k.b_out[:, :].unsqueeze(1).broadcast_to([P, TB, D])
                    out = k.xn[:, ds(b * S, S)].rearrange("p (t d) -> p t d", d=D)
                    pool.tensor_tensor(out, xn[:, par], bias, ALU.add).then_inc(xn_copied, 1)

        @block.vector
        def _(dve):
            dve.wait_ge(k.x_loaded, B * 16)
            with dve.Fori(0, B // 2) as i:
                for par in range(2):
                    b = i * 2 + par
                    step = Chain(dve, dve_steps, TB + NORM_STEPS, b)
                    for j in range(TB):
                        step.did(dve.bn_stats(stats[:, j], k.x[:, ds((b * TB + j) * D, D)]))
                    step.wait()
                    gather_stats(dve, step, stats, moments, mean, var_eps[:, :]).then_inc(var_ready, 1)
                    step.end()
                    dve.wait_ge(rstd_ready, b + 1)
                    dve.wait_ge(xn_copied, b + 1)
                    dve.wait_ge(xn_turned, b + 1)
                    for j in range(TB):
                        dve.tensor_scalar(xn[:, par, j], k.x[:, ds((b * TB + j) * D, D)], mean[:, j:j + 1],
                                          rstd[:, j:j + 1], ALU.subtract, ALU.mult).then_inc(xn_ready, 1)
                    dve.wait_ge(first_ready, b * 2 + 1)
                    dve.scalar_tensor_tensor(out=q_rest[:, :], in0=psQ[:, :], scalar=scale, in1=q_part[:, 0],
                                             op0=ALU.mult, op1=ALU.subtract).then_inc(qk_taken, 1)
                    dve.wait_ge(first_ready, b * 2 + 2)
                    dve.tensor_tensor(k_rest[:, :], psK[:, :], k_part[:, 0], ALU.subtract).then_inc(qk_taken, 1)
                    dve.wait_ge(second_ready, b * 2 + 1)
                    dve.tensor_tensor(q_part[:, 2], q_rest[:, :], q_part[:, 1], ALU.subtract).then_inc(third_ready, 1)
                    dve.wait_ge(second_ready, b * 2 + 2)
                    dve.tensor_tensor(k_part[:, 2], k_rest[:, :], k_part[:, 1], ALU.subtract).then_inc(third_ready, 1)

        @block.scalar
        def _(act):
            with act.Fori(0, B) as b:
                act.wait_ge(xn_turned, b + 3)
                act.wait_ge(v_ready, b + 1)
                act.copy(xnT[:, :], psT[:, :]).then_inc(xnT_ready, 1)
                act.wait_ge(q_ready, b + 1)
                act.wait_ge(stored, (b + 1) * STORES)
                act.mul(q_part[:, 0], psQ[:, :], scale).then_inc(first_ready, 1)
                act.wait_ge(k_ready, b + 1)
                act.copy(k_part[:, 0], psK[:, :]).then_inc(first_ready, 1)
                act.wait_ge(v_ready, b + 2)
                v_out = k.v[:, ds(b * S, S)].rearrange("p (g t c) -> p t g c", g=GB, c=GW)
                act.copy(v_out, psV[:, :].rearrange("p (t g c) -> p t g c", t=TB, g=GB)).then_inc(v_copied, 1)
                act.wait_ge(qk_taken, b * 2 + 2)
                act.copy(q_part[:, 1], q_rest[:, :]).then_inc(second_ready, 1)
                act.wait_ge(qk_taken, b * 2 + 3)
                act.copy(k_part[:, 1], k_rest[:, :]).then_inc(second_ready, 1)

        @block.tensor
        def _(pe):
            pe.sem_inc(xn_turned, 2)
            pe.sem_inc(xn_copied, 2)
            pe.sem_inc(v_ready, 1)
            pe.sem_inc(xnT_ready, 1)
            pe.sem_inc(qk_taken, 1)
            pe.sem_inc(v_copied, 1)
            pe.wait_ge(k.attn_weights_loaded, k.attn_weights_total)
            pe.wait_ge(k.consts_loaded, k.consts_total)
            with pe.Fori(0, B // 2) as i:
                for par in range(2):
                    b = i * 2 + par
                    pe.wait_ge(xn_ready, (b + 1) * TB)
                    pe.wait_ge(xnT_ready, b + 1)
                    for j in range(TB):
                        mm = pe.transpose(psT[:, j * P:(j + 1) * P], xn[:, par, j], k.ident[:, :])
                    mm.then_inc(xn_turned, 1)
                    pe.wait_ge(xnT_ready, b + 2)
                    pe.wait_ge(qk_taken, b * 2 + 1)
                    for ps, w, done in ((psQ, k.w_q, q_ready), (psK, k.w_k, k_ready)):
                        for h in range(2):
                            cols = slice(h * HALF, (h + 1) * HALF)
                            mm = pe.matmul(ps[:, cols], w, xnT[:, cols], start=True, stop=True)
                        mm.then_inc(done, 1)
                    pe.wait_ge(v_copied, b + 1)
                    for j in range(TB):
                        cols = slice(j * P, (j + 1) * P)
                        mm = pe.matmul(psV[:, cols], xnT[:, cols], k.w_v, start=True, stop=True)
                    mm.then_inc(v_ready, 1)


def attend(nc, k):
    with ExitStack() as ctx:
        sb = lambda n, s, d=F32: ctx.enter_context(nc.sbuf_tensor("att_" + n, s, d))
        pb = lambda n, w: ctx.enter_context(nc.psum_tensor("att_" + n, [P, w], F32))
        sem = lambda n: ctx.enter_context(nc.semaphore("att_" + n))
        q_in = sb("q_in", [P, 2, HG // 2, S], BF16)
        k_in = sb("k_in", [P, 2, HG, S], BF16)
        v_in = sb("v_in", [P, 2, TB, HG, STRIP])
        w = sb("w", [P, 2, HG, HALF])
        oT = sb("oT", [P, 2, HALF])
        den = sb("den", [P, CT, HG])
        inv_den = sb("inv_den", [P, CT, HG])
        psA, psB = pb("psA", 2 * HALF), pb("psB", 2 * HALF)
        psO = [pb("psO0", HALF), pb("psO1", HALF)]
        psT = pb("psT", HALF)
        zeroed, ones_set = sem("zeroed"), sem("ones_set")
        qk_loaded, v_ready = [sem("qk_loaded0"), sem("qk_loaded1")], sem("v_ready")
        scored_a, scored_b = sem("scored_a"), sem("scored_b")
        relu_a, relu_b = sem("relu_a"), sem("relu_b")
        summed = sem("summed")
        o_copied, o_turned, o_done = sem("o_copied"), sem("o_turned"), sem("o_done")
        dve_steps = sem("dve_steps")
        block = ctx.enter_context(nc.Block())
        rows = NT * HD
        q_src = k.q_terms.rearrange("b (g p a) t d s -> (b g) p a (t d) s", g=GB, a=2)
        k_src = k.k_terms.rearrange("b (g p a) t d s -> (b g) p a (t d) s", g=GB, a=2)
        BODY = 2 * STEPS
        AHEAD = 2 * STEPS
        LAST = NG // 2 - 1

        @block.sync
        def _(sp):
            sp.wait_ge(zeroed, 2)
            with sp.Fori(0, NG // 2) as i:
                for par in range(2):
                    n = i * 2 + par
                    sp.wait_ge(scored_b, (n + 1) * STEPS)
                    for a in range(2):
                        r = slice(64 * a, 64 * a + rows)
                        sp.dma_start(q_in[r, par], q_src[ds(n, 1), :, a].rearrange("o p r s -> r (o p) s")).then_inc(qk_loaded[par], 16)
                        out = k_in[r, par].rearrange("r (p a) s -> r p a s", a=2)[:, :, a]
                        sp.dma_start(out, k_src[ds(n, 1), :, a].rearrange("o p r s -> r (o p) s")).then_inc(qk_loaded[par], 16)

        @block.gpsimd
        def _(pool):
            pool.memset(k_in[:, :, :, :], 0.0).then_inc(zeroed, 1)
            pool.memset(v_in[:, :, :, :, :], 0.0).then_inc(ones_set, 1)
            pool.wait_ge(ones_set, 1)
            pool.memset(v_in[:, :, :, :, HD:HD + 1], 1.0).then_inc(ones_set, 1)
            with pool.Fori(0, NG // 2) as i:
                for par in range(2):
                    n = i * 2 + par
                    pool.wait_ge(summed, (n + 1) * STEPS)
                    src = k.v[:, ds(n * TB * GW, TB * GW)].rearrange("p (t h d) -> p t h d", t=TB, d=HD)
                    pool.tensor_copy(v_in[:, par, :, :, 0:HD], src).then_inc(v_ready, 1)

        @block.scalar
        def _(act):
            def relu(m, buf):
                act.wait_ge(scored_a, m + 1)
                act.wait_ge(summed, AHEAD + m - 1)
                act.activation(w[:, buf, 0:2], psA[:, :].rearrange("p (h q) -> p h q", h=2), ACT.Relu).then_inc(relu_a, 1)

            def body(i, last):
                for q in range(BODY):
                    m = i * BODY + q
                    if not (last and q == BODY - 1):
                        relu(m + 1, (q + 1) % 2)
                    if q % TB == TB - 1:
                        o, n = q // TB % 2, i * 4 + q // TB
                        act.wait_ge(summed, AHEAD + m + 1)
                        act.wait_ge(o_turned, n + 1)
                        act.copy(oT[:, o], psO[o][:, :]).then_inc(o_copied, 1)

            relu(0, 0)
            with act.Fori(0, LAST) as i:
                body(i, False)
            body(LAST, True)

        @block.vector
        def _(dve):
            dve.memset(q_in[:, :, :, :], 0.0).then_inc(zeroed, 1)
            dve.wait_ge(ones_set, 2)

            def relu(m, buf):
                dve.wait_ge(scored_b, AHEAD + m + 1)
                dve.wait_ge(summed, AHEAD + m - 1)
                dve.tensor_scalar(w[:, buf, 2:4], psB[:, :].rearrange("p (h q) -> p h q", h=2), 0.0, None,
                                  ALU.max).then_inc(relu_b, 1)

            def normalise(i, j):
                n = i * 4 + j
                t = psT[:, :].rearrange("p (t h c) -> p t h c", t=CT, h=HG)
                dve.wait_ge(o_turned, n + 3)
                dve.tensor_scalar(den[:, :, :], t[:, :, :, HD], KERN_EPS, None, ALU.add).then_inc(dve_steps, 1)
                dve.wait_ge(dve_steps, n * 2 + 1)
                dve.reciprocal(inv_den[:, :, :], den[:, :, :]).then_inc(dve_steps, 1)
                dve.wait_ge(dve_steps, n * 2 + 2)
                out = k.att[:, ds(n * CT * GW, CT * GW)].rearrange("p (m d) -> p m d", d=HD)
                dve.tensor_tensor(out, t[:, :, :, 0:HD].rearrange("p t h d -> p (t h) d"),
                                  inv_den[:, :, :].rearrange("p t h -> p (t h)").unsqueeze(2).broadcast_to([P, CT * HG, HD]),
                                  ALU.mult).then_inc(o_done, 1)

            def body(i, last):
                for q in range(BODY):
                    if not (last and q == BODY - 1):
                        relu(i * BODY + q + 1, (q + 1) % 2)
                    if q % TB == 4 and q > TB:
                        normalise(i, q // TB - 1)
                normalise(i, 3)

            relu(0, 0)
            with dve.Fori(0, LAST) as i:
                body(i, False)
            body(LAST, True)

        @block.tensor
        def _(pe):
            pe.sem_inc(scored_b, AHEAD)
            pe.sem_inc(summed, AHEAD)
            pe.sem_inc(o_turned, 2)
            pe.sem_inc(o_copied, 2)
            pe.sem_inc(o_done, 1)
            pe.sem_inc(relu_a, 1)
            pe.sem_inc(relu_b, 1)

            def scores(n_of_par, m, q):
                par, qh, kt = q // STEPS % 2, q // TB % 2, q % TB
                if q % STEPS == 0:
                    pe.wait_ge(qk_loaded[par], (n_of_par + 1) * 64)
                for ps, pair, taken, done in ((psA, 0, relu_a, scored_a), (psB, 1, relu_b, scored_b)):
                    pe.wait_ge(taken, m + 1)
                    for a in range(2):
                        mm = pe.matmul(ps[:, a * HALF:(a + 1) * HALF], k_in[:, par, 2 * pair + a, kt * P:(kt + 1) * P],
                                       q_in[:, par, pair, qh * HALF:(qh + 1) * HALF], start=True, stop=True)
                    mm.then_inc(done, 1)

            def values(i, q):
                par, o, kt = q // STEPS, q // TB % 2, q % TB
                m = i * BODY + q
                if q % STEPS == 0:
                    pe.wait_ge(v_ready, i * 2 + par + 1)
                if kt == 0:
                    pe.wait_ge(o_copied, i * 4 + q // TB + 1)
                pe.wait_ge(relu_a, m + 2)
                pe.wait_ge(relu_b, m + 2)
                for h in range(HG):
                    mm = pe.matmul(psO[o][h * STRIP:(h + 1) * STRIP, :], v_in[:, par, kt, h], w[:, q % 2, h],
                                   start=(kt == 0), stop=(kt == TB - 1))
                mm.then_inc(summed, 1)

            def turn(i, j):
                n = i * 4 + j
                pe.wait_ge(o_copied, n + 3)
                pe.wait_ge(o_done, n + 1)
                for t in range(CT):
                    mm = pe.transpose(psT[:, t * P:(t + 1) * P], oT[:, j % 2, t * P:(t + 1) * P], k.ident[:, :])
                mm.then_inc(o_turned, 1)

            def body(i, last):
                for q in range(BODY):
                    if not (last and q == BODY - 1):
                        scores(i + (q + 1) // BODY, i * BODY + q + 1, (q + 1) % BODY)
                    values(i, q)
                    if q % TB == 2 and q > TB:
                        turn(i, q // TB - 1)
                turn(i, 3)

            scores(0, 0, 0)
            with pe.Fori(0, LAST) as i:
                body(i, False)
            body(LAST, True)


def feed_forward(nc, k, name, after_attention):
    with ExitStack() as ctx:
        sb = lambda n, s, d=F32: ctx.enter_context(nc.sbuf_tensor(name + "_" + n, s, d))
        pb = lambda n: ctx.enter_context(nc.psum_tensor(name + "_" + n, [P, CH], F32))
        sem = lambda n: ctx.enter_context(nc.semaphore(name + "_" + n))
        heads = sb("heads", [P, CT, D])
        headsT = sb("headsT", [P, CH])
        y = sb("y", [P, CT, D])
        yn = sb("yn", [P, CT, D])
        xn = sb("xn", [P, CT, D])
        xnT = sb("xnT", [P, 2, CH])
        stats = sb("stats", [P, CT, 6])
        moments = sb("moments", [P, CT, 8])
        mean = sb("mean", [P, CT])
        var_eps = sb("var_eps", [P, 2, CT])
        rstd = sb("rstd", [P, 2, CT])
        logit = sb("logit", [P, CT, E])
        above = sb("above", [P, CT, E, E])
        equal = sb("equal", [P, CT, E, E])
        rank = sb("rank", [P, CT, E])
        taken = sb("taken", [P, CT, E])
        taken_logit = sb("taken_logit", [P, CT, E])
        logit_sum = sb("logit_sum", [P, CT])
        margin = sb("margin", [P, CT, E])
        half_tanh = sb("half_tanh", [P, CT, E])
        share = sb("share", [P, CT, E])
        rest = sb("rest", [P, CT, E])
        parts = sb("parts", [P, CT, P], BF16)
        partsT = sb("partsT", [P, 2, CH], BF16)
        silu = sb("silu", [P, 2, CH])
        scaled = sb("scaled", [P, 2, CH])
        hidden = sb("hidden", [P, 2, CH])
        oT = sb("oT", [P, CH])
        psP = [pb("psP0"), pb("psP1")]
        psG = [pb("psG0"), pb("psG1")]
        psC, psO, psX, psY = pb("psC"), pb("psO"), pb("psX"), pb("psY")
        in_steps, out_steps = sem("in_steps"), sem("out_steps")
        pool_steps = sem("pool_steps")
        parts_zeroed = sem("parts_zeroed")
        heads_ready, heads_turned, headsT_ready = sem("heads_ready"), sem("heads_turned"), sem("headsT_ready")
        projected, y_taken, yn_ready, x_added = sem("projected"), sem("y_taken"), sem("yn_ready"), sem("x_added")
        var_ready, rstd_ready = sem("var_ready"), sem("rstd_ready")
        y_var_ready, y_rstd_ready = sem("y_var_ready"), sem("y_rstd_ready")
        xn_ready, xn_turned, xnT_ready = sem("xn_ready"), sem("xn_turned"), sem("xnT_ready")
        routed, logit_taken, margin_ready, tanh_ready = sem("routed"), sem("logit_taken"), sem("margin_ready"), sem("tanh_ready")
        parts_ready, parts_turned, partsT_ready = sem("parts_ready"), sem("parts_turned"), sem("partsT_ready")
        p_ready, g_ready, c_ready = sem("p_ready"), sem("g_ready"), sem("c_ready")
        silu_ready, scaled_ready, hidden_ready = sem("silu_ready"), sem("scaled_ready"), sem("hidden_ready")
        down_steps, o_copied, o_turned, o_added = sem("down_steps"), sem("o_copied"), sem("o_turned"), sem("o_added")
        block = ctx.enter_context(nc.Block())
        LAST = NCH // 2 - 1

        def chunk(t, c):
            return t[:, ds(c * CT * D, CT * D)].rearrange("p (t d) -> p t d", d=D)

        @block.gpsimd
        def _(pool):
            pool.memset(parts[:, :, :], 0.0).then_inc(parts_zeroed, 1)
            pool.wait_ge(k.consts_loaded, k.consts_total)

            def gather(i, half):
                c = i * 2 + half
                pool.wait_ge(heads_turned, c + 1)
                src = k.att[:, ds(i * S, S)].rearrange("p (g t c) -> p t g c", g=GB, c=GW)[:, half * CT:(half + 1) * CT]
                pool.tensor_copy(heads[:, :, :].rearrange("p t (g c) -> p t g c", c=GW), src).then_inc(heads_ready, 1)

            def root(c, n, var, done):
                pool.wait_ge(var, c + 1)
                pool.tensor_tensor(rstd[:, n], var_eps[:, n], k.minus_half[:, 0:CT], ALU.pow).then_inc(done, 1)

            def add_normed(c):
                pool.wait_ge(yn_ready, (c + 1) * CT)
                gamma = k.gamma[:, :].unsqueeze(1).broadcast_to([P, CT, D])
                beta = k.beta[:, :].unsqueeze(1).broadcast_to([P, CT, D])
                pool.tensor_tensor(yn[:, :, :], yn[:, :, :], gamma, ALU.mult).then_inc(pool_steps, 1)
                pool.wait_ge(pool_steps, c * 2 + 1)
                pool.tensor_tensor(yn[:, :, :], yn[:, :, :], beta, ALU.add).then_inc(pool_steps, 1)
                pool.wait_ge(pool_steps, c * 2 + 2)
                pool.tensor_tensor(chunk(k.x, c), chunk(k.x, c), yn[:, :, :], ALU.add).then_inc(x_added, 1)

            def out_ready(i, half):
                c = i * 2 + half
                gather(i, half)
                root(c, 1, y_var_ready, y_rstd_ready)
                add_normed(c)

            def in_ready(c):
                root(c, 0, var_ready, rstd_ready)

            def body(i, par, last):
                if not (last and par):
                    in_ready(i * 2 + par + 1)
                if after_attention and not last:
                    out_ready(i + 1, par)

            if after_attention:
                out_ready(0, 0)
                out_ready(0, 1)
            in_ready(0)
            with pool.Fori(0, LAST) as i:
                body(i, 0, False)
                body(i, 1, False)
            body(LAST, 0, True)

        @block.scalar
        def _(act):
            def heads_out(c):
                act.wait_ge(heads_turned, c + 2)
                act.copy(headsT[:, :], psX[:, :]).then_inc(headsT_ready, 1)

            def xn_out(c, par):
                act.wait_ge(xn_turned, c + 2)
                act.copy(xnT[:, par], psX[:, :]).then_inc(xnT_ready, 1)

            def tanh(c):
                act.wait_ge(margin_ready, c + 1)
                act.activation(half_tanh[:, :, :], margin[:, :, :], ACT.Tanh).then_inc(tanh_ready, 1)

            def parts_out(c, par):
                act.wait_ge(parts_turned, c + 2)
                act.copy(partsT[:, par], psX[:, 0:CH // 2].bitcast(BF16)).then_inc(partsT_ready, 1)

            def gate(c, e):
                n = c * NE + e
                act.wait_ge(p_ready, n + 1)
                act.wait_ge(hidden_ready, n + 1)
                act.activation(silu[:, e % 2], psP[e % 2][:, :], ACT.Silu).then_inc(silu_ready, 1)

            def body(i, par, last):
                c = i * 2 + par
                for e in range(NE):
                    if e + 1 < NE:
                        gate(c, e + 1)
                    elif not (last and par):
                        gate(c + 1, 0)
                    if not (last and par):
                        if e == 1:
                            xn_out(c + 1, 1 - par)
                        if e == 4:
                            tanh(c + 1)
                        if e == 6:
                            parts_out(c + 1, 1 - par)
                    if after_attention and not last and e == 4:
                        heads_out(c + 2)
                act.wait_ge(down_steps, (c + 1) * NE + 2)
                act.wait_ge(o_turned, c + 1)
                act.copy(oT[:, :], psO[:, :]).then_inc(o_copied, 1)

            if after_attention:
                heads_out(0)
                heads_out(1)
            xn_out(0, 0)
            tanh(0)
            parts_out(0, 0)
            gate(0, 0)
            with act.Fori(0, LAST) as i:
                body(i, 0, False)
                body(i, 1, False)
            body(LAST, 0, True)
            body(LAST, 1, True)

        @block.vector
        def _(dve):
            dve.wait_ge(parts_zeroed, 1)
            dve.wait_ge(k.consts_loaded, k.consts_total)
            dve.wait_ge(k.x_loaded, B * 16)
            OUT_PER, IN_PER = CT + NORM_STEPS, CT + NORM_STEPS + 13

            def norm(c, n, step, src, out, var, root, done):
                for t in range(CT):
                    step.did(dve.bn_stats(stats[:, t], src(t)))
                step.wait()
                gather_stats(dve, step, stats, moments, mean, var_eps[:, n]).then_inc(var, 1)
                dve.wait_ge(root, c + 1)
                for t in range(CT):
                    dve.tensor_scalar(out[:, t], src(t), mean[:, t:t + 1], rstd[:, n, t:t + 1],
                                      ALU.subtract, ALU.mult).then_inc(done, 1)

            def out_norm(c):
                step = Chain(dve, out_steps, OUT_PER, c)
                dve.wait_ge(projected, c + 1)
                dve.tensor_tensor(y[:, :, :], psY[:, :].rearrange("p (t d) -> p t d", d=D), chunk(k.xn, c),
                                  ALU.add).then_inc(y_taken, 1)
                dve.wait_ge(y_taken, c + 2)
                dve.wait_ge(x_added, c + 1)
                norm(c, 1, step, lambda t: y[:, t], yn, y_var_ready, y_rstd_ready, yn_ready)
                step.end()

            def in_norm(c, step):
                if after_attention:
                    dve.wait_ge(x_added, c + 2)
                dve.wait_ge(xn_turned, c + 1)
                norm(c, 0, step, lambda t: k.x[:, ds((c * CT + t) * D, D)], xn, var_ready, rstd_ready, xn_ready)

            def rank_experts(c, step):
                dve.wait_ge(routed, c + 1)
                dve.tensor_copy(logit[:, :, :], psY[:, 0:CT * E].rearrange("p (t e) -> p t e", e=E)).then_inc(logit_taken, 1)
                dve.wait_ge(logit_taken, c + 2)
                of = logit[:, :, :].unsqueeze(3).broadcast_to([P, CT, E, E])
                other = logit[:, :, :].unsqueeze(2).broadcast_to([P, CT, E, E])
                before = k.before[:, :].rearrange("p (a b) -> p a b", a=E).unsqueeze(1).broadcast_to([P, CT, E, E])
                step.did(dve.tensor_tensor(above[:, :, :, :], other, of, ALU.is_gt))
                step.did(dve.tensor_tensor(equal[:, :, :, :], other, of, ALU.is_equal))
                step.wait()
                step.did(dve.tensor_tensor(equal[:, :, :, :], equal[:, :, :, :], before, ALU.mult))
                step.wait()
                step.did(dve.tensor_tensor(above[:, :, :, :], above[:, :, :, :], equal[:, :, :, :], ALU.add))
                step.wait()
                step.did(dve.tensor_reduce(rank[:, :, :], above[:, :, :, :], AX_X, ALU.add))
                step.wait()

            def take_experts(c, step):
                step.did(dve.tensor_scalar(taken[:, :, :], rank[:, :, :], TOPK - 0.5, None, ALU.is_lt))
                step.wait()
                step.did(dve.tensor_tensor(taken_logit[:, :, :], logit[:, :, :], taken[:, :, :], ALU.mult))
                step.wait()
                step.did(dve.tensor_reduce(logit_sum[:, :], taken_logit[:, :, :], AX_X, ALU.add))
                step.wait()
                dve.scalar_tensor_tensor(out=margin[:, :, :], in0=logit_sum[:, :].unsqueeze(2).broadcast_to([P, CT, E]),
                                         scalar=-0.5, in1=logit[:, :, :], op0=ALU.mult, op1=ALU.add).then_inc(margin_ready, 1)

            def split_shares(c, step):
                dve.wait_ge(tanh_ready, c + 1)
                step.did(dve.tensor_scalar(share[:, :, :], half_tanh[:, :, :], 0.5, 0.5, ALU.mult, ALU.add))
                step.wait()
                step.did(dve.tensor_tensor(share[:, :, :], share[:, :, :], taken[:, :, :], ALU.mult))
                step.wait()
                dve.wait_ge(parts_turned, c + 1)
                step.did(dve.tensor_copy(parts[:, :, 0:E], share[:, :, :]))
                step.wait()
                step.did(dve.tensor_tensor(rest[:, :, :], share[:, :, :], parts[:, :, 0:E], ALU.subtract))
                step.wait()
                step.did(dve.tensor_copy(parts[:, :, E:2 * E], rest[:, :, :]))
                step.wait()
                dve.tensor_tensor(parts[:, :, 2 * E:3 * E], rest[:, :, :], parts[:, :, E:2 * E],
                                  ALU.subtract).then_inc(parts_ready, 1)

            def hide(c, e):
                n = c * NE + e
                dve.wait_ge(silu_ready, n + 1)
                src = silu[:, e % 2]
                if e < E:
                    dve.wait_ge(c_ready, c * E + e + 1)
                    dve.tensor_tensor(scaled[:, e % 2], silu[:, e % 2], psC[:, :], ALU.mult).then_inc(scaled_ready, 1)
                    dve.wait_ge(scaled_ready, c * E + e + 2)
                    src = scaled[:, e % 2]
                dve.wait_ge(g_ready, n + 1)
                dve.wait_ge(down_steps, n + 1)
                dve.tensor_tensor(hidden[:, e % 2], src, psG[e % 2][:, :], ALU.mult).then_inc(hidden_ready, 1)

            def finish(c):
                dve.wait_ge(o_turned, c + 2)
                dve.tensor_tensor(chunk(k.x, c), chunk(k.x, c), psY[:, :].rearrange("p (t d) -> p t d", d=D),
                                  ALU.add).then_inc(o_added, 2)

            def body(i, par, last):
                c = i * 2 + par
                step = Chain(dve, in_steps, IN_PER, c + 1)
                for e in range(NE):
                    if e + 1 < NE:
                        hide(c, e + 1)
                    elif not (last and par):
                        hide(c + 1, 0)
                    if not (last and par):
                        if e == 0:
                            in_norm(c + 1, step)
                        if e == 3:
                            rank_experts(c + 1, step)
                            take_experts(c + 1, step)
                        if e == 4:
                            split_shares(c + 1, step)
                            step.end()
                    if after_attention and not last and e == 6:
                        out_norm(c + 2)
                finish(c)

            if after_attention:
                out_norm(0)
                out_norm(1)
            step = Chain(dve, in_steps, IN_PER, 0)
            in_norm(0, step)
            rank_experts(0, step)
            take_experts(0, step)
            split_shares(0, step)
            step.end()
            hide(0, 0)
            with dve.Fori(0, LAST) as i:
                body(i, 0, False)
                body(i, 1, False)
            body(LAST, 0, True)
            body(LAST, 1, True)

        @block.tensor
        def _(pe):
            for s, n in ((heads_turned, 1), (y_taken, 1), (x_added, 1), (xn_turned, 1), (parts_turned, 1),
                         (logit_taken, 1), (hidden_ready, 2), (down_steps, 2), (scaled_ready, 1), (o_turned, 1),
                         (o_copied, 1), (o_added, 2), (headsT_ready, 1), (xnT_ready, 1), (partsT_ready, 1)):
                pe.sem_inc(s, n)
            pe.wait_ge(k.ffn_weights_loaded, k.ffn_weights_total)
            pe.wait_ge(k.consts_loaded, k.consts_total)

            def turn_heads(c):
                pe.wait_ge(heads_ready, c + 1)
                for t in range(CT):
                    mm = pe.transpose(psX[:, t * P:(t + 1) * P], heads[:, t], k.ident[:, :])
                mm.then_inc(heads_turned, 1)

            def project_heads(c):
                pe.wait_ge(headsT_ready, c + 2)
                for t in range(CT):
                    cols = slice(t * P, (t + 1) * P)
                    mm = pe.matmul(psY[:, cols], headsT[:, cols], k.w_out[:, :], start=True, stop=True)
                mm.then_inc(projected, 1)

            def turn_xn(c):
                pe.wait_ge(xn_ready, (c + 1) * CT)
                for t in range(CT):
                    mm = pe.transpose(psX[:, t * P:(t + 1) * P], xn[:, t], k.ident[:, :])
                mm.then_inc(xn_turned, 1)

            def route(c, par):
                pe.wait_ge(xnT_ready, c + 2)
                pe.wait_ge(o_added, c + 1)
                for t in range(CT):
                    mm = pe.matmul(psY[:, t * E:(t + 1) * E], xnT[:, par, t * P:(t + 1) * P], k.w_router[:, :],
                                   start=True, stop=True)
                mm.then_inc(routed, 1)

            def turn_parts(c):
                pe.wait_ge(parts_ready, c + 1)
                pe.wait_ge(xnT_ready, c + 2)
                for t in range(CT):
                    mm = pe.transpose(psX[:, t * P // 2:(t + 1) * P // 2].bitcast(BF16), parts[:, t], k.ident_b[:, :])
                mm.then_inc(parts_turned, 1)

            def up(c, par, e):
                n = c * NE + e
                if e == 0:
                    pe.wait_ge(xnT_ready, c + 2)
                pe.wait_ge(hidden_ready, n + 1)
                pe.matmul(psP[e % 2][:, :], k.w1[:, e, 0:I], xnT[:, par], start=True, stop=True).then_inc(p_ready, 1)
                pe.matmul(psG[e % 2][:, :], k.w1[:, e, I:2 * I], xnT[:, par], start=True, stop=True).then_inc(g_ready, 1)
                if e < E:
                    if e == 0:
                        pe.wait_ge(partsT_ready, c + 2)
                    pe.wait_ge(scaled_ready, c * E + e + 1)
                    pe.matmul(psC[:, :], k.spread[:, e], partsT[:, par], start=True, stop=True).then_inc(c_ready, 1)

            def down(c, e):
                n = c * NE + e
                pe.wait_ge(hidden_ready, n + 3)
                if e == 0:
                    pe.wait_ge(o_copied, c + 1)
                mm = pe.matmul(psO[:, :], k.w2[:, e], hidden[:, e % 2], start=(e == 0), stop=(e == NE - 1))
                mm.then_inc(down_steps, 1)

            def turn_out(c):
                pe.wait_ge(o_copied, c + 2)
                for t in range(CT):
                    mm = pe.transpose(psY[:, t * P:(t + 1) * P], oT[:, t * P:(t + 1) * P], k.ident[:, :])
                mm.then_inc(o_turned, 1)

            def body(i, par, last):
                c = i * 2 + par
                for e in range(NE):
                    if e + 2 < NE:
                        up(c, par, e + 2)
                    elif not (last and par):
                        up(c + 1, 1 - par, e + 2 - NE)
                    down(c, e)
                    if not (last and par):
                        if e == 1:
                            turn_xn(c + 1)
                        if e == 3:
                            route(c + 1, 1 - par)
                    if after_attention and not last:
                        if e == 4:
                            turn_heads(c + 2)
                        if e == 6:
                            pe.wait_ge(logit_taken, c + 3)
                            project_heads(c + 2)
                    if not (last and par) and e == 6:
                        turn_parts(c + 1)
                if after_attention and not last:
                    pe.wait_ge(y_taken, c + 4)
                turn_out(c)

            if after_attention:
                turn_heads(0)
                project_heads(0)
                turn_heads(1)
                pe.wait_ge(y_taken, 2)
                project_heads(1)
                pe.wait_ge(y_taken, 3)
            turn_xn(0)
            route(0, 0)
            turn_parts(0)
            up(0, 0, 0)
            up(0, 0, 1)
            with pe.Fori(0, LAST) as i:
                body(i, 0, False)
                body(i, 1, False)
            body(LAST, 0, True)
            body(LAST, 1, True)


def state_space(nc, k):
    with ExitStack() as ctx:
        sb = lambda n, s, d=F32: ctx.enter_context(nc.sbuf_tensor("ssm_" + n, s, d))
        sem = lambda n: ctx.enter_context(nc.semaphore("ssm_" + n))
        PAD = 4
        stats = sb("stats", [P, TB, 6])
        moments = sb("moments", [P, TB, 8])
        mean, var_eps, rstd = sb("mean", [P, TB]), sb("var_eps", [P, TB]), sb("rstd", [P, TB])
        square = sb("square", [P, D])
        square_sum, ms_eps, rrms = sb("square_sum", [P, TB]), sb("ms_eps", [P, TB]), sb("rrms", [P, TB])
        resid = sb("resid", [P, TB, D])
        xr = sb("xr", [P, TB, D])
        xT = sb("xT", [P, PAD + S])
        gate = sb("gate", [P, MT, S])
        xs = sb("xs", [P, MT, S])
        low = sb("low", [P, S])
        bc = sb("bc", [2 * MN, S])
        z = sb("z", [P, MT, S])
        soft = sb("soft", [P, S])
        delta = sb("delta", [P, MT, S])
        dx = sb("dx", [P, MT, S])
        b_all = sb("b_all", [P, 2, S])
        c_all = sb("c_all", [P, 2, S])
        decay = sb("decay", [P, 2, S])
        feed = sb("feed", [P, 3, S])
        state = sb("state", [P, 2, S])
        part = sb("part", [P, 2, S])
        conv_in = sb("conv_in", [P, MC, ME])
        neg_a = sb("neg_a", [P, MT, MN])
        psY = ctx.enter_context(nc.psum_tensor("ssm_psY", [P, MT, S], F32))
        ps = [ctx.enter_context(nc.psum_tensor(f"ssm_ps{j}", [P, S], F32)) for j in range(2)]
        folded, exp_a, a_ready, padded = sem("folded"), sem("exp_a"), sem("a_ready"), sem("padded")
        dve_steps = sem("dve_steps")
        var_ready, rstd_ready, resid_ready = sem("var_ready"), sem("rstd_ready"), sem("resid_ready")
        squared, ms_ready, rrms_ready, xr_ready = sem("squared"), sem("ms_ready"), sem("rrms_ready"), sem("xr_ready")
        turned, xT_ready = sem("turned"), sem("xT_ready")
        skip_done, gate_ready = sem("skip_done"), sem("gate_ready")
        conv_done, xs_ready = sem("conv_done"), sem("xs_ready")
        low_done, low_ready = sem("low_done"), sem("low_ready")
        bc_done, bc_ready, bc_stored = sem("bc_done"), sem("bc_ready"), sem("bc_stored")
        z_done, z_ready, abs_ready, exp_ready, log_ready = sem("z_done"), sem("z_ready"), sem("abs_ready"), sem("exp_ready"), sem("log_ready")
        delta_ready, dx_ready = sem("delta_ready"), sem("dx_ready")
        b_loaded, c_loaded = [sem("b_loaded0"), sem("b_loaded1")], [sem("c_loaded0"), sem("c_loaded1")]
        decay_ready, feed_ready, state_ready, part_ready = sem("decay_ready"), sem("feed_ready"), sem("state_ready"), sem("part_ready")
        summed = sem("summed")
        skipped, y_ready, out_done = sem("skipped"), sem("y_ready"), sem("out_done")
        resid_added, batch_done = sem("resid_added"), sem("batch_done")
        block = ctx.enter_context(nc.Block())
        halves = [slice(h * HALF, (h + 1) * HALF) for h in range(2)]
        batch = lambda b: k.x[:, ds(b * S, S)].rearrange("p (t d) -> p t d", d=D)

        @block.sync
        def _(sp):
            with sp.Fori(0, B) as b:
                sp.wait_ge(bc_ready, b + 1)
                sp.dma_start(k.bc_rows[ds(b, 1)].rearrange("o r s -> (o r) s"), bc[:, :]).then_inc(bc_stored, 16)
                sp.wait_ge(bc_stored, b * 16 + 16)
                for n in range(MN):
                    if n >= 2:
                        sp.wait_ge(feed_ready, b * UNITS + (n - 1) * MT)
                    sp.dma_start(b_all[:, n % 2], k.bc_rows[ds(b, 1), n, :].broadcast_to([P, S])).then_inc(b_loaded[n % 2], 16)
                    if n >= 2:
                        sp.wait_ge(part_ready, b * UNITS + (n - 1) * MT + 2)
                    sp.dma_start(c_all[:, n % 2], k.bc_rows[ds(b, 1), MN + n, :].broadcast_to([P, S])).then_inc(c_loaded[n % 2], 16)

        @block.gpsimd
        def _(pool):
            pool.wait_ge(k.consts_loaded, k.consts_total)
            pool.memset(xT[:, 0:PAD], 0.0).then_inc(padded, 1)
            pool.memset(low[:, :], 0.0).then_inc(padded, 1)
            with pool.Fori(0, B) as b:
                pool.wait_ge(var_ready, b + 1)
                pool.tensor_tensor(rstd[:, :], var_eps[:, :], k.minus_half[:, 0:TB], ALU.pow).then_inc(rstd_ready, 1)
                pool.wait_ge(ms_ready, b + 1)
                pool.tensor_tensor(rrms[:, :], ms_eps[:, :], k.minus_half[:, 0:TB], ALU.pow).then_inc(rrms_ready, 1)
                pool.wait_ge(resid_ready, (b + 1) * TB)
                pool.tensor_tensor(batch(b), batch(b), resid[:, :, :], ALU.add).then_inc(resid_added, 1)
                for u in range(UNITS):
                    n, et, m = u // MT, u % MT, b * UNITS + u
                    if et == 0:
                        pool.wait_ge(c_loaded[n % 2], (b * (MN // 2) + n // 2 + 1) * 16)
                    pool.wait_ge(state_ready, m + 3)
                    pool.wait_ge(summed, m + 1)
                    pool.tensor_tensor(part[:, et], state[:, et], c_all[:, n % 2], ALU.mult).then_inc(part_ready, 1)

        @block.scalar
        def _(act):
            act.wait_ge(k.ssm_weights_loaded, k.ssm_weights_total)
            act.activation(neg_a[:, :, :], k.a_log[:, :, :], ACT.Exp).then_inc(exp_a, 1)
            act.wait_ge(padded, 2)
            act.wait_ge(a_ready, 1)
            with act.Fori(0, B) as b:
                act.wait_ge(resid_ready, (b + 1) * TB)
                for j in range(TB):
                    if j:
                        act.wait_ge(squared, b * TB + j)
                    act.activation(square[:, :], resid[:, j], ACT.Square, accum_out=square_sum[:, j:j + 1]).then_inc(squared, 1)
                act.wait_ge(turned, b + 1)
                act.mul(xT[:, PAD:], ps[0][:, :], k.norm_w[:, 0:1]).then_inc(xT_ready, 1)
                for et in range(MT):
                    act.wait_ge(skip_done, b * MT + et + 1)
                    act.activation(gate[:, et], ps[1 - et][:, :], ACT.Silu).then_inc(gate_ready, 1)
                for et in range(MT):
                    act.wait_ge(conv_done, b * MT + et + 1)
                    act.activation(xs[:, et], ps[1 - et][:, :], ACT.Silu, bias=k.conv_b[:, et:et + 1]).then_inc(xs_ready, 1)
                act.wait_ge(low_done, b + 1)
                act.copy(low[0:MR, :], ps[1][0:MR, :]).then_inc(low_ready, 1)
                act.wait_ge(bc_done, b + 1)
                act.copy(bc[:, :], ps[0][0:2 * MN, :]).then_inc(bc_ready, 1)
                for et in range(MT):
                    m = b * MT + et
                    act.wait_ge(z_ready, m + 1)
                    act.wait_ge(delta_ready, m + 1)
                    act.activation(soft[:, :], z[:, et], ACT.Abs).then_inc(abs_ready, 1)
                    act.wait_ge(abs_ready, m + 1)
                    act.activation(soft[:, :], soft[:, :], ACT.Exp, scale=-1.0).then_inc(exp_ready, 1)
                    act.wait_ge(exp_ready, m + 1)
                    act.activation(soft[:, :], soft[:, :], ACT.Ln, bias=1.0).then_inc(log_ready, 1)
                act.wait_ge(delta_ready, (b + 1) * MT + 1)
                for u in range(UNITS):
                    n, et, m = u // MT, u % MT, b * UNITS + u
                    act.wait_ge(state_ready, m + 1)
                    act.activation(decay[:, et], delta[:, et], ACT.Exp, scale=neg_a[:, et, n:n + 1]).then_inc(decay_ready, 1)

        @block.vector
        def _(dve):
            dve.wait_ge(k.x_loaded, B * 16)
            dve.wait_ge(k.ssm_weights_loaded, k.ssm_weights_total)
            for t in range(MC):
                dve.tensor_tensor(conv_in[:, t], k.in_w[:, :], k.conv_w[:, t], ALU.mult).then_inc(folded, 1)
            dve.wait_ge(exp_a, 1)
            dve.tensor_scalar(neg_a[:, :, :], neg_a[:, :, :], -1.0, None, ALU.mult).then_inc(a_ready, 1)
            with dve.Fori(0, B) as b:
                step = Chain(dve, dve_steps, TB + NORM_STEPS, b)
                for j in range(TB):
                    step.did(dve.bn_stats(stats[:, j], k.x[:, ds((b * TB + j) * D, D)]))
                step.wait()
                gather_stats(dve, step, stats, moments, mean, var_eps[:, :]).then_inc(var_ready, 1)
                step.end()
                dve.wait_ge(rstd_ready, b + 1)
                for j in range(TB):
                    dve.tensor_scalar(resid[:, j], k.x[:, ds((b * TB + j) * D, D)], mean[:, j:j + 1],
                                      rstd[:, j:j + 1], ALU.subtract, ALU.mult).then_inc(resid_ready, 1)
                dve.wait_ge(squared, (b + 1) * TB)
                dve.tensor_scalar(ms_eps[:, :], square_sum[:, :], 1.0 / D, LN_EPS, ALU.mult, ALU.add).then_inc(ms_ready, 1)
                dve.wait_ge(rrms_ready, b + 1)
                for j in range(TB):
                    dve.tensor_scalar(xr[:, j], resid[:, j], rrms[:, j:j + 1], None, ALU.mult).then_inc(xr_ready, 1)
                for et in range(MT):
                    m = b * MT + et
                    dve.wait_ge(z_done, m + 1)
                    dve.tensor_scalar(z[:, et], ps[1 - et][:, :], k.wd2_b[:, et:et + 1], None, ALU.add).then_inc(z_ready, 1)
                for et in range(MT):
                    m = b * MT + et
                    dve.wait_ge(log_ready, m + 1)
                    dve.scalar_tensor_tensor(out=delta[:, et], in0=z[:, et], scalar=0.0, in1=soft[:, :], op0=ALU.max,
                                             op1=ALU.add).then_inc(delta_ready, 1)
                    dve.wait_ge(delta_ready, m + 2)
                    dve.tensor_tensor(dx[:, et], delta[:, et], xs[:, et], ALU.mult).then_inc(dx_ready, 1)
                dve.wait_ge(dx_ready, (b + 1) * MT)

                def feed_unit(u):
                    n, et = u // MT, u % MT
                    if et == 0:
                        dve.wait_ge(b_loaded[n % 2], (b * (MN // 2) + n // 2 + 1) * 16)
                    dve.wait_ge(state_ready, b * UNITS + u)
                    dve.tensor_tensor(feed[:, u % 3], dx[:, et], b_all[:, n % 2], ALU.mult).then_inc(feed_ready, 1)

                feed_unit(0)
                for u in range(UNITS):
                    et, m = u % MT, b * UNITS + u
                    if u + 1 < UNITS:
                        feed_unit(u + 1)
                    dve.wait_ge(feed_ready, m + 1)
                    dve.wait_ge(decay_ready, m + 1)
                    dve.wait_ge(part_ready, m + 1)
                    dve.tensor_tensor_scan(state[:, et], decay[:, et], feed[:, u % 3], 0.0, ALU.mult, ALU.add).then_inc(state_ready, 1)
                dve.wait_ge(summed, (b + 1) * UNITS + 2)
                for et in range(MT):
                    m = b * MT + et
                    dve.scalar_tensor_tensor(out=z[:, et], in0=xs[:, et], scalar=k.w_d[:, et:et + 1], in1=psY[:, et],
                                             op0=ALU.mult, op1=ALU.add).then_inc(skipped, 1)
                for et in range(MT):
                    m = b * MT + et
                    dve.wait_ge(skipped, m + 1)
                    dve.tensor_tensor(xs[:, et], z[:, et], gate[:, et], ALU.mult).then_inc(y_ready, 1)
                dve.wait_ge(out_done, b + 1)
                dve.wait_ge(resid_added, b + 1)
                dve.tensor_tensor(batch(b), batch(b), ps[1][:, :].rearrange("p (t d) -> p t d", d=D), ALU.add).then_inc(batch_done, 1)

        @block.tensor
        def _(pe):
            pe.wait_ge(folded, MC)
            pe.wait_ge(k.consts_loaded, k.consts_total)
            pe.wait_ge(k.ssm_weights_loaded, k.ssm_weights_total)
            for s, n in ((state_ready, 2), (part_ready, 2), (summed, 2), (delta_ready, 1), (batch_done, 1)):
                pe.sem_inc(s, n)
            with pe.Fori(0, B) as b:
                pe.wait_ge(xr_ready, (b + 1) * TB)
                for j in range(TB):
                    mm = pe.transpose(ps[0][:, j * P:(j + 1) * P], xr[:, j], k.ident[:, :])
                mm.then_inc(turned, 1)

                def product(out, rows, w, src, done):
                    for cols in halves:
                        for j in range(len(w)):
                            mm = pe.matmul(out[0:rows, cols], w[j], src(j, cols), start=(j == 0), stop=(j == len(w) - 1))
                    mm.then_inc(done, 1)

                shift = lambda t: lambda j, cols: xT[:, PAD + t + j + cols.start:PAD + t + j + cols.stop]
                channels = [slice(et * P, (et + 1) * P) for et in range(MT)]
                pe.wait_ge(xT_ready, b + 1)
                pe.wait_ge(batch_done, b + 1)
                for et in range(MT):
                    product(ps[1 - et], P, [k.skip_w[:, channels[et]]], shift(0), skip_done)
                for et in range(MT):
                    pe.wait_ge(gate_ready, b * MT + et + 1)
                    product(ps[1 - et], P, [conv_in[:, t, channels[et]] for t in range(MC)], shift(1 - MC), conv_done)
                pe.wait_ge(xs_ready, (b + 1) * MT)
                channel_tile = lambda j, cols: xs[:, j, cols]
                product(ps[1], MR, [k.wd1[:, et] for et in range(MT)], channel_tile, low_done)
                product(ps[0], 2 * MN, [k.wbc[:, et] for et in range(MT)], channel_tile, bc_done)
                pe.wait_ge(low_ready, b + 1)
                product(ps[1], P, [k.wd2[:, channels[0]]], lambda j, cols: low[:, cols], z_done)
                pe.wait_ge(bc_ready, b + 1)
                product(ps[0], P, [k.wd2[:, channels[1]]], lambda j, cols: low[:, cols], z_done)
                for u in range(UNITS):
                    n, et, m = u // MT, u % MT, b * UNITS + u
                    pe.wait_ge(part_ready, m + 3)
                    for cols in halves:
                        mm = pe.matmul(psY[:, et, cols], k.ident[:, :], part[:, et, cols], start=(n == 0), stop=(n == MN - 1))
                    mm.then_inc(summed, 1)
                pe.wait_ge(y_ready, (b + 1) * MT)
                for j in range(TB):
                    cols = slice(j * P, (j + 1) * P)
                    for et in range(MT):
                        mm = pe.matmul(ps[1][:, cols], xs[:, et, cols], k.out_w[:, et], start=(et == 0), stop=(et == MT - 1))
                mm.then_inc(out_done, 1)
def build_program(nc, a, out):
    with ExitStack() as ctx:
        sb = lambda n, s, d=F32: ctx.enter_context(nc.sbuf_tensor(n, s, d))
        sem = lambda n: ctx.enter_context(nc.semaphore(n))
        k = Names()
        k.x = sb("x", [P, B * S])
        w_qkv = sb("w_qkv", [P, 3, D])
        k.w_q, k.w_k, k.w_v = (w_qkv[:, j] for j in range(3))
        k.w_out = sb("w_out", [P, D])
        k.b_out, k.gamma, k.beta = sb("b_out", [P, D]), sb("gamma", [P, D]), sb("beta", [P, D])
        k.ident = sb("ident", [P, P])
        k.minus_half = sb("minus_half", [P, 2 * TB])
        k.before = sb("before", [P, E * E])
        k.ident_b = sb("ident_b", [P, P], BF16)
        k.spread = sb("spread", [P, E, P], BF16)
        k.w_router = sb("w_router", [P, E])
        k.w1 = sb("w1", [P, NE, 2 * I])
        k.w2 = sb("w2", [P, NE, D])
        k.norm_w = sb("norm_w", [P, 1])
        k.skip_w, k.in_w = sb("skip_w", [P, ME]), sb("in_w", [P, ME])
        k.conv_w = sb("conv_w", [P, MC, ME])
        k.conv_b, k.wd2_b, k.w_d = sb("conv_b", [P, MT]), sb("wd2_b", [P, MT]), sb("w_d", [P, MT])
        k.wd1, k.wbc, k.wd2 = sb("wd1", [P, MT, MR]), sb("wbc", [P, MT, 2 * MN]), sb("wd2", [P, ME])
        k.a_log, k.out_w = sb("a_log", [P, MT, MN]), sb("out_w", [P, MT, D])
        k.bc_rows = nc.dram_tensor("bc_rows", [B, 2 * MN, S], F32, kind="Internal").ap()
        k.ssm_weights_loaded, wd2_zeroed = sem("ssm_weights_loaded"), sem("wd2_zeroed")
        k.q_terms = nc.dram_tensor("q_terms", [B, H, NT, HD, S], BF16, kind="Internal").ap()
        k.k_terms = nc.dram_tensor("k_terms", [B, H, NT, HD, S], BF16, kind="Internal").ap()
        k.x_loaded, k.consts_loaded = sem("x_loaded"), sem("consts_loaded")
        k.attn_weights_loaded, k.ffn_weights_loaded = sem("attn_weights_loaded"), sem("ffn_weights_loaded")
        stored = sem("out_stored")
        spread_loaded, cast = sem("spread_loaded"), sem("cast")
        spread_f = sb("spread_f", [P, E * P])
        with nc.Block() as block:
            @block.sync
            def _(sp):
                sp.dma_start(k.ident[:, :], a["ident"]).then_inc(k.consts_loaded, 16)
                sp.dma_start(spread_f[:, :], a["spread"]).then_inc(spread_loaded, 16)
                sp.dma_start(k.minus_half[:, :], a["minus_half"]).then_inc(k.consts_loaded, 16)
                for b in range(B):
                    src = a["x"][b * S:(b + 1) * S].rearrange("(t p) d -> p t d", p=P)
                    sp.dma_start(k.x[:, b * S:(b + 1) * S].rearrange("p (t d) -> p t d", d=D), src).then_inc(k.x_loaded, 16)

            @block.gpsimd
            def _(pool):
                pool.memset(k.wd2[:, :], 0.0).then_inc(wd2_zeroed, 1)
                pool.wait_ge(wd2_zeroed, 1)
                tiles = lambda name: a[name].rearrange("(t p) c -> p t c", p=P)
                for dst, src in ((k.norm_w[:, :], a["norm_w"]), (k.skip_w[:, :], a["skip_w"]), (k.in_w[:, :], a["in_w"]),
                                 (k.conv_w[:, :, :], a["conv_w"].unsqueeze(0).broadcast_to([P, MC, ME])),
                                 (k.wd1[:, :, :], tiles("wd1")), (k.wd2[0:MR, :], a["wd2"]),
                                 (k.wbc[:, :, 0:MN], tiles("wb")), (k.wbc[:, :, MN:], tiles("wc")),
                                 (k.a_log[:, :, :], tiles("A_log")), (k.out_w[:, :, :], tiles("out_w"))):
                    pool.dma_start(dst, src).then_inc(k.ssm_weights_loaded, 16)
                for dst, name in ((k.conv_b, "conv_b"), (k.wd2_b, "wd2_b"), (k.w_d, "W_D")):
                    pool.dma_start(dst[:, :], a[name]).then_inc(k.ssm_weights_loaded, 16)

            @block.vector
            def _(dve):
                dve.wait_ge(spread_loaded, 16)
                dve.tensor_copy(k.spread[:, :, :], spread_f[:, :].rearrange("p (e q) -> p e q", e=E)).then_inc(cast, 1)
                dve.wait_ge(k.consts_loaded, 6 * 16)
                dve.tensor_copy(k.ident_b[:, :], k.ident[:, :]).then_inc(cast, 1)

            @block.scalar
            def _(act):
                act.dma_start(w_qkv[:, :, :], a["w_qkv"].rearrange("j d c -> d j c")).then_inc(k.attn_weights_loaded, 16)
                for dst, name in ((k.b_out, "b_out"), (k.gamma, "gamma"), (k.beta, "beta"), (k.before, "before")):
                    act.dma_start(dst[:, :], a[name].broadcast_to([P, a[name].shape[1]])).then_inc(k.consts_loaded, 16)
                act.dma_start(k.w_out[:, :], a["w_out"]).then_inc(k.ffn_weights_loaded, 16)
                act.dma_start(k.w_router[:, :], a["w_router"]).then_inc(k.ffn_weights_loaded, 16)
                act.dma_start(k.w1[:, 0:E], a["fc1"].rearrange("e d f -> d e f")).then_inc(k.ffn_weights_loaded, 16)
                act.dma_start(k.w1[:, E:NE, 0:I], a["gate_w"].rearrange("d (s f) -> d s f", s=2)).then_inc(k.ffn_weights_loaded, 16)
                act.dma_start(k.w1[:, E:NE, I:2 * I], a["up_w"].rearrange("d (s f) -> d s f", s=2)).then_inc(k.ffn_weights_loaded, 16)
                act.dma_start(k.w2[:, 0:E], a["fc2"].rearrange("e i d -> i e d")).then_inc(k.ffn_weights_loaded, 16)
                act.dma_start(k.w2[:, E:NE], a["down_w"].rearrange("(s i) d -> i s d", s=2)).then_inc(k.ffn_weights_loaded, 16)
        k.consts_total, k.attn_weights_total, k.ffn_weights_total = 6 * 16, 16, 7 * 16
        k.ssm_weights_total = 13 * 16
        with ExitStack() as attn:
            sa = lambda n: attn.enter_context(nc.sbuf_tensor(n, [P, B * S], F32))
            k.xn = sa("attn_in")
            k.v = sa("v")
            k.att = sa("att")
            project_qkv(nc, k)
            attend(nc, k)
            feed_forward(nc, k, "ffn1", True)
        state_space(nc, k)
        feed_forward(nc, k, "ffn2", False)
        with nc.Block() as block:
            @block.sync
            def _(sp):
                sp.wait_ge(k.ffn_weights_loaded, k.ffn_weights_total)
                sp.wait_ge(k.ssm_weights_loaded, k.ssm_weights_total)
                src = k.x
                for b in range(B):
                    dst = out[b * S:(b + 1) * S].rearrange("(t p) d -> p t d", p=P)
                    sp.dma_start(dst, src[:, b * S:(b + 1) * S].rearrange("p (t d) -> p t d", d=D)).then_inc(stored, 16)
                sp.wait_ge(stored, 16 * B)


def layout(inp):
    import numpy as np
    g = {n.replace("L0_attn_a_", "a_").replace("L0_attn_b_", "b_").replace("L0_ffn_", "f_"): np.asarray(v) for n, v in inp.items()}
    r = {
        "x": g["a_x"].reshape(B * S, D),
        "w_qkv": g["a_w_qkv"].reshape(D, H, 3, HD).transpose(2, 0, 1, 3).reshape(3, D, D),
        "w_out": g["a_w_out"], "b_out": g["a_b_out"].reshape(1, D), "gamma": g["a_gamma"].reshape(1, D),
        "beta": g["a_beta"].reshape(1, D), "norm_w": g["b_norm_w"].reshape(D, 1), "skip_w": g["b_skip_w"].T,
        "in_w": g["b_in_w"].T, "conv_w": g["b_conv_w"].reshape(ME, MC).T, "conv_b": g["b_conv_b"].reshape(MT, P).T,
        "wd1": g["b_wd1"].T, "wd2": g["b_wd2"].T, "wd2_b": g["b_wd2_b"].reshape(MT, P).T,
        "wb": g["b_wb"].T, "wc": g["b_wc"].T, "A_log": g["b_A_log"], "W_D": g["b_W_D"].reshape(MT, P).T,
        "out_w": g["b_out_w"].T, "w_router": g["f_w_router"], "fc1": g["f_fc1_w"], "fc2": g["f_fc2_w"],
        "gate_w": g["f_gate_w"], "up_w": g["f_up_w"], "down_w": g["f_down_w"],
    }
    spread = np.zeros((P, E, P), np.float32)
    for e in range(E):
        for part in range(PARTS):
            spread[part * E + e, e, :] = 1
    r["ident"] = np.eye(P, dtype=np.float32)
    r["spread"] = spread.reshape(P, E * P)
    r["before"] = np.tril(np.ones((E, E), np.float32), -1).reshape(1, E * E)
    r["minus_half"] = np.full((P, 2 * TB), -0.5, np.float32)
    return {n: np.ascontiguousarray(v) for n, v in r.items()}


def kernel(**inputs):
    import numpy as np
    import concourse.bacc as bacc
    from concourse.bass_utils import run_bass_kernel_spmd as run

    nc = bacc.Bacc("TRN2", target_bir_lowering=False, num_devices=1)
    arrays = {f"in_{n}": v for n, v in layout(inputs).items()}
    a = {n[3:]: nc.dram_tensor(n, v.shape, mybir.dt.from_np(v.dtype), kind="ExternalInput").ap() for n, v in arrays.items()}
    out = nc.dram_tensor("out", (B * S, D), F32, kind="ExternalOutput").ap()
    build_program(nc, a, out)
    r = run(nc, [arrays], core_ids=[0])
    return np.asarray(r.results[0]["out"]).reshape(B, S, D)
```

```python
from contextlib import ExitStack

import concourse.bass as bass
from concourse import mybir

F32 = mybir.dt.float32
BF16 = mybir.dt.bfloat16
ALU = mybir.AluOpType
ACT = mybir.ActivationFunctionType
AX_X = mybir.AxisListType.X
ds = bass.ds

P = 128
B, S, D = 4, 1024, 128
H, HD = 16, 8
TB = S // P
HG = 4
GB = H // HG
NG = B * GB
STRIP = 32
GW = HG * HD
PARTS = 3
Q_TERM = (0, 0, 0, 1, 1, 2)
K_TERM = (0, 1, 2, 0, 1, 0)
NT = len(Q_TERM)
HALF = 512
STEPS = 2 * TB
CH = 512
NCH = B * S // CH
CT = CH // P
E, TOPK, I = 8, 2, 128
NE = E + 2
ME, MN, MR, MC = 256, 16, 64, 4
MT = ME // P
UNITS = MN * MT
LN_EPS = 1e-5
KERN_EPS = 1e-6


class Names:
    pass


class Chain:

    def __init__(self, eng, sem, per, turn):
        self.eng, self.sem, self.per, self.turn, self.n = eng, sem, per, turn, 0

    def did(self, ins):
        ins.then_inc(self.sem, 1)
        self.n += 1

    def wait(self):
        self.eng.wait_ge(self.sem, self.turn * self.per + self.n)

    def end(self):
        assert self.n == self.per, self.n


NORM_STEPS = 5


def gather_stats(dve, step, stats, moments, mean, var_eps):
    even, odd = stats[:, :, 0:3], stats[:, :, 3:6]
    step.did(dve.tensor_tensor(moments[:, :, 0:3], even, odd, ALU.add))
    step.did(dve.tensor_tensor(moments[:, :, 3:4], even[:, :, 1:2], odd[:, :, 1:2], ALU.subtract))
    step.wait()
    step.did(dve.tensor_scalar(mean[:, :], moments[:, :, 1], 0.5, None, ALU.mult))
    step.did(dve.tensor_tensor(moments[:, :, 4:5], moments[:, :, 3:4], moments[:, :, 3:4], ALU.mult))
    step.did(dve.tensor_scalar(moments[:, :, 5:6], moments[:, :, 2:3], 1.0 / D, LN_EPS, ALU.mult, ALU.add))
    step.wait()
    return dve.scalar_tensor_tensor(out=var_eps, in0=moments[:, :, 4], scalar=0.25, in1=moments[:, :, 5],
                                    op0=ALU.mult, op1=ALU.add)


def project_qkv(nc, k):
    with ExitStack() as ctx:
        sb = lambda n, s, d=F32: ctx.enter_context(nc.sbuf_tensor("qkv_" + n, s, d))
        pb = lambda n: ctx.enter_context(nc.psum_tensor("qkv_" + n, [P, S], F32))
        sem = lambda n: ctx.enter_context(nc.semaphore("qkv_" + n))
        stats = sb("stats", [P, TB, 6])
        moments = sb("moments", [P, TB, 8])
        mean = sb("mean", [P, 2, TB])
        var_eps = sb("var_eps", [P, 2, TB])
        rstd = sb("rstd", [P, 2, TB])
        xn = sb("xn", [P, 2, TB, D])
        xnT = sb("xnT", [P, 2, S])
        q_part = sb("q_part", [P, 2, PARTS, S], BF16)
        k_part = sb("k_part", [P, 2, PARTS, S], BF16)
        q_rest = sb("q_rest", [P, S])
        k_rest = sb("k_rest", [P, S])
        psT, psQ, psK, psV = pb("psT"), pb("psQ"), pb("psK"), pb("psV")
        dve_steps, spread_cast = sem("dve_steps"), sem("spread_cast")
        var_ready, rstd_ready = sem("var_ready"), sem("rstd_ready")
        xn_ready, xn_copied, xn_turned = sem("xn_ready"), sem("xn_copied"), sem("xn_turned")
        xnT_ready = sem("xnT_ready")
        q_ready, k_ready, v_ready = sem("q_ready"), sem("k_ready"), sem("v_ready")
        qk_taken, v_copied = sem("qk_taken"), sem("v_copied")
        first_ready, second_ready, third_ready = sem("first_ready"), sem("second_ready"), sem("third_ready")
        stored = [sem("stored0"), sem("stored1")]
        block = ctx.enter_context(nc.Block())
        scale = float(HD) ** -0.5
        STORES = 2 * NT * 16

        def over_batches(eng, body):
            with eng.Fori(0, B // 2 - 1) as i:
                body(i, 0, False)
                body(i, 1, False)
            body(B // 2 - 1, 0, False)
            body(B // 2 - 1, 1, True)

        @block.sync
        def _(sp):
            k.load_later_weights(sp)

            def body(pair, par, last):
                b = pair * 2 + par
                for part, ready in enumerate((first_ready, second_ready, third_ready)):
                    sp.wait_ge(ready, b * 2 + 2)
                    for src, terms, dst in ((q_part, Q_TERM, k.q_terms), (k_part, K_TERM, k.k_terms)):
                        for t in range(NT):
                            if terms[t] == part:
                                out = dst[ds(b, 1), :, t].rearrange("o h d s -> (o h) d s")
                                sp.dma_start(out, src[:, par, part, :]).then_inc(stored[par], 16)

            over_batches(sp, body)
            for par in range(2):
                sp.wait_ge(stored[par], (B // 2 + 1) * STORES)

        @block.gpsimd
        def _(pool):
            pool.wait_ge(k.consts_loaded, k.consts_total)
            pool.tensor_copy(k.ident_b[:, :], k.ident[:, :])

            def body(pair, par, last):
                b = pair * 2 + par
                pool.wait_ge(var_ready, b + 1)
                pool.tensor_tensor(rstd[:, par], var_eps[:, par], k.minus_half[:, 0:TB], ALU.pow).then_inc(rstd_ready, 1)
                pool.wait_ge(xn_ready, (b + 1) * TB)
                bias = k.b_out[:, :].unsqueeze(1).broadcast_to([P, TB, D])
                out = k.xn[:, ds(b * S, S)].rearrange("p (t d) -> p t d", d=D)
                pool.tensor_tensor(out, xn[:, par], bias, ALU.add).then_inc(xn_copied, 1)

            over_batches(pool, body)
            pool.wait_ge(k.spread_loaded, 16)
            pool.tensor_copy(k.spread[:, :, :], k.spread_f[:, :].rearrange("p (e q) -> p e q", e=E)).then_inc(spread_cast, 1)

        @block.vector
        def _(dve):
            def take_stats(b, par):
                step = Chain(dve, dve_steps, TB + NORM_STEPS, b)
                for j in range(TB):
                    step.did(dve.bn_stats(stats[:, j], k.x[:, ds((b * TB + j) * D, D)]))
                step.wait()
                gather_stats(dve, step, stats, moments, mean[:, par], var_eps[:, par]).then_inc(var_ready, 1)
                step.end()

            def norm(b, par):
                dve.wait_ge(rstd_ready, b + 1)
                dve.wait_ge(xn_copied, b + 1)
                dve.wait_ge(xn_turned, b + 1)
                for j in range(TB):
                    dve.tensor_scalar(xn[:, par, j], k.x[:, ds((b * TB + j) * D, D)], mean[:, par, j:j + 1],
                                      rstd[:, par, j:j + 1], ALU.subtract, ALU.mult).then_inc(xn_ready, 1)

            def body(pair, par, last):
                b = pair * 2 + par
                if not last:
                    take_stats(b + 1, 1 - par)
                    norm(b + 1, 1 - par)
                dve.wait_ge(first_ready, b * 2 + 1)
                dve.wait_ge(second_ready, b * 2)
                dve.wait_ge(third_ready, b * 2)
                dve.scalar_tensor_tensor(out=q_rest[:, :], in0=psQ[:, :], scalar=scale, in1=q_part[:, par, 0],
                                         op0=ALU.mult, op1=ALU.subtract).then_inc(qk_taken, 1)
                dve.wait_ge(first_ready, b * 2 + 2)
                dve.tensor_tensor(k_rest[:, :], psK[:, :], k_part[:, par, 0], ALU.subtract).then_inc(qk_taken, 1)
                dve.wait_ge(second_ready, b * 2 + 1)
                dve.tensor_tensor(q_part[:, par, 2], q_rest[:, :], q_part[:, par, 1], ALU.subtract).then_inc(third_ready, 1)
                dve.wait_ge(second_ready, b * 2 + 2)
                dve.tensor_tensor(k_part[:, par, 2], k_rest[:, :], k_part[:, par, 1], ALU.subtract).then_inc(third_ready, 1)

            dve.wait_ge(k.x_loaded[0], 16)
            take_stats(0, 0)
            for b in range(1, B):
                dve.wait_ge(k.x_loaded[b], 16)
            norm(0, 0)
            over_batches(dve, body)

        @block.scalar
        def _(act):
            def xnT_out(b, par):
                act.wait_ge(xn_turned, b + 3)
                act.wait_ge(v_ready, b + 1)
                act.copy(xnT[:, par], psT[:, :]).then_inc(xnT_ready, 1)

            def body(pair, par, last):
                b = pair * 2 + par
                act.wait_ge(q_ready, b + 1)
                act.wait_ge(stored[par], (pair + 1) * STORES)
                act.mul(q_part[:, par, 0], psQ[:, :], scale).then_inc(first_ready, 1)
                act.wait_ge(k_ready, b + 1)
                act.copy(k_part[:, par, 0], psK[:, :]).then_inc(first_ready, 1)
                if not last:
                    xnT_out(b + 1, 1 - par)
                act.wait_ge(v_ready, b + 3)
                v_out = k.v[:, ds(b * S, S)].rearrange("p (g t c) -> p t g c", g=GB, c=GW)
                act.copy(v_out, psV[:, :].rearrange("p (t g c) -> p t g c", t=TB, g=GB)).then_inc(v_copied, 1)
                act.wait_ge(qk_taken, b * 2 + 2)
                act.copy(q_part[:, par, 1], q_rest[:, :]).then_inc(second_ready, 1)
                act.wait_ge(qk_taken, b * 2 + 3)
                act.copy(k_part[:, par, 1], k_rest[:, :]).then_inc(second_ready, 1)

            xnT_out(0, 0)
            over_batches(act, body)

        @block.tensor
        def _(pe):
            for s, n in ((xn_turned, 2), (xn_copied, 2), (v_ready, 2), (xnT_ready, 1), (qk_taken, 1), (v_copied, 1),
                         (stored[0], STORES), (stored[1], STORES)):
                pe.sem_inc(s, n)
            pe.wait_ge(k.attn_weights_loaded, k.attn_weights_total)
            pe.wait_ge(k.consts_loaded, k.consts_total)

            def turn(b, par):
                pe.wait_ge(xn_ready, (b + 1) * TB)
                pe.wait_ge(xnT_ready, b + 1)
                for j in range(TB):
                    mm = pe.transpose(psT[:, j * P:(j + 1) * P], xn[:, par, j], k.ident[:, :])
                mm.then_inc(xn_turned, 1)

            def body(pair, par, last):
                b = pair * 2 + par
                pe.wait_ge(xnT_ready, b + 2)
                pe.wait_ge(qk_taken, b * 2 + 1)
                for ps, w, done in ((psQ, k.w_q, q_ready), (psK, k.w_k, k_ready)):
                    for h in range(2):
                        cols = slice(h * HALF, (h + 1) * HALF)
                        mm = pe.matmul(ps[:, cols], w, xnT[:, par, cols], start=True, stop=True)
                    mm.then_inc(done, 1)
                if not last:
                    turn(b + 1, 1 - par)
                pe.wait_ge(v_copied, b + 1)
                for j in range(TB):
                    cols = slice(j * P, (j + 1) * P)
                    mm = pe.matmul(psV[:, cols], xnT[:, par, cols], k.w_v, start=True, stop=True)
                mm.then_inc(v_ready, 1)

            turn(0, 0)
            over_batches(pe, body)


def attend(nc, k):
    with ExitStack() as ctx:
        sb = lambda n, s, d=F32: ctx.enter_context(nc.sbuf_tensor("att_" + n, s, d))
        pb = lambda n, w: ctx.enter_context(nc.psum_tensor("att_" + n, [P, w], F32))
        sem = lambda n: ctx.enter_context(nc.semaphore("att_" + n))
        q_in = sb("q_in", [P, 2, HG // 2, S], BF16)
        k_in = sb("k_in", [P, 2, HG, S], BF16)
        v_in = sb("v_in", [P, 2, TB, HG, STRIP])
        w = sb("w", [P, 2, HG, HALF])
        oT = sb("oT", [P, 2, HALF])
        den = sb("den", [P, CT, HG])
        inv_den = sb("inv_den", [P, CT, HG])
        psA, psB = pb("psA", 2 * HALF), pb("psB", 2 * HALF)
        psO = [pb("psO0", HALF), pb("psO1", HALF)]
        psT = pb("psT", HALF)
        zeroed, ones_set = sem("zeroed"), sem("ones_set")
        qk_loaded, v_ready = [sem("qk_loaded0"), sem("qk_loaded1")], sem("v_ready")
        scored_a, scored_b = sem("scored_a"), sem("scored_b")
        relu_a, relu_b = sem("relu_a"), sem("relu_b")
        summed = sem("summed")
        o_copied, o_turned, o_done = sem("o_copied"), sem("o_turned"), sem("o_done")
        dve_steps = sem("dve_steps")
        block = ctx.enter_context(nc.Block())
        rows = NT * HD
        q_src = k.q_terms.rearrange("b (g p a) t d s -> (b g) p a (t d) s", g=GB, a=2)
        k_src = k.k_terms.rearrange("b (g p a) t d s -> (b g) p a (t d) s", g=GB, a=2)
        BODY = 2 * STEPS
        AHEAD = 2 * STEPS
        LAST = NG // 2 - 1

        @block.sync
        def _(sp):
            sp.wait_ge(zeroed, 2)
            with sp.Fori(0, NG // 2) as i:
                for par in range(2):
                    n = i * 2 + par
                    sp.wait_ge(scored_b, (n + 1) * STEPS)
                    for a in range(2):
                        r = slice(64 * a, 64 * a + rows)
                        sp.dma_start(q_in[r, par], q_src[ds(n, 1), :, a].rearrange("o p r s -> r (o p) s")).then_inc(qk_loaded[par], 16)
                        out = k_in[r, par].rearrange("r (p a) s -> r p a s", a=2)[:, :, a]
                        sp.dma_start(out, k_src[ds(n, 1), :, a].rearrange("o p r s -> r (o p) s")).then_inc(qk_loaded[par], 16)

        @block.gpsimd
        def _(pool):
            pool.memset(k_in[:, :, :, :], 0.0).then_inc(zeroed, 1)
            pool.memset(v_in[:, :, :, :, :], 0.0).then_inc(ones_set, 1)
            pool.wait_ge(ones_set, 1)
            pool.memset(v_in[:, :, :, :, HD:HD + 1], 1.0).then_inc(ones_set, 1)
            with pool.Fori(0, NG // 2) as i:
                for par in range(2):
                    n = i * 2 + par
                    pool.wait_ge(summed, (n + 1) * STEPS)
                    src = k.v[:, ds(n * TB * GW, TB * GW)].rearrange("p (t h d) -> p t h d", t=TB, d=HD)
                    pool.tensor_copy(v_in[:, par, :, :, 0:HD], src).then_inc(v_ready, 1)

        @block.scalar
        def _(act):
            def relu(m, buf):
                act.wait_ge(scored_a, m + 1)
                act.wait_ge(summed, AHEAD + m - 1)
                act.activation(w[:, buf, 0:2], psA[:, :].rearrange("p (h q) -> p h q", h=2), ACT.Relu).then_inc(relu_a, 1)

            def body(i, last):
                for q in range(BODY):
                    m = i * BODY + q
                    if not (last and q == BODY - 1):
                        relu(m + 1, (q + 1) % 2)
                    if q % TB == TB - 1:
                        o, n = q // TB % 2, i * 4 + q // TB
                        act.wait_ge(summed, AHEAD + m + 1)
                        act.wait_ge(o_turned, n + 1)
                        act.copy(oT[:, o], psO[o][:, :]).then_inc(o_copied, 1)

            relu(0, 0)
            with act.Fori(0, LAST) as i:
                body(i, False)
            body(LAST, True)

        @block.vector
        def _(dve):
            dve.memset(q_in[:, :, :, :], 0.0).then_inc(zeroed, 1)
            dve.wait_ge(ones_set, 2)

            def relu(m, buf):
                dve.wait_ge(scored_b, AHEAD + m + 1)
                dve.wait_ge(summed, AHEAD + m - 1)
                dve.tensor_scalar(w[:, buf, 2:4], psB[:, :].rearrange("p (h q) -> p h q", h=2), 0.0, None,
                                  ALU.max).then_inc(relu_b, 1)

            def normalise(i, j):
                n = i * 4 + j
                t = psT[:, :].rearrange("p (t h c) -> p t h c", t=CT, h=HG)
                dve.wait_ge(o_turned, n + 3)
                dve.tensor_scalar(den[:, :, :], t[:, :, :, HD], KERN_EPS, None, ALU.add).then_inc(dve_steps, 1)
                dve.wait_ge(dve_steps, n * 2 + 1)
                dve.reciprocal(inv_den[:, :, :], den[:, :, :]).then_inc(dve_steps, 1)
                dve.wait_ge(dve_steps, n * 2 + 2)
                out = k.att[:, ds(n * CT * GW, CT * GW)].rearrange("p (m d) -> p m d", d=HD)
                dve.tensor_tensor(out, t[:, :, :, 0:HD].rearrange("p t h d -> p (t h) d"),
                                  inv_den[:, :, :].rearrange("p t h -> p (t h)").unsqueeze(2).broadcast_to([P, CT * HG, HD]),
                                  ALU.mult).then_inc(o_done, 1)

            def body(i, last):
                for q in range(BODY):
                    if not (last and q == BODY - 1):
                        relu(i * BODY + q + 1, (q + 1) % 2)
                    if q % TB == 4 and q > TB:
                        normalise(i, q // TB - 1)
                normalise(i, 3)

            relu(0, 0)
            with dve.Fori(0, LAST) as i:
                body(i, False)
            body(LAST, True)

        @block.tensor
        def _(pe):
            pe.sem_inc(scored_b, AHEAD)
            pe.sem_inc(summed, AHEAD)
            pe.sem_inc(o_turned, 2)
            pe.sem_inc(o_copied, 2)
            pe.sem_inc(o_done, 1)
            pe.sem_inc(relu_a, 1)
            pe.sem_inc(relu_b, 1)

            def scores(n_of_par, m, q):
                par, qh, kt = q // STEPS % 2, q // TB % 2, q % TB
                if q % STEPS == 0:
                    pe.wait_ge(qk_loaded[par], (n_of_par + 1) * 64)
                for ps, pair, taken, done in ((psA, 0, relu_a, scored_a), (psB, 1, relu_b, scored_b)):
                    pe.wait_ge(taken, m + 1)
                    for a in range(2):
                        mm = pe.matmul(ps[:, a * HALF:(a + 1) * HALF], k_in[:, par, 2 * pair + a, kt * P:(kt + 1) * P],
                                       q_in[:, par, pair, qh * HALF:(qh + 1) * HALF], start=True, stop=True)
                    mm.then_inc(done, 1)

            def values(i, q):
                par, o, kt = q // STEPS, q // TB % 2, q % TB
                m = i * BODY + q
                if q % STEPS == 0:
                    pe.wait_ge(v_ready, i * 2 + par + 1)
                if kt == 0:
                    pe.wait_ge(o_copied, i * 4 + q // TB + 1)
                pe.wait_ge(relu_a, m + 2)
                pe.wait_ge(relu_b, m + 2)
                for h in range(HG):
                    mm = pe.matmul(psO[o][h * STRIP:(h + 1) * STRIP, :], v_in[:, par, kt, h], w[:, q % 2, h],
                                   start=(kt == 0), stop=(kt == TB - 1))
                mm.then_inc(summed, 1)

            def turn(i, j):
                n = i * 4 + j
                pe.wait_ge(o_copied, n + 3)
                pe.wait_ge(o_done, n + 1)
                for t in range(CT):
                    mm = pe.transpose(psT[:, t * P:(t + 1) * P], oT[:, j % 2, t * P:(t + 1) * P], k.ident[:, :])
                mm.then_inc(o_turned, 1)

            def body(i, last):
                for q in range(BODY):
                    if not (last and q == BODY - 1):
                        scores(i + (q + 1) // BODY, i * BODY + q + 1, (q + 1) % BODY)
                    values(i, q)
                    if q % TB == 2 and q > TB:
                        turn(i, q // TB - 1)
                turn(i, 3)

            scores(0, 0, 0)
            with pe.Fori(0, LAST) as i:
                body(i, False)
            body(LAST, True)


def feed_forward(nc, k, name, after_attention):
    with ExitStack() as ctx:
        sb = lambda n, s, d=F32: ctx.enter_context(nc.sbuf_tensor(name + "_" + n, s, d))
        pb = lambda n: ctx.enter_context(nc.psum_tensor(name + "_" + n, [P, CH], F32))
        sem = lambda n: ctx.enter_context(nc.semaphore(name + "_" + n))
        heads = sb("heads", [P, CT, D])
        headsT = sb("headsT", [P, CH])
        y = sb("y", [P, CT, D])
        yn = sb("yn", [P, CT, D])
        xn = sb("xn", [P, CT, D])
        xnT = sb("xnT", [P, 2, CH])
        stats = sb("stats", [P, CT, 6])
        moments = sb("moments", [P, CT, 8])
        mean = sb("mean", [P, CT])
        var_eps = sb("var_eps", [P, 2, CT])
        rstd = sb("rstd", [P, 2, CT])
        logit = sb("logit", [P, CT, E])
        above = sb("above", [P, CT, E, E])
        equal = sb("equal", [P, CT, E, E])
        rank = sb("rank", [P, CT, E])
        taken = sb("taken", [P, CT, E])
        taken_logit = sb("taken_logit", [P, CT, E])
        logit_sum = sb("logit_sum", [P, CT])
        margin = sb("margin", [P, CT, E])
        half_tanh = sb("half_tanh", [P, CT, E])
        share = sb("share", [P, CT, E])
        rest = sb("rest", [P, CT, E])
        parts = sb("parts", [P, CT, P], BF16)
        partsT = sb("partsT", [P, 2, CH], BF16)
        silu = sb("silu", [P, 2, CH])
        scaled = sb("scaled", [P, 2, CH])
        hidden = sb("hidden", [P, 2, CH])
        oT = sb("oT", [P, CH])
        psP = [pb("psP0"), pb("psP1")]
        psG = [pb("psG0"), pb("psG1")]
        psC, psO, psX, psY = pb("psC"), pb("psO"), pb("psX"), pb("psY")
        in_steps = sem("in_steps")
        parts_zeroed = sem("parts_zeroed")
        if after_attention:
            out_steps, pool_steps = sem("out_steps"), sem("pool_steps")
            heads_ready, heads_turned, headsT_ready = sem("heads_ready"), sem("heads_turned"), sem("headsT_ready")
            projected, y_taken, yn_ready, x_added = sem("projected"), sem("y_taken"), sem("yn_ready"), sem("x_added")
            y_var_ready, y_rstd_ready = sem("y_var_ready"), sem("y_rstd_ready")
        var_ready, rstd_ready = sem("var_ready"), sem("rstd_ready")
        xn_ready, xn_turned, xnT_ready = sem("xn_ready"), sem("xn_turned"), sem("xnT_ready")
        routed, logit_taken, margin_ready, tanh_ready = sem("routed"), sem("logit_taken"), sem("margin_ready"), sem("tanh_ready")
        parts_ready, parts_turned, partsT_ready = sem("parts_ready"), sem("parts_turned"), sem("partsT_ready")
        p_ready, g_ready, c_ready = sem("p_ready"), sem("g_ready"), sem("c_ready")
        silu_ready, scaled_ready, hidden_ready = sem("silu_ready"), sem("scaled_ready"), sem("hidden_ready")
        down_steps, o_copied, o_turned, o_added = sem("down_steps"), sem("o_copied"), sem("o_turned"), sem("o_added")
        block = ctx.enter_context(nc.Block())
        LAST = NCH // 2 - 1

        def chunk(t, c):
            return t[:, ds(c * CT * D, CT * D)].rearrange("p (t d) -> p t d", d=D)

        @block.gpsimd
        def _(pool):
            pool.memset(parts[:, :, :], 0.0).then_inc(parts_zeroed, 1)
            pool.wait_ge(k.consts_loaded, k.consts_total)

            def gather(i, half):
                c = i * 2 + half
                pool.wait_ge(heads_turned, c + 1)
                src = k.att[:, ds(i * S, S)].rearrange("p (g t c) -> p t g c", g=GB, c=GW)[:, half * CT:(half + 1) * CT]
                pool.tensor_copy(heads[:, :, :].rearrange("p t (g c) -> p t g c", c=GW), src).then_inc(heads_ready, 1)

            def root(c, n, var, done):
                pool.wait_ge(var, c + 1)
                pool.tensor_tensor(rstd[:, n], var_eps[:, n], k.minus_half[:, 0:CT], ALU.pow).then_inc(done, 1)

            def add_normed(c):
                pool.wait_ge(yn_ready, (c + 1) * CT)
                gamma = k.gamma[:, :].unsqueeze(1).broadcast_to([P, CT, D])
                beta = k.beta[:, :].unsqueeze(1).broadcast_to([P, CT, D])
                pool.tensor_tensor(yn[:, :, :], yn[:, :, :], gamma, ALU.mult).then_inc(pool_steps, 1)
                pool.wait_ge(pool_steps, c * 2 + 1)
                pool.tensor_tensor(yn[:, :, :], yn[:, :, :], beta, ALU.add).then_inc(pool_steps, 1)
                pool.wait_ge(pool_steps, c * 2 + 2)
                pool.tensor_tensor(chunk(k.x, c), chunk(k.x, c), yn[:, :, :], ALU.add).then_inc(x_added, 1)

            def out_ready(i, half):
                c = i * 2 + half
                gather(i, half)
                root(c, 1, y_var_ready, y_rstd_ready)
                add_normed(c)

            def in_ready(c):
                root(c, 0, var_ready, rstd_ready)

            def body(i, par, last):
                if not (last and par):
                    in_ready(i * 2 + par + 1)
                if after_attention and not last:
                    out_ready(i + 1, par)

            if after_attention:
                out_ready(0, 0)
                out_ready(0, 1)
            in_ready(0)
            with pool.Fori(0, LAST) as i:
                body(i, 0, False)
                body(i, 1, False)
            body(LAST, 0, True)

        @block.scalar
        def _(act):
            def heads_out(c):
                act.wait_ge(heads_turned, c + 2)
                act.copy(headsT[:, :], psX[:, :]).then_inc(headsT_ready, 1)

            def xn_out(c, par):
                act.wait_ge(xn_turned, c + 2)
                act.copy(xnT[:, par], psX[:, :]).then_inc(xnT_ready, 1)

            def tanh(c):
                act.wait_ge(margin_ready, c + 1)
                act.activation(half_tanh[:, :, :], margin[:, :, :], ACT.Tanh).then_inc(tanh_ready, 1)

            def parts_out(c, par):
                act.wait_ge(parts_turned, c + 2)
                act.copy(partsT[:, par], psX[:, 0:CH // 2].bitcast(BF16)).then_inc(partsT_ready, 1)

            def gate(c, e):
                n = c * NE + e
                act.wait_ge(p_ready, n + 1)
                act.wait_ge(hidden_ready, n + 1)
                act.activation(silu[:, e % 2], psP[e % 2][:, :], ACT.Silu).then_inc(silu_ready, 1)

            def body(i, par, last):
                c = i * 2 + par
                for e in range(NE):
                    if e + 1 < NE:
                        gate(c, e + 1)
                    elif not (last and par):
                        gate(c + 1, 0)
                    if not (last and par):
                        if e == 1:
                            xn_out(c + 1, 1 - par)
                        if e == 4:
                            tanh(c + 1)
                        if e == 6:
                            parts_out(c + 1, 1 - par)
                    if after_attention and not last and e == 4:
                        heads_out(c + 2)
                act.wait_ge(down_steps, (c + 1) * NE + 2)
                act.wait_ge(o_turned, c + 1)
                act.copy(oT[:, :], psO[:, :]).then_inc(o_copied, 1)

            if after_attention:
                heads_out(0)
                heads_out(1)
            xn_out(0, 0)
            tanh(0)
            parts_out(0, 0)
            gate(0, 0)
            with act.Fori(0, LAST) as i:
                body(i, 0, False)
                body(i, 1, False)
            body(LAST, 0, True)
            body(LAST, 1, True)

        @block.vector
        def _(dve):
            dve.wait_ge(parts_zeroed, 1)
            dve.wait_ge(k.consts_loaded, k.consts_total)
            for b in range(B):
                dve.wait_ge(k.x_loaded[b], 16)
            OUT_PER, IN_PER = CT + NORM_STEPS, CT + NORM_STEPS + 13

            def norm(c, n, step, src, out, var, root, done):
                for t in range(CT):
                    step.did(dve.bn_stats(stats[:, t], src(t)))
                step.wait()
                gather_stats(dve, step, stats, moments, mean, var_eps[:, n]).then_inc(var, 1)
                dve.wait_ge(root, c + 1)
                for t in range(CT):
                    dve.tensor_scalar(out[:, t], src(t), mean[:, t:t + 1], rstd[:, n, t:t + 1],
                                      ALU.subtract, ALU.mult).then_inc(done, 1)

            def out_norm(c):
                step = Chain(dve, out_steps, OUT_PER, c)
                dve.wait_ge(projected, c + 1)
                dve.tensor_tensor(y[:, :, :], psY[:, :].rearrange("p (t d) -> p t d", d=D), chunk(k.xn, c),
                                  ALU.add).then_inc(y_taken, 1)
                dve.wait_ge(y_taken, c + 2)
                dve.wait_ge(x_added, c + 1)
                norm(c, 1, step, lambda t: y[:, t], yn, y_var_ready, y_rstd_ready, yn_ready)
                step.end()

            def in_norm(c, step):
                if after_attention:
                    dve.wait_ge(x_added, c + 2)
                dve.wait_ge(xn_turned, c + 1)
                norm(c, 0, step, lambda t: k.x[:, ds((c * CT + t) * D, D)], xn, var_ready, rstd_ready, xn_ready)

            def rank_experts(c, step):
                dve.wait_ge(routed, c + 1)
                dve.tensor_copy(logit[:, :, :], psY[:, 0:CT * E].rearrange("p (t e) -> p t e", e=E)).then_inc(logit_taken, 1)
                dve.wait_ge(logit_taken, c + 2)
                of = logit[:, :, :].unsqueeze(3).broadcast_to([P, CT, E, E])
                other = logit[:, :, :].unsqueeze(2).broadcast_to([P, CT, E, E])
                before = k.before[:, :].rearrange("p (a b) -> p a b", a=E).unsqueeze(1).broadcast_to([P, CT, E, E])
                step.did(dve.tensor_tensor(above[:, :, :, :], other, of, ALU.is_gt))
                step.did(dve.tensor_tensor(equal[:, :, :, :], other, of, ALU.is_equal))
                step.wait()
                step.did(dve.tensor_tensor(equal[:, :, :, :], equal[:, :, :, :], before, ALU.mult))
                step.wait()
                step.did(dve.tensor_tensor(above[:, :, :, :], above[:, :, :, :], equal[:, :, :, :], ALU.add))
                step.wait()
                step.did(dve.tensor_reduce(rank[:, :, :], above[:, :, :, :], AX_X, ALU.add))
                step.wait()

            def take_experts(c, step):
                step.did(dve.tensor_scalar(taken[:, :, :], rank[:, :, :], TOPK - 0.5, None, ALU.is_lt))
                step.wait()
                step.did(dve.tensor_tensor(taken_logit[:, :, :], logit[:, :, :], taken[:, :, :], ALU.mult))
                step.wait()
                step.did(dve.tensor_reduce(logit_sum[:, :], taken_logit[:, :, :], AX_X, ALU.add))
                step.wait()
                dve.scalar_tensor_tensor(out=margin[:, :, :], in0=logit_sum[:, :].unsqueeze(2).broadcast_to([P, CT, E]),
                                         scalar=-0.5, in1=logit[:, :, :], op0=ALU.mult, op1=ALU.add).then_inc(margin_ready, 1)

            def split_shares(c, step):
                dve.wait_ge(tanh_ready, c + 1)
                step.did(dve.tensor_scalar(share[:, :, :], half_tanh[:, :, :], 0.5, 0.5, ALU.mult, ALU.add))
                step.wait()
                step.did(dve.tensor_tensor(share[:, :, :], share[:, :, :], taken[:, :, :], ALU.mult))
                step.wait()
                dve.wait_ge(parts_turned, c + 1)
                step.did(dve.tensor_copy(parts[:, :, 0:E], share[:, :, :]))
                step.wait()
                step.did(dve.tensor_tensor(rest[:, :, :], share[:, :, :], parts[:, :, 0:E], ALU.subtract))
                step.wait()
                step.did(dve.tensor_copy(parts[:, :, E:2 * E], rest[:, :, :]))
                step.wait()
                dve.tensor_tensor(parts[:, :, 2 * E:3 * E], rest[:, :, :], parts[:, :, E:2 * E],
                                  ALU.subtract).then_inc(parts_ready, 1)

            def hide(c, e):
                n = c * NE + e
                dve.wait_ge(silu_ready, n + 1)
                src = silu[:, e % 2]
                if e < E:
                    dve.wait_ge(c_ready, c * E + e + 1)
                    dve.tensor_tensor(scaled[:, e % 2], silu[:, e % 2], psC[:, :], ALU.mult).then_inc(scaled_ready, 1)
                    dve.wait_ge(scaled_ready, c * E + e + 2)
                    src = scaled[:, e % 2]
                dve.wait_ge(g_ready, n + 1)
                dve.wait_ge(down_steps, n + 1)
                dve.tensor_tensor(hidden[:, e % 2], src, psG[e % 2][:, :], ALU.mult).then_inc(hidden_ready, 1)

            def finish(c):
                dve.wait_ge(o_turned, c + 2)
                dve.tensor_tensor(chunk(k.x, c), chunk(k.x, c), psY[:, :].rearrange("p (t d) -> p t d", d=D),
                                  ALU.add).then_inc(o_added, 2)

            def body(i, par, last):
                c = i * 2 + par
                step = Chain(dve, in_steps, IN_PER, c + 1)
                for e in range(NE):
                    if e + 1 < NE:
                        hide(c, e + 1)
                    elif not (last and par):
                        hide(c + 1, 0)
                    if not (last and par):
                        if e == 0:
                            in_norm(c + 1, step)
                        if e == 3:
                            rank_experts(c + 1, step)
                            take_experts(c + 1, step)
                        if e == 4:
                            split_shares(c + 1, step)
                            step.end()
                    if after_attention and not last and e == 6:
                        out_norm(c + 2)
                finish(c)

            if after_attention:
                out_norm(0)
                out_norm(1)
            step = Chain(dve, in_steps, IN_PER, 0)
            in_norm(0, step)
            rank_experts(0, step)
            take_experts(0, step)
            split_shares(0, step)
            step.end()
            hide(0, 0)
            with dve.Fori(0, LAST) as i:
                body(i, 0, False)
                body(i, 1, False)
            body(LAST, 0, True)
            body(LAST, 1, True)

        @block.tensor
        def _(pe):
            for s, n in ((xn_turned, 1), (parts_turned, 1), (logit_taken, 1), (hidden_ready, 2), (down_steps, 2),
                         (scaled_ready, 1), (o_turned, 1), (o_copied, 1), (o_added, 2), (xnT_ready, 1), (partsT_ready, 1)):
                pe.sem_inc(s, n)
            if after_attention:
                for s in (heads_turned, y_taken, x_added, headsT_ready):
                    pe.sem_inc(s, 1)
            pe.wait_ge(k.ffn_weights_loaded, k.ffn_weights_total)
            pe.wait_ge(k.consts_loaded, k.consts_total)

            def turn_heads(c):
                pe.wait_ge(heads_ready, c + 1)
                for t in range(CT):
                    mm = pe.transpose(psX[:, t * P:(t + 1) * P], heads[:, t], k.ident[:, :])
                mm.then_inc(heads_turned, 1)

            def project_heads(c):
                pe.wait_ge(headsT_ready, c + 2)
                for t in range(CT):
                    cols = slice(t * P, (t + 1) * P)
                    mm = pe.matmul(psY[:, cols], headsT[:, cols], k.w_out[:, :], start=True, stop=True)
                mm.then_inc(projected, 1)

            def turn_xn(c):
                pe.wait_ge(xn_ready, (c + 1) * CT)
                for t in range(CT):
                    mm = pe.transpose(psX[:, t * P:(t + 1) * P], xn[:, t], k.ident[:, :])
                mm.then_inc(xn_turned, 1)

            def route(c, par):
                pe.wait_ge(xnT_ready, c + 2)
                pe.wait_ge(o_added, c + 1)
                for t in range(CT):
                    mm = pe.matmul(psY[:, t * E:(t + 1) * E], xnT[:, par, t * P:(t + 1) * P], k.w_router[:, :],
                                   start=True, stop=True)
                mm.then_inc(routed, 1)

            def turn_parts(c):
                pe.wait_ge(parts_ready, c + 1)
                pe.wait_ge(xnT_ready, c + 2)
                for t in range(CT):
                    mm = pe.transpose(psX[:, t * P // 2:(t + 1) * P // 2].bitcast(BF16), parts[:, t], k.ident_b[:, :])
                mm.then_inc(parts_turned, 1)

            def up(c, par, e):
                n = c * NE + e
                if e == 0:
                    pe.wait_ge(xnT_ready, c + 2)
                pe.wait_ge(hidden_ready, n + 1)
                pe.matmul(psP[e % 2][:, :], k.w1[:, e, 0:I], xnT[:, par], start=True, stop=True).then_inc(p_ready, 1)
                pe.matmul(psG[e % 2][:, :], k.w1[:, e, I:2 * I], xnT[:, par], start=True, stop=True).then_inc(g_ready, 1)
                if e < E:
                    if e == 0:
                        pe.wait_ge(partsT_ready, c + 2)
                    pe.wait_ge(scaled_ready, c * E + e + 1)
                    pe.matmul(psC[:, :], k.spread[:, e], partsT[:, par], start=True, stop=True).then_inc(c_ready, 1)

            def down(c, e):
                n = c * NE + e
                pe.wait_ge(hidden_ready, n + 3)
                if e == 0:
                    pe.wait_ge(o_copied, c + 1)
                mm = pe.matmul(psO[:, :], k.w2[:, e], hidden[:, e % 2], start=(e == 0), stop=(e == NE - 1))
                mm.then_inc(down_steps, 1)

            def turn_out(c):
                pe.wait_ge(o_copied, c + 2)
                for t in range(CT):
                    mm = pe.transpose(psY[:, t * P:(t + 1) * P], oT[:, t * P:(t + 1) * P], k.ident[:, :])
                mm.then_inc(o_turned, 1)

            def body(i, par, last):
                c = i * 2 + par
                for e in range(NE):
                    if e + 2 < NE:
                        up(c, par, e + 2)
                    elif not (last and par):
                        up(c + 1, 1 - par, e + 2 - NE)
                    down(c, e)
                    if not (last and par):
                        if e == 1:
                            turn_xn(c + 1)
                        if e == 3:
                            route(c + 1, 1 - par)
                    if after_attention and not last:
                        if e == 4:
                            turn_heads(c + 2)
                        if e == 6:
                            pe.wait_ge(logit_taken, c + 3)
                            project_heads(c + 2)
                    if not (last and par) and e == 6:
                        turn_parts(c + 1)
                if after_attention and not last:
                    pe.wait_ge(y_taken, c + 4)
                turn_out(c)

            if after_attention:
                turn_heads(0)
                project_heads(0)
                turn_heads(1)
                pe.wait_ge(y_taken, 2)
                project_heads(1)
                pe.wait_ge(y_taken, 3)
            turn_xn(0)
            route(0, 0)
            turn_parts(0)
            up(0, 0, 0)
            up(0, 0, 1)
            with pe.Fori(0, LAST) as i:
                body(i, 0, False)
                body(i, 1, False)
            body(LAST, 0, True)
            body(LAST, 1, True)


SSM_UNITS = dict(
    take_stats=0, mix=1, norm=2, mean_square=5, rms_norm=9, add_out=10, take_z=28,
    norm_root=0, rms_root=6, add_resid=5,
    squares=4, gates=5, xT_out=11, channels_out=24, low_out=26, soften=31,
    skip=1, project_out=6, turn=6, convolve=12, lower=21, raise_z=23,
)


def state_space(nc, k):
    with ExitStack() as ctx:
        sb = lambda n, s, d=F32: ctx.enter_context(nc.sbuf_tensor("ssm_" + n, s, d))
        sem = lambda n: ctx.enter_context(nc.semaphore("ssm_" + n))
        RING, ROWS = 3, 4
        PARTS_OUT = 4
        FREE = ROWS * MT
        PAD = 4
        stats = sb("stats", [P, TB, 6])
        moments = sb("moments", [P, TB, 8])
        mean, var_eps, rstd = sb("mean", [P, TB]), sb("var_eps", [P, TB]), sb("rstd", [P, TB])
        square_sum, ms_eps, rrms = sb("square_sum", [P, TB]), sb("ms_eps", [P, TB]), sb("rrms", [P, TB])
        resid = sb("resid", [P, TB, D])
        xr = sb("xr", [P, TB, D])
        xT = sb("xT", [P, PAD + S])
        gate = sb("gate", [P, MT, S])
        xs = sb("xs", [P, 2, MT, S])
        low = sb("low", [MR + 2 * MN, S])
        z = sb("z", [P, MT, S])
        soft = sb("soft", [P, MT, S])
        delta = sb("delta", [P, MT, S])
        dx = sb("dx", [P, MT, S])
        b_all = sb("b_all", [P, ROWS, S])
        c_all = sb("c_all", [P, ROWS, S])
        decay = sb("decay", [P, RING, S])
        feed = sb("feed", [P, RING, S])
        state = sb("state", [P, RING, S])
        part = sb("part", [P, PARTS_OUT, S])
        conv_in = k.conv_w
        neg_a = sb("neg_a", [P, MT, MN])
        psY = ctx.enter_context(nc.psum_tensor("ssm_psY", [P, MT, S], F32))
        ps = [ctx.enter_context(nc.psum_tensor(f"ssm_ps{j}", [P, S], F32)) for j in range(2)]
        folded, exp_a, a_ready, padded = sem("folded"), sem("exp_a"), sem("a_ready"), sem("padded")
        dve_steps = sem("dve_steps")
        var_ready, rstd_ready, resid_ready = sem("var_ready"), sem("rstd_ready"), sem("resid_ready")
        squared, ms_ready, rrms_ready, xr_ready = sem("squared"), sem("ms_ready"), sem("rrms_ready"), sem("xr_ready")
        turned, xT_ready = sem("turned"), sem("xT_ready")
        skip_done, gate_ready = sem("skip_done"), sem("gate_ready")
        conv_done, xs_ready = sem("conv_done"), sem("xs_ready")
        low_done, low_ready = sem("low_done"), sem("low_ready")
        bc_stored = sem("bc_stored")
        z_done, z_ready, abs_ready, exp_ready, log_ready = sem("z_done"), sem("z_ready"), sem("abs_ready"), sem("exp_ready"), sem("log_ready")
        delta_ready, dx_ready = sem("delta_ready"), sem("dx_ready")
        b_loaded, c_loaded = ([sem(f"{r}_loaded{n}") for n in range(ROWS)] for r in "bc")
        decay_ready, feed_ready, state_ready, part_ready = sem("decay_ready"), sem("feed_ready"), sem("state_ready"), sem("part_ready")
        summed = sem("summed")
        skipped, y_ready, out_done = sem("skipped"), sem("y_ready"), sem("out_done")
        resid_added, batch_done = sem("resid_added"), sem("batch_done")
        block = ctx.enter_context(nc.Block())
        halves = [slice(h * HALF, (h + 1) * HALF) for h in range(2)]
        batch = lambda b: k.x[:, ds(b * S, S)].rearrange("p (t d) -> p t d", d=D)

        at = SSM_UNITS

        def over_batches(eng, body):
            body(0, 0, True, False)
            with eng.Fori(0, (B - 2) // 2) as i:
                body(i * 2 + 1, 1, False, False)
                body(i * 2 + 2, 0, False, False)
            body(B - 1, 1, False, True)

        def ring_free(b, u):
            return b * UNITS + max(u + 1, RING if u else UNITS % RING)

        @block.sync
        def _(sp):
            with sp.Fori(0, B) as b:
                sp.wait_ge(low_ready, b + 1)
                sp.dma_start(k.bc_rows[ds(b, 1)].rearrange("o r s -> (o r) s"), low[MR:, :]).then_inc(bc_stored, 16)
                sp.wait_ge(bc_stored, b * 16 + 16)
                for n in range(MN):
                    sp.wait_ge(feed_ready, b * UNITS + (n + 1) * MT)
                    sp.dma_start(b_all[:, n % ROWS], k.bc_rows[ds(b, 1), n, :].broadcast_to([P, S])).then_inc(b_loaded[n % ROWS], 16)
                    sp.wait_ge(part_ready, b * UNITS + (n + 1) * MT)
                    sp.dma_start(c_all[:, n % ROWS], k.bc_rows[ds(b, 1), MN + n, :].broadcast_to([P, S])).then_inc(c_loaded[n % ROWS], 16)

        @block.gpsimd
        def _(pool):
            pool.wait_ge(k.consts_loaded, k.consts_total)
            pool.memset(xT[:, 0:PAD], 0.0).then_inc(padded, 1)

            def norm_root(c):
                pool.wait_ge(var_ready, c + 1)
                pool.tensor_tensor(rstd[:, :], var_eps[:, :], k.minus_half[:, 0:TB], ALU.pow).then_inc(rstd_ready, 1)

            def add_resid(c):
                pool.wait_ge(resid_ready, (c + 1) * TB)
                pool.tensor_tensor(batch(c), batch(c), resid[:, :, :], ALU.add).then_inc(resid_added, 1)

            def rms_root(c):
                pool.wait_ge(ms_ready, c + 1)
                pool.tensor_tensor(rrms[:, :], ms_eps[:, :], k.minus_half[:, 0:TB], ALU.pow).then_inc(rrms_ready, 1)

            def body(b, par, first, last):
                for u in range(UNITS):
                    n, et, m = u // MT, u % MT, b * UNITS + u
                    if et == 0:
                        pool.wait_ge(c_loaded[n % ROWS], (b * (MN // ROWS) + n // ROWS + 1) * 16)
                    pool.wait_ge(state_ready, RING + m + 1)
                    pool.wait_ge(summed, m + 1)
                    pool.tensor_tensor(part[:, u % PARTS_OUT], state[:, u % RING], c_all[:, n % ROWS], ALU.mult).then_inc(part_ready, 1)
                    if last:
                        continue
                    if u == at["norm_root"]:
                        norm_root(b + 1)
                    if u == at["rms_root"]:
                        rms_root(b + 1)
                    if u == at["add_resid"]:
                        add_resid(b + 1)

            norm_root(0)
            rms_root(0)
            add_resid(0)
            over_batches(pool, body)

        @block.scalar
        def _(act):
            act.wait_ge(k.ssm_weights_loaded, k.ssm_weights_total)
            act.activation(neg_a[:, :, :], k.a_log[:, :, :], ACT.Exp).then_inc(exp_a, 1)
            act.wait_ge(padded, 1)
            act.wait_ge(a_ready, 1)

            def squares(c):
                act.wait_ge(turned, c)
                act.wait_ge(resid_ready, (c + 1) * TB)
                for j in range(TB):
                    act.activation(xr[:, j], resid[:, j], ACT.Square, accum_out=square_sum[:, j:j + 1]).then_inc(squared, 1)

            def xT_out(c):
                act.wait_ge(turned, c + 1)
                act.wait_ge(skip_done, c * MT)
                act.mul(xT[:, PAD:], ps[0][:, :], k.norm_w[:, 0:1]).then_inc(xT_ready, 1)

            def gates(b):
                act.wait_ge(y_ready, (b + 1) * MT)
                for et in range(MT):
                    act.wait_ge(skip_done, b * MT + et + 1)
                    act.activation(gate[:, et], ps[et][:, :], ACT.Silu).then_inc(gate_ready, 1)

            def channels_out(c, par):
                act.wait_ge(skipped, c * MT)
                for et in range(MT):
                    act.wait_ge(conv_done, c * MT + et + 1)
                    act.activation(xs[:, par, et], ps[1 - et][:, :], ACT.Silu, bias=k.conv_b[:, et:et + 1]).then_inc(xs_ready, 1)

            def low_out(c):
                act.wait_ge(low_done, c + 1)
                act.wait_ge(bc_stored, c * 16)
                act.copy(low[:, :], ps[1][0:MR + 2 * MN, :]).then_inc(low_ready, 1)

            def soften(c):
                act.wait_ge(z_ready, (c + 1) * MT)
                act.wait_ge(delta_ready, c * MT)
                act.activation(soft[:, :, :], z[:, :, :], ACT.Abs).then_inc(abs_ready, 1)
                act.wait_ge(abs_ready, c + 1)
                act.activation(soft[:, :, :], soft[:, :, :], ACT.Exp, scale=-1.0).then_inc(exp_ready, 1)
                act.wait_ge(exp_ready, c + 1)
                act.activation(soft[:, :, :], soft[:, :, :], ACT.Ln, bias=1.0).then_inc(log_ready, 1)

            def body(b, par, first, last):
                for u in range(UNITS):
                    n, et, m = u // MT, u % MT, b * UNITS + u
                    if u < MT:
                        act.wait_ge(delta_ready, b * MT + et + 1)
                    act.wait_ge(state_ready, ring_free(b, u))
                    act.activation(decay[:, u % RING], delta[:, et], ACT.Exp, scale=neg_a[:, et, n:n + 1]).then_inc(decay_ready, 1)
                    if u == at["gates"]:
                        gates(b)
                    if last:
                        continue
                    if u == at["squares"]:
                        squares(b + 1)
                    if u == at["xT_out"]:
                        xT_out(b + 1)
                    if u == at["channels_out"]:
                        channels_out(b + 1, 1 - par)
                    if u == at["low_out"]:
                        low_out(b + 1)
                    if u == at["soften"]:
                        soften(b + 1)

            squares(0)
            xT_out(0)
            channels_out(0, 0)
            low_out(0)
            soften(0)
            over_batches(act, body)

        @block.vector
        def _(dve):
            for b in range(B):
                dve.wait_ge(k.x_loaded[b], 16)
            dve.wait_ge(k.ssm_weights_loaded, k.ssm_weights_total)
            for t in range(MC):
                dve.tensor_tensor(conv_in[:, t], k.in_w[:, :], k.conv_w[:, t], ALU.mult).then_inc(folded, 1)
            dve.wait_ge(exp_a, 1)
            dve.tensor_scalar(neg_a[:, :, :], neg_a[:, :, :], -1.0, None, ALU.mult).then_inc(a_ready, 1)

            def take_stats(c):
                step = Chain(dve, dve_steps, TB + NORM_STEPS, c)
                for j in range(TB):
                    step.did(dve.bn_stats(stats[:, j], k.x[:, ds((c * TB + j) * D, D)]))
                step.wait()
                gather_stats(dve, step, stats, moments, mean, var_eps[:, :]).then_inc(var_ready, 1)
                step.end()

            def norm(c):
                dve.wait_ge(rstd_ready, c + 1)
                dve.wait_ge(resid_added, c)
                dve.wait_ge(xr_ready, c * TB)
                for j in range(TB):
                    dve.tensor_scalar(resid[:, j], k.x[:, ds((c * TB + j) * D, D)], mean[:, j:j + 1],
                                      rstd[:, j:j + 1], ALU.subtract, ALU.mult).then_inc(resid_ready, 1)

            def mean_square(c):
                dve.wait_ge(squared, (c + 1) * TB)
                dve.tensor_scalar(ms_eps[:, :], square_sum[:, :], 1.0 / D, LN_EPS, ALU.mult, ALU.add).then_inc(ms_ready, 1)

            def rms_norm(c):
                dve.wait_ge(rrms_ready, c + 1)
                for j in range(TB):
                    dve.tensor_scalar(xr[:, j], resid[:, j], rrms[:, j:j + 1], None, ALU.mult).then_inc(xr_ready, 1)

            def take_z(c, et):
                dve.wait_ge(z_done, c * MT + et + 1)
                dve.tensor_scalar(z[:, et], ps[et][:, :], k.wd2_b[:, et:et + 1], None, ALU.add).then_inc(z_ready, 1)

            def make_delta(c, par):
                dve.wait_ge(log_ready, c + 1)
                for et in range(MT):
                    dve.scalar_tensor_tensor(out=delta[:, et], in0=z[:, et], scalar=0.0, in1=soft[:, et], op0=ALU.max,
                                             op1=ALU.add).then_inc(delta_ready, 1)
                for et in range(MT):
                    dve.wait_ge(delta_ready, c * MT + et + 1)
                    dve.tensor_tensor(dx[:, et], delta[:, et], xs[:, par, et], ALU.mult).then_inc(dx_ready, 1)

            def mix(f, par):
                dve.wait_ge(summed, PARTS_OUT + (f + 1) * UNITS)
                for et in range(MT):
                    dve.scalar_tensor_tensor(out=z[:, et], in0=xs[:, par, et], scalar=k.w_d[:, et:et + 1], in1=psY[:, et],
                                             op0=ALU.mult, op1=ALU.add).then_inc(skipped, 1)
                for et in range(MT):
                    dve.wait_ge(skipped, (f + 1) * MT + et + 1)
                    dve.tensor_tensor(z[:, et], z[:, et], gate[:, et], ALU.mult).then_inc(y_ready, 1)

            def add_out(f):
                dve.wait_ge(out_done, f + 1)
                dve.wait_ge(resid_added, f + 1)
                dve.tensor_tensor(batch(f), batch(f), ps[1][:, :].rearrange("p (t d) -> p t d", d=D), ALU.add).then_inc(batch_done, 1)

            def feed_unit(b, u):
                n, et = u // MT, u % MT
                if u < MT:
                    dve.wait_ge(dx_ready, b * MT + et + 1)
                if et == 0:
                    dve.wait_ge(b_loaded[n % ROWS], (b * (MN // ROWS) + n // ROWS + 1) * 16)
                dve.wait_ge(state_ready, ring_free(b, u))
                dve.tensor_tensor(feed[:, u % RING], dx[:, et], b_all[:, n % ROWS], ALU.mult).then_inc(feed_ready, 1)

            def body(b, par, first, last):
                feed_unit(b, 0)
                for u in range(UNITS):
                    et, m = u % MT, b * UNITS + u
                    if u + 1 < UNITS:
                        feed_unit(b, u + 1)
                    dve.wait_ge(feed_ready, FREE + m + 1)
                    dve.wait_ge(decay_ready, m + 1)
                    dve.wait_ge(part_ready, FREE + ring_free(b, u) - RING)
                    dve.tensor_tensor_scan(state[:, u % RING], decay[:, u % RING], feed[:, u % RING], 0.0, ALU.mult, ALU.add).then_inc(state_ready, 1)
                    if not first:
                        if u == at["mix"]:
                            mix(b - 1, 1 - par)
                        if u == at["add_out"]:
                            add_out(b - 1)
                    if last:
                        continue
                    if u == at["take_stats"]:
                        take_stats(b + 1)
                    if u == at["norm"]:
                        norm(b + 1)
                    if u == at["mean_square"]:
                        mean_square(b + 1)
                    if u == at["rms_norm"]:
                        rms_norm(b + 1)
                    if u == at["take_z"]:
                        take_z(b + 1, 0)
                        take_z(b + 1, 1)
                if not last:
                    make_delta(b + 1, 1 - par)

            take_stats(0)
            norm(0)
            mean_square(0)
            rms_norm(0)
            take_z(0, 0)
            take_z(0, 1)
            make_delta(0, 0)
            over_batches(dve, body)
            mix(B - 1, 1)
            add_out(B - 1)

        @block.tensor
        def _(pe):
            pe.wait_ge(folded, MC)
            pe.wait_ge(k.consts_loaded, k.consts_total)
            pe.wait_ge(k.ssm_weights_loaded, k.ssm_weights_total)
            for s, n in ((state_ready, RING), (part_ready, FREE), (feed_ready, FREE), (summed, PARTS_OUT),
                         (batch_done, 1), (skipped, MT), (y_ready, MT)):
                pe.sem_inc(s, n)

            def product(out, rows, cols, w, src):
                for j in range(len(w)):
                    mm = pe.matmul(out[0:rows, cols], w[j], src(j, cols), start=(j == 0), stop=(j == len(w) - 1))
                return mm

            shift = lambda t: lambda j, cols: xT[:, PAD + t + j + cols.start:PAD + t + j + cols.stop]
            channels = [slice(et * P, (et + 1) * P) for et in range(MT)]

            def turn(c):
                pe.wait_ge(xr_ready, (c + 1) * TB)
                for j in range(TB):
                    mm = pe.transpose(ps[0][:, j * P:(j + 1) * P], xr[:, j], k.ident[:, :])
                mm.then_inc(turned, 1)

            def skip(b, et):
                pe.wait_ge(z_ready, (b + 1) * MT)
                for cols in halves:
                    mm = product(ps[et], P, cols, [k.skip_w[:, channels[et]]], shift(0))
                mm.then_inc(skip_done, 1)

            def convolve(c, et, h):
                if et == 0 and h == 0:
                    pe.wait_ge(xT_ready, c + 1)
                    pe.wait_ge(batch_done, c)
                mm = product(ps[1 - et], P, halves[h], [conv_in[:, t, channels[et]] for t in range(MC)], shift(1 - MC))
                if h == 1:
                    mm.then_inc(conv_done, 1)

            def lower(c, par, h):
                pe.wait_ge(xs_ready, (c + 1) * MT)
                mm = product(ps[1], MR + 2 * MN, halves[h], [k.w_low[:, et] for et in range(MT)],
                             lambda j, cols: xs[:, par, j, cols])
                if h == 1:
                    mm.then_inc(low_done, 1)

            def raise_z(c, et):
                pe.wait_ge(low_ready, c + 1)
                for cols in halves:
                    mm = product(ps[et], P, cols, [k.wd2[0:MR + 2 * MN, channels[et]]], lambda j, cols: low[:, cols])
                mm.then_inc(z_done, 1)

            def project_out(f, idle):
                pe.wait_ge(y_ready, (f + 2) * MT)
                if not idle:
                    pe.wait_ge(gate_ready, (f + 2) * MT)
                for j in range(TB):
                    cols = slice(j * P, (j + 1) * P)
                    for et in range(MT):
                        mm = pe.matmul(ps[1][:, cols], z[:, et, cols], k.out_w[:, et], start=(et == 0), stop=(et == MT - 1))
                mm.then_inc(out_done, 1)

            def body(b, par, first, last):
                for u in range(UNITS):
                    n, et, m = u // MT, u % MT, b * UNITS + u
                    if n == 0:
                        pe.wait_ge(skipped, b * MT + et + 1)
                    pe.wait_ge(part_ready, FREE + m + 1)
                    for cols in halves:
                        mm = pe.matmul(psY[:, et, cols], k.ident[:, :], part[:, u % PARTS_OUT, cols], start=(n == 0), stop=(n == MN - 1))
                    mm.then_inc(summed, 1)
                    if u - at["skip"] in range(MT):
                        skip(b, u - at["skip"])
                    if not first and u == at["project_out"]:
                        project_out(b - 1, False)
                    if last:
                        continue
                    if u == at["turn"]:
                        turn(b + 1)
                    if u - at["convolve"] in range(0, 4 * MT, 2):
                        convolve(b + 1, (u - at["convolve"]) // 4, (u - at["convolve"]) // 2 % 2)
                    if u - at["lower"] in range(2):
                        lower(b + 1, 1 - par, u - at["lower"])
                    if u - at["raise_z"] in range(MT):
                        raise_z(b + 1, u - at["raise_z"])

            turn(0)
            for et in range(MT):
                for h in range(2):
                    convolve(0, et, h)
            lower(0, 0, 0)
            lower(0, 0, 1)
            raise_z(0, 0)
            raise_z(0, 1)
            over_batches(pe, body)
            project_out(B - 1, True)
def build_program(nc, a, out):
    with ExitStack() as ctx:
        sb = lambda n, s, d=F32: ctx.enter_context(nc.sbuf_tensor(n, s, d))
        sem = lambda n: ctx.enter_context(nc.semaphore(n))
        k = Names()
        k.x = sb("x", [P, B * S])
        w_qkv = sb("w_qkv", [P, 3, D])
        k.w_q, k.w_k, k.w_v = (w_qkv[:, j] for j in range(3))
        k.w_out = sb("w_out", [P, D])
        k.b_out, k.gamma, k.beta = sb("b_out", [P, D]), sb("gamma", [P, D]), sb("beta", [P, D])
        k.ident = sb("ident", [P, P])
        k.minus_half = sb("minus_half", [P, 2 * TB])
        k.before = sb("before", [P, E * E])
        k.ident_b = sb("ident_b", [P, P], BF16)
        k.spread = sb("spread", [P, E, P], BF16)
        k.w_router = sb("w_router", [P, E])
        k.w1 = sb("w1", [P, NE, 2 * I])
        k.w2 = sb("w2", [P, NE, D])
        k.norm_w = sb("norm_w", [P, 1])
        k.skip_w, k.in_w = sb("skip_w", [P, ME]), sb("in_w", [P, ME])
        k.conv_w = sb("conv_w", [P, MC, ME])
        k.conv_b, k.wd2_b, k.w_d = sb("conv_b", [P, MT]), sb("wd2_b", [P, MT]), sb("w_d", [P, MT])
        k.w_low, k.wd2 = sb("w_low", [P, MT, MR + 2 * MN]), sb("wd2", [P, ME])
        k.a_log, k.out_w = sb("a_log", [P, MT, MN]), sb("out_w", [P, MT, D])
        k.bc_rows = nc.dram_tensor("bc_rows", [B, 2 * MN, S], F32, kind="Internal").ap()
        k.ssm_weights_loaded = sem("ssm_weights_loaded")
        k.q_terms = nc.dram_tensor("q_terms", [B, H, NT, HD, S], BF16, kind="Internal").ap()
        k.k_terms = nc.dram_tensor("k_terms", [B, H, NT, HD, S], BF16, kind="Internal").ap()
        k.x_loaded, k.consts_loaded = [sem(f"x_loaded{b}") for b in range(B)], sem("consts_loaded")
        k.attn_weights_loaded, k.ffn_weights_loaded = sem("attn_weights_loaded"), sem("ffn_weights_loaded")
        stored = sem("out_stored")
        k.spread_loaded, wd2_zeroed = sem("spread_loaded"), sem("wd2_zeroed")

        def load_later_weights(sp):
            tiles = lambda name: a[name].rearrange("(t p) c -> p t c", p=P)
            sp.dma_start(k.spread_f[:, :], a["spread"]).then_inc(k.spread_loaded, 16)
            for dst, src in ((k.w_out[:, :], a["w_out"]), (k.w_router[:, :], a["w_router"]),
                             (k.w1[:, 0:E], a["fc1"].rearrange("e d f -> d e f")),
                             (k.w1[:, E:NE, 0:I], a["gate_w"].rearrange("d (s f) -> d s f", s=2)),
                             (k.w1[:, E:NE, I:2 * I], a["up_w"].rearrange("d (s f) -> d s f", s=2)),
                             (k.w2[:, 0:E], a["fc2"].rearrange("e i d -> i e d")),
                             (k.w2[:, E:NE], a["down_w"].rearrange("(s i) d -> i s d", s=2))):
                sp.dma_start(dst, src).then_inc(k.ffn_weights_loaded, 16)
            sp.wait_ge(wd2_zeroed, 1)
            for dst, src in ((k.norm_w[:, :], a["norm_w"]), (k.skip_w[:, :], a["skip_w"]), (k.in_w[:, :], a["in_w"]),
                             (k.conv_w[:, :, :], a["conv_w"].unsqueeze(0).broadcast_to([P, MC, ME])),
                             (k.w_low[:, :, 0:MR], tiles("wd1")), (k.wd2[0:MR, :], a["wd2"]),
                             (k.w_low[:, :, MR:MR + MN], tiles("wb")), (k.w_low[:, :, MR + MN:], tiles("wc")),
                             (k.a_log[:, :, :], tiles("A_log")), (k.out_w[:, :, :], tiles("out_w")),
                             (k.conv_b[:, :], a["conv_b"]), (k.wd2_b[:, :], a["wd2_b"]), (k.w_d[:, :], a["W_D"])):
                sp.dma_start(dst, src).then_inc(k.ssm_weights_loaded, 16)

        k.load_later_weights = load_later_weights
        with nc.Block() as block:
            @block.sync
            def _(sp):
                for b in range(B):
                    src = a["x"][b * S:(b + 1) * S].rearrange("(t p) d -> p t d", p=P)
                    sp.dma_start(k.x[:, b * S:(b + 1) * S].rearrange("p (t d) -> p t d", d=D), src).then_inc(k.x_loaded[b], 16)

            @block.gpsimd
            def _(pool):
                pool.memset(k.wd2[:, :], 0.0).then_inc(wd2_zeroed, 1)

            @block.scalar
            def _(act):
                act.dma_start(k.minus_half[:, :], a["minus_half"]).then_inc(k.consts_loaded, 16)
                act.dma_start(k.ident[:, :], a["ident"]).then_inc(k.consts_loaded, 16)
                act.dma_start(w_qkv[:, :, :], a["w_qkv"].rearrange("j d c -> d j c")).then_inc(k.attn_weights_loaded, 16)
                for dst, name in ((k.b_out, "b_out"), (k.gamma, "gamma"), (k.beta, "beta"), (k.before, "before")):
                    act.dma_start(dst[:, :], a[name].broadcast_to([P, a[name].shape[1]])).then_inc(k.consts_loaded, 16)
        k.consts_total, k.attn_weights_total, k.ffn_weights_total = 6 * 16, 16, 7 * 16
        k.ssm_weights_total = 13 * 16
        with ExitStack() as attn:
            sa = lambda n: attn.enter_context(nc.sbuf_tensor(n, [P, B * S], F32))
            k.xn = sa("attn_in")
            k.v = sa("v")
            k.att = sa("att")
            k.spread_f = attn.enter_context(nc.sbuf_tensor("spread_f", [P, E * P], F32))
            project_qkv(nc, k)
            attend(nc, k)
            feed_forward(nc, k, "ffn1", True)
        state_space(nc, k)
        feed_forward(nc, k, "ffn2", False)
        with nc.Block() as block:
            @block.sync
            def _(sp):
                sp.wait_ge(k.ffn_weights_loaded, k.ffn_weights_total)
                sp.wait_ge(k.ssm_weights_loaded, k.ssm_weights_total)
                src = k.x
                for b in range(B):
                    dst = out[b * S:(b + 1) * S].rearrange("(t p) d -> p t d", p=P)
                    sp.dma_start(dst, src[:, b * S:(b + 1) * S].rearrange("p (t d) -> p t d", d=D)).then_inc(stored, 16)
                sp.wait_ge(stored, 16 * B)


def layout(inp):
    import numpy as np
    g = {n.replace("L0_attn_a_", "a_").replace("L0_attn_b_", "b_").replace("L0_ffn_", "f_"): np.asarray(v) for n, v in inp.items()}
    r = {
        "x": g["a_x"].reshape(B * S, D),
        "w_qkv": g["a_w_qkv"].reshape(D, H, 3, HD).transpose(2, 0, 1, 3).reshape(3, D, D),
        "w_out": g["a_w_out"], "b_out": g["a_b_out"].reshape(1, D), "gamma": g["a_gamma"].reshape(1, D),
        "beta": g["a_beta"].reshape(1, D), "norm_w": g["b_norm_w"].reshape(D, 1), "skip_w": g["b_skip_w"].T,
        "in_w": g["b_in_w"].T, "conv_w": g["b_conv_w"].reshape(ME, MC).T, "conv_b": g["b_conv_b"].reshape(MT, P).T,
        "wd1": g["b_wd1"].T, "wd2": g["b_wd2"].T, "wd2_b": g["b_wd2_b"].reshape(MT, P).T,
        "wb": g["b_wb"].T, "wc": g["b_wc"].T, "A_log": g["b_A_log"], "W_D": g["b_W_D"].reshape(MT, P).T,
        "out_w": g["b_out_w"].T, "w_router": g["f_w_router"], "fc1": g["f_fc1_w"], "fc2": g["f_fc2_w"],
        "gate_w": g["f_gate_w"], "up_w": g["f_up_w"], "down_w": g["f_down_w"],
    }
    spread = np.zeros((P, E, P), np.float32)
    for e in range(E):
        for part in range(PARTS):
            spread[part * E + e, e, :] = 1
    r["ident"] = np.eye(P, dtype=np.float32)
    r["spread"] = spread.reshape(P, E * P)
    r["before"] = np.tril(np.ones((E, E), np.float32), -1).reshape(1, E * E)
    r["minus_half"] = np.full((P, 2 * TB), -0.5, np.float32)
    return {n: np.ascontiguousarray(v) for n, v in r.items()}


def kernel(**inputs):
    import numpy as np
    import concourse.bacc as bacc
    from concourse.bass_utils import run_bass_kernel_spmd as run

    nc = bacc.Bacc("TRN2", target_bir_lowering=False, num_devices=1)
    arrays = {f"in_{n}": v for n, v in layout(inputs).items()}
    a = {n[3:]: nc.dram_tensor(n, v.shape, mybir.dt.from_np(v.dtype), kind="ExternalInput").ap() for n, v in arrays.items()}
    out = nc.dram_tensor("out", (B * S, D), F32, kind="ExternalOutput").ap()
    build_program(nc, a, out)
    r = run(nc, [arrays], core_ids=[0])
    return np.asarray(r.results[0]["out"]).reshape(B, S, D)
```

```python
from contextlib import ExitStack

import concourse.bass as bass
from concourse import mybir

F32 = mybir.dt.float32
F32R = mybir.dt.float32r
BF16 = mybir.dt.bfloat16
ALU = mybir.AluOpType
ACT = mybir.ActivationFunctionType
AX_X = mybir.AxisListType.X
ds = bass.ds

P = 128
B, S, D = 4, 1024, 128
H, HD = 16, 8
TB = S // P
HG = 4
GB = H // HG
NG = B * GB
STRIP = 32
GW = HG * HD
PARTS = 3
Q_TERM = (0, 0, 0, 1, 2, 1)
K_TERM = (2, 1, 0, 0, 0, 1)
NT = len(Q_TERM)
HALF = 512
STEPS = 2 * TB
CH = 512
NCH = B * S // CH
CT = CH // P
E, TOPK, I = 8, 2, 128
NE = E + 2
ME, MN, MR, MC = 256, 16, 64, 4
MT = ME // P
UNITS = MN * MT
LN_EPS = 1e-5
KERN_EPS = 1e-6


STORES = 2 * PARTS * 16


class Names:
    pass


class Chain:

    def __init__(self, eng, sem, per, turn):
        self.eng, self.sem, self.per, self.turn, self.n = eng, sem, per, turn, 0

    def did(self, ins):
        ins.then_inc(self.sem, 1)
        self.n += 1

    def wait(self):
        self.eng.wait_ge(self.sem, self.turn * self.per + self.n)

    def end(self):
        assert self.n == self.per, self.n


NORM_STEPS = 5


def gather_stats(dve, step, stats, moments, mean, var_eps):
    even, odd = stats[:, :, 0:3], stats[:, :, 3:6]
    step.did(dve.tensor_tensor(moments[:, :, 0:3], even, odd, ALU.add))
    step.did(dve.tensor_tensor(moments[:, :, 3:4], even[:, :, 1:2], odd[:, :, 1:2], ALU.subtract))
    step.wait()
    step.did(dve.tensor_scalar(mean[:, :], moments[:, :, 1], 0.5, None, ALU.mult))
    step.did(dve.tensor_tensor(moments[:, :, 4:5], moments[:, :, 3:4], moments[:, :, 3:4], ALU.mult))
    step.did(dve.tensor_scalar(moments[:, :, 5:6], moments[:, :, 2:3], 1.0 / D, LN_EPS, ALU.mult, ALU.add))
    step.wait()
    return dve.scalar_tensor_tensor(out=var_eps, in0=moments[:, :, 4], scalar=0.25, in1=moments[:, :, 5],
                                    op0=ALU.mult, op1=ALU.add)


def project_qkv(nc, k):
    with ExitStack() as ctx:
        sb = lambda n, s, d=F32: ctx.enter_context(nc.sbuf_tensor("qkv_" + n, s, d))
        pb = lambda n: ctx.enter_context(nc.psum_tensor("qkv_" + n, [P, S], F32))
        sem = lambda n: ctx.enter_context(nc.semaphore("qkv_" + n))
        stats = sb("stats", [P, B * TB, 6])
        moments = sb("moments", [P, B * TB, 8])
        mean = sb("mean", [P, B * TB])
        var_eps = sb("var_eps", [P, B * TB])
        rstd = sb("rstd", [P, B * TB])
        xn = sb("xn", [P, 2, TB, D])
        xnT = sb("xnT", [P, 2, S])
        q_part, k_part = k.q_part, k.k_part
        q_rest = sb("q_rest", [P, S])
        k_rest = sb("k_rest", [P, S])
        psT, psQ, psK, psV = pb("psT"), pb("psQ"), pb("psK"), pb("psV")
        dve_steps = sem("dve_steps")
        var_ready, rstd_ready = sem("var_ready"), sem("rstd_ready")
        xn_ready, xn_copied, xn_turned = sem("xn_ready"), sem("xn_copied"), sem("xn_turned")
        xnT_ready = sem("xnT_ready")
        q_ready, k_ready, v_ready = sem("q_ready"), sem("k_ready"), sem("v_ready")
        qk_taken, v_copied = sem("qk_taken"), sem("v_copied")
        first_ready, second_ready, third_ready = sem("first_ready"), sem("second_ready"), sem("third_ready")
        block = ctx.enter_context(nc.Block())
        scale = float(HD) ** -0.5

        def over_batches(eng, body):
            with eng.Fori(0, B // 2 - 1) as i:
                body(i, 0, False)
                body(i, 1, False)
            body(B // 2 - 1, 0, False)
            body(B // 2 - 1, 1, True)

        @block.sync
        def _(sp):
            def body(pair, par, last):
                b = pair * 2 + par
                for part, ready in enumerate((first_ready, second_ready, third_ready)):
                    sp.wait_ge(ready, b * 2 + 2)
                    for src, terms, dst in ((q_part, Q_TERM, k.q_terms), (k_part, K_TERM, k.k_terms)):
                        at = [t for t in range(NT) if terms[t] == part]
                        out = dst[ds(b, 1), :, :, at[0]:at[-1] + 1:at[1] - at[0] if len(at) > 1 else 1]
                        copies = src[:, par, part, :].unsqueeze(1).broadcast_to([P, len(at), S])
                        sp.dma_start(out.rearrange("o h d t s -> (o h d) t s"), copies).then_inc(k.parts_stored[par], 16)

            with sp.Fori(0, B // 2 - 1) as i:
                body(i, 0, False)
                body(i, 1, False)
            sp.wait_ge(k.zeroed, 3)
            for par in range(2):
                sp.wait_ge(k.parts_stored[par], (B // 2) * STORES)
            for par in range(2):
                load_heads(sp, k, par, par)
            body(B // 2 - 1, 0, False)
            body(B // 2 - 1, 1, True)

        @block.gpsimd
        def _(pool):
            pool.wait_ge(k.consts_loaded, k.consts_total)

            def body(pair, par, last):
                b = pair * 2 + par
                pool.wait_ge(xn_ready, (b + 1) * TB)
                bias = k.b_out[:, :].unsqueeze(1).broadcast_to([P, TB, D])
                out = k.xn[:, ds(b * S, S)].rearrange("p (t d) -> p t d", d=D)
                pool.tensor_tensor(out, xn[:, par], bias, ALU.add).then_inc(xn_copied, 1)

            for n, tiles in enumerate((slice(0, TB), slice(TB, B * TB))):
                pool.wait_ge(var_ready, n + 1)
                pool.tensor_tensor(rstd[:, tiles], var_eps[:, tiles], k.minus_half[:, tiles], ALU.pow).then_inc(rstd_ready, 1)
            over_batches(pool, body)
            pool.tensor_copy(k.ident_b[:, :], k.ident[:, :])

        @block.vector
        def _(dve):
            def take_stats(tiles):
                for j in range(tiles.start, tiles.stop):
                    step.did(dve.bn_stats(stats[:, j], k.x[:, j * D:(j + 1) * D]))
                step.wait()
                gather_stats(dve, step, stats[:, tiles], moments[:, tiles], mean[:, tiles], var_eps[:, tiles]).then_inc(var_ready, 1)

            def norm(b, par):
                dve.wait_ge(xn_copied, b + 1)
                dve.wait_ge(xn_turned, b + 1)
                for j in range(TB):
                    t = b * TB + j
                    dve.tensor_scalar(xn[:, par, j], k.x[:, ds(t * D, D)], mean[:, ds(t, 1)], rstd[:, ds(t, 1)],
                                      ALU.subtract, ALU.mult).then_inc(xn_ready, 1)

            def body(pair, par, last):
                b = pair * 2 + par
                if not last:
                    norm(b + 1, 1 - par)
                dve.wait_ge(first_ready, b * 2 + 1)
                dve.wait_ge(second_ready, b * 2)
                dve.wait_ge(third_ready, b * 2)
                dve.scalar_tensor_tensor(out=q_rest[:, :], in0=psQ[:, :], scalar=scale, in1=q_part[:, par, 0],
                                         op0=ALU.mult, op1=ALU.subtract).then_inc(qk_taken, 1)
                dve.wait_ge(first_ready, b * 2 + 2)
                dve.tensor_tensor(k_rest[:, :], psK[:, :], k_part[:, par, 0], ALU.subtract).then_inc(qk_taken, 1)
                dve.wait_ge(second_ready, b * 2 + 1)
                dve.tensor_tensor(q_part[:, par, 2], q_rest[:, :], q_part[:, par, 1], ALU.subtract).then_inc(third_ready, 1)
                dve.wait_ge(second_ready, b * 2 + 2)
                dve.tensor_tensor(k_part[:, par, 2], k_rest[:, :], k_part[:, par, 1], ALU.subtract).then_inc(third_ready, 1)

            step = Chain(dve, dve_steps, B * TB + 2 * NORM_STEPS, 0)
            dve.wait_ge(k.x_loaded[0], 16)
            take_stats(slice(0, TB))
            dve.wait_ge(rstd_ready, 1)
            norm(0, 0)
            for b in range(1, B):
                dve.wait_ge(k.x_loaded[b], 16)
            take_stats(slice(TB, B * TB))
            step.end()
            dve.wait_ge(rstd_ready, 2)
            over_batches(dve, body)

        @block.scalar
        def _(act):
            def xnT_out(b, par):
                act.wait_ge(xn_turned, b + 3)
                act.wait_ge(v_ready, b + 1)
                act.copy(xnT[:, par], psT[:, :]).then_inc(xnT_ready, 1)

            def body(pair, par, last):
                b = pair * 2 + par
                act.wait_ge(q_ready, b + 1)
                act.wait_ge(k.parts_stored[par], (pair + 1) * STORES)
                act.mul(q_part[:, par, 0], psQ[:, :], scale).then_inc(first_ready, 1)
                act.wait_ge(k_ready, b + 1)
                act.copy(k_part[:, par, 0], psK[:, :]).then_inc(first_ready, 1)
                if not last:
                    xnT_out(b + 1, 1 - par)
                act.wait_ge(v_ready, b + 3)
                v_out = k.v[:, ds(b * S, S)].rearrange("p (g t c) -> p t g c", g=GB, c=GW)
                act.copy(v_out, psV[:, :].rearrange("p (t g c) -> p t g c", t=TB, g=GB)).then_inc(v_copied, 1)
                act.wait_ge(qk_taken, b * 2 + 2)
                act.copy(q_part[:, par, 1], q_rest[:, :]).then_inc(second_ready, 1)
                act.wait_ge(qk_taken, b * 2 + 3)
                act.copy(k_part[:, par, 1], k_rest[:, :]).then_inc(second_ready, 1)

            xnT_out(0, 0)
            over_batches(act, body)

        @block.tensor
        def _(pe):
            for s, n in ((xn_turned, 2), (xn_copied, 2), (v_ready, 2), (xnT_ready, 1), (qk_taken, 1), (v_copied, 1),
                         (k.parts_stored[0], STORES), (k.parts_stored[1], STORES)):
                pe.sem_inc(s, n)
            pe.wait_ge(k.attn_weights_loaded, k.attn_weights_total)
            pe.wait_ge(k.consts_loaded, k.consts_total)

            def turn(b, par):
                pe.wait_ge(xn_ready, (b + 1) * TB)
                pe.wait_ge(xnT_ready, b + 1)
                for j in range(TB):
                    mm = pe.transpose(psT[:, j * P:(j + 1) * P], xn[:, par, j], k.ident[:, :])
                mm.then_inc(xn_turned, 1)

            def body(pair, par, last):
                b = pair * 2 + par
                pe.wait_ge(xnT_ready, b + 2)
                pe.wait_ge(qk_taken, b * 2 + 1)
                for ps, w, done in ((psQ, k.w_q, q_ready), (psK, k.w_k, k_ready)):
                    for h in range(2):
                        cols = slice(h * HALF, (h + 1) * HALF)
                        mm = pe.matmul(ps[:, cols], w, xnT[:, par, cols], start=True, stop=True)
                    mm.then_inc(done, 1)
                if not last:
                    turn(b + 1, 1 - par)
                pe.wait_ge(v_copied, b + 1)
                for j in range(TB):
                    cols = slice(j * P, (j + 1) * P)
                    mm = pe.matmul(psV[:, cols], xnT[:, par, cols], k.w_v, start=True, stop=True)
                mm.then_inc(v_ready, 1)

            turn(0, 0)
            over_batches(pe, body)


LOADS = 4 * 16


def load_heads(sp, k, n, par):
    rows = NT * HD
    q_src = k.q_terms.rearrange("b (g p a) d t s -> (b g) p a (d t) s", g=GB, a=2)
    k_src = k.k_terms.rearrange("b (g p a) d t s -> (b g) p a (d t) s", g=GB, a=2)
    for a in range(2):
        r = slice(64 * a, 64 * a + rows)
        sp.dma_start(k.q_in[r, par], q_src[ds(n, 1), :, a].rearrange("o p r s -> r (o p) s")).then_inc(k.qk_loaded[par], 16)
        out = k.k_in[r, par].rearrange("r (p a) s -> r p a s", a=2)[:, :, a]
        sp.dma_start(out, k_src[ds(n, 1), :, a].rearrange("o p r s -> r (o p) s")).then_inc(k.qk_loaded[par], 16)


def attend(nc, k):
    with ExitStack() as ctx:
        sb = lambda n, s, d=F32: ctx.enter_context(nc.sbuf_tensor("att_" + n, s, d))
        pb = lambda n, w: ctx.enter_context(nc.psum_tensor("att_" + n, [P, w], F32))
        sem = lambda n: ctx.enter_context(nc.semaphore("att_" + n))
        q_in, k_in = k.q_in, k.k_in
        v_in = sb("v_in", [P, 2, TB, HG, STRIP])
        w = sb("w", [P, 2, HG, HALF])
        oT = sb("oT", [P, 2, HALF])
        den = sb("den", [P, CT, HG])
        inv_den = sb("inv_den", [P, CT, HG])
        psA, psB = pb("psA", 2 * HALF), pb("psB", 2 * HALF)
        psO = [pb("psO0", HALF), pb("psO1", HALF)]
        psT = pb("psT", HALF)
        ones_set, v_ready = sem("ones_set"), sem("v_ready")
        scored_a, scored_b = sem("scored_a"), sem("scored_b")
        relu_a, relu_b = sem("relu_a"), sem("relu_b")
        summed = sem("summed")
        o_copied, o_turned, o_done = sem("o_copied"), sem("o_turned"), sem("o_done")
        dve_steps = sem("dve_steps")
        block = ctx.enter_context(nc.Block())
        BODY = 2 * STEPS
        AHEAD = 2 * STEPS
        LAST = NG // 2 - 1

        @block.sync
        def _(sp):
            k.load_later_weights(sp)
            for par in range(2):
                sp.wait_ge(k.parts_stored[par], (B // 2 + 1) * STORES)
            with sp.Fori(0, NG // 2 - 1) as i:
                for par in range(2):
                    sp.wait_ge(scored_b, (i * 2 + par + 3) * 2 * STEPS)
                    load_heads(sp, k, (i + 1) * 2 + par, par)

        @block.gpsimd
        def _(pool):
            pool.memset(v_in[:, :, :, :, :], 0.0).then_inc(ones_set, 1)
            pool.wait_ge(ones_set, 1)
            pool.memset(v_in[:, :, :, :, HD:HD + 1], 1.0).then_inc(ones_set, 1)
            with pool.Fori(0, NG // 2) as i:
                for par in range(2):
                    n = i * 2 + par
                    pool.wait_ge(summed, (n + 1) * STEPS)
                    src = k.v[:, ds(n * TB * GW, TB * GW)].rearrange("p (t h d) -> p t h d", t=TB, d=HD)
                    pool.tensor_copy(v_in[:, par, :, :, 0:HD], src).then_inc(v_ready, 1)
            pool.wait_ge(k.spread_loaded, 16)
            pool.tensor_copy(k.spread[:, :, :], k.spread_f[:, :].rearrange("p (e q) -> p e q", e=E))

        @block.scalar
        def _(act):
            def relu(m, buf):
                act.wait_ge(scored_a, m + 1)
                act.wait_ge(summed, AHEAD + m - 1)
                act.activation(w[:, buf, 0:2], psA[:, :].rearrange("p (h q) -> p h q", h=2), ACT.Relu).then_inc(relu_a, 1)

            def body(i, last):
                for q in range(BODY):
                    m = i * BODY + q
                    if not (last and q == BODY - 1):
                        relu(m + 1, (q + 1) % 2)
                    if q % TB == TB - 1:
                        o, n = q // TB % 2, i * 4 + q // TB
                        act.wait_ge(summed, AHEAD + m + 1)
                        act.wait_ge(o_turned, n + 1)
                        act.copy(oT[:, o], psO[o][:, :]).then_inc(o_copied, 1)

            relu(0, 0)
            with act.Fori(0, LAST) as i:
                body(i, False)
            body(LAST, True)

        @block.vector
        def _(dve):
            dve.wait_ge(ones_set, 2)

            def relu(m, buf):
                dve.wait_ge(summed, AHEAD + m - 1)
                for a in range(2):
                    dve.wait_ge(scored_b, (AHEAD + m) * 2 + a + 1)
                    dve.tensor_scalar(w[:, buf, 2 + a], psB[:, a * HALF:(a + 1) * HALF], 0.0, None,
                                      ALU.max).then_inc(relu_b, 1)

            def normalise(i, j):
                n = i * 4 + j
                t = psT[:, :].rearrange("p (t h c) -> p t h c", t=CT, h=HG)
                dve.wait_ge(o_turned, n + 3)
                dve.tensor_scalar(den[:, :, :], t[:, :, :, HD], KERN_EPS, None, ALU.add).then_inc(dve_steps, 1)
                dve.wait_ge(dve_steps, n * 2 + 1)
                dve.reciprocal(inv_den[:, :, :], den[:, :, :]).then_inc(dve_steps, 1)
                dve.wait_ge(dve_steps, n * 2 + 2)
                out = k.att[:, ds(n * CT * GW, CT * GW)].rearrange("p (m d) -> p m d", d=HD)
                dve.tensor_tensor(out, t[:, :, :, 0:HD].rearrange("p t h d -> p (t h) d"),
                                  inv_den[:, :, :].rearrange("p t h -> p (t h)").unsqueeze(2).broadcast_to([P, CT * HG, HD]),
                                  ALU.mult).then_inc(o_done, 1)

            def body(i, last):
                for q in range(BODY):
                    if not (last and q == BODY - 1):
                        relu(i * BODY + q + 1, (q + 1) % 2)
                    if q % TB == 4 and q > TB:
                        normalise(i, q // TB - 1)
                normalise(i, 3)

            relu(0, 0)
            with dve.Fori(0, LAST) as i:
                body(i, False)
            body(LAST, True)

        @block.tensor
        def _(pe):
            pe.sem_inc(scored_b, 2 * AHEAD)
            pe.sem_inc(summed, AHEAD)
            pe.sem_inc(o_turned, 2)
            pe.sem_inc(o_copied, 2)
            pe.sem_inc(o_done, 1)
            pe.sem_inc(relu_a, 1)
            pe.sem_inc(relu_b, 2)

            def scores(n_of_par, m, q):
                par, qh, kt = q // STEPS % 2, q // TB % 2, q % TB
                if q % STEPS == 0:
                    pe.wait_ge(k.qk_loaded[par], (n_of_par + 1) * LOADS)
                product = lambda ps, pair, a: pe.matmul(ps[:, a * HALF:(a + 1) * HALF], k_in[:, par, 2 * pair + a, kt * P:(kt + 1) * P],
                                                        q_in[:, par, pair, qh * HALF:(qh + 1) * HALF], start=True, stop=True)
                pe.wait_ge(relu_a, m + 1)
                product(psA, 0, 0)
                product(psA, 0, 1).then_inc(scored_a, 1)
                for a in range(2):
                    pe.wait_ge(relu_b, m * 2 + a + 1)
                    product(psB, 1, a).then_inc(scored_b, 1)

            def values(i, q):
                par, o, kt = q // STEPS, q // TB % 2, q % TB
                m = i * BODY + q
                if q % STEPS == 0:
                    pe.wait_ge(v_ready, i * 2 + par + 1)
                if kt == 0:
                    pe.wait_ge(o_copied, i * 4 + q // TB + 1)
                pe.wait_ge(relu_a, m + 2)
                pe.wait_ge(relu_b, m * 2 + 4)
                for h in range(HG):
                    mm = pe.matmul(psO[o][h * STRIP:(h + 1) * STRIP, :], v_in[:, par, kt, h], w[:, q % 2, h],
                                   start=(kt == 0), stop=(kt == TB - 1))
                mm.then_inc(summed, 1)

            def turn(i, j):
                n = i * 4 + j
                pe.wait_ge(o_copied, n + 3)
                pe.wait_ge(o_done, n + 1)
                for t in range(CT):
                    mm = pe.transpose(psT[:, t * P:(t + 1) * P], oT[:, j % 2, t * P:(t + 1) * P], k.ident[:, :])
                mm.then_inc(o_turned, 1)

            def body(i, last):
                for q in range(BODY):
                    if not (last and q == BODY - 1):
                        scores(i + (q + 1) // BODY, i * BODY + q + 1, (q + 1) % BODY)
                    values(i, q)
                    if q % TB == 2 and q > TB:
                        turn(i, q // TB - 1)
                turn(i, 3)

            scores(0, 0, 0)
            with pe.Fori(0, LAST) as i:
                body(i, False)
            body(LAST, True)


FFN_EXPERTS = dict(
    in_stats=0, in_moments=0, in_norm=1, xn_low=3, compare=4, rank=4, take=5, shares=6, out_sum=6, out_stats=7, out_moments=7, out_norm=8,
    in_root=1, gather=3, out_root=7, gamma=9, beta=9, add=9,
    xn_out=3, heads_out=5, tanh=6, parts_out=8,
    turn_xn=2, route=3, turn_heads=4, project_heads=5, turn_parts=7,
)


def feed_forward(nc, k, name, after_attention, out=None, norms=None):
    with ExitStack() as ctx:
        sb = lambda n, s, d=F32: ctx.enter_context(nc.sbuf_tensor(name + "_" + n, s, d))
        pb = lambda n: ctx.enter_context(nc.psum_tensor(name + "_" + n, [P, CH], F32))
        sem = lambda n: ctx.enter_context(nc.semaphore(name + "_" + n))
        heads = sb("heads", [P, CT, D])
        headsT = sb("headsT", [P, CH])
        y = sb("y", [P, CT, D])
        yn = sb("yn", [P, CT, D])
        xn = sb("xn", [P, CT, D])
        split = lambda n, s: (sb(n + "_high", s, F32R), sb(n + "_low", s, F32R))
        xnT = split("xnT", [P, 2, CH])
        w1, w2, w_router = split("w1", [P, NE, 2 * I]), split("w2", [P, NE, D]), split("w_router", [P, E])
        stats = sb("stats", [P, CT, 6])
        moments = sb("moments", [P, CT, 8])
        mean = sb("mean", [P, 2, CT])
        var_eps = sb("var_eps", [P, 2, CT])
        rstd = sb("rstd", [P, 2, CT])
        logit = sb("logit", [P, CT, E])
        above = sb("above", [P, CT, E, E])
        equal = sb("equal", [P, CT, E, E])
        rank = sb("rank", [P, CT, E])
        taken = sb("taken", [P, CT, E])
        taken_logit = sb("taken_logit", [P, CT, E])
        logit_sum = sb("logit_sum", [P, CT])
        margin = sb("margin", [P, CT, E])
        half_tanh = sb("half_tanh", [P, CT, E])
        share = sb("share", [P, CT, E])
        rest = sb("rest", [P, CT, E])
        parts = sb("parts", [P, CT, P], BF16)
        partsT = sb("partsT", [P, 2, CH], BF16)
        silu = sb("silu", [P, 2, CH])
        scaled = sb("scaled", [P, 2, CH])
        hidden = sb("hidden", [P, 2, CH])
        hidden_high, hidden_low = split("hidden", [P, 2, CH])
        oT = sb("oT", [P, CH])
        psP = [pb("psP0"), pb("psP1")]
        psG = [pb("psG0"), pb("psG1")]
        psC, psO, psX, psY = pb("psC"), pb("psO"), pb("psX"), pb("psY")
        in_steps = sem("in_steps")
        parts_zeroed = sem("parts_zeroed")
        if after_attention:
            out_steps, pool_steps = sem("out_steps"), sem("pool_steps")
            heads_ready, heads_turned, headsT_ready = sem("heads_ready"), sem("heads_turned"), sem("headsT_ready")
            projected, y_taken, yn_ready, x_added = sem("projected"), sem("y_taken"), sem("yn_ready"), sem("x_added")
            y_var_ready, y_rstd_ready = sem("y_var_ready"), sem("y_rstd_ready")
        var_ready, rstd_ready = sem("var_ready"), sem("rstd_ready")
        xn_ready, xn_turned, xnT_ready = sem("xn_ready"), sem("xn_turned"), sem("xnT_ready")
        routed, logit_taken, margin_ready, tanh_ready = sem("routed"), sem("logit_taken"), sem("margin_ready"), sem("tanh_ready")
        parts_ready, parts_turned, partsT_ready = sem("parts_ready"), sem("parts_turned"), sem("partsT_ready")
        p_ready, g_ready, c_ready = sem("p_ready"), sem("g_ready"), sem("c_ready")
        w_high_ready, w_low_ready, xn_low_ready = sem("w_high_ready"), sem("w_low_ready"), sem("xn_low_ready")
        high_ready, low_ready = sem("high_ready"), sem("low_ready")
        silu_ready, scaled_ready, hidden_ready = sem("silu_ready"), sem("scaled_ready"), sem("hidden_ready")
        down_steps, o_copied, o_turned, o_added = sem("down_steps"), sem("o_copied"), sem("o_turned"), sem("o_added")
        block = ctx.enter_context(nc.Block())
        LAST = NCH // 2 - 1
        at = FFN_EXPERTS

        def chunk(t, c):
            return t[:, ds(c * CT * D, CT * D)].rearrange("p (t d) -> p t d", d=D)

        WEIGHTS = ((k.w_router, w_router), (k.w1, w1), (k.w2, w2))

        if out is not None:
            @block.sync
            def _(sp):
                with sp.Fori(0, NCH) as c:
                    sp.wait_ge(o_added, c + 3)
                    dst = out[ds(c * CH, CH)].rearrange("(t p) d -> p t d", p=P)
                    sp.dma_start(dst, chunk(k.x, c)).then_inc(k.stored, 16)
                sp.wait_ge(k.stored, NCH * 16)

        @block.gpsimd
        def _(pool):
            pool.memset(parts[:, :, :], 0.0).then_inc(parts_zeroed, 1)
            pool.wait_ge(k.consts_loaded, k.consts_total)

            def gather(i, half):
                c = i * 2 + half
                pool.wait_ge(heads_turned, c + 1)
                src = k.att[:, ds(i * S, S)].rearrange("p (g t c) -> p t g c", g=GB, c=GW)[:, half * CT:(half + 1) * CT]
                pool.tensor_copy(heads[:, :, :].rearrange("p t (g c) -> p t g c", c=GW), src).then_inc(heads_ready, 1)

            def root(c, n, var, done):
                pool.wait_ge(var, c + 1)
                pool.tensor_tensor(rstd[:, n], var_eps[:, n], k.minus_half[:, 0:CT], ALU.pow).then_inc(done, 1)

            def add_normed(c, n):
                if n == 0:
                    pool.wait_ge(yn_ready, (c + 1) * CT)
                    gamma = k.gamma[:, :].unsqueeze(1).broadcast_to([P, CT, D])
                    pool.tensor_tensor(yn[:, :, :], yn[:, :, :], gamma, ALU.mult).then_inc(pool_steps, 1)
                if n == 1:
                    beta = k.beta[:, :].unsqueeze(1).broadcast_to([P, CT, D])
                    pool.wait_ge(pool_steps, c * 2 + 1)
                    pool.tensor_tensor(yn[:, :, :], yn[:, :, :], beta, ALU.add).then_inc(pool_steps, 1)
                if n == 2:
                    pool.wait_ge(pool_steps, c * 2 + 2)
                    pool.tensor_tensor(chunk(k.x, c), chunk(k.x, c), yn[:, :, :], ALU.add).then_inc(x_added, 1)

            def out_ready(i, half):
                c = i * 2 + half
                gather(i, half)
                root(c, 1, y_var_ready, y_rstd_ready)
                for n in range(3):
                    add_normed(c, n)

            def in_ready(c):
                root(c, 0, var_ready, rstd_ready)

            def low_out(c, e):
                pool.wait_ge(high_ready, c * NE + e + 1)
                pool.tensor_tensor(hidden_low[:, e % 2], hidden[:, e % 2], hidden_high[:, e % 2].bitcast(F32),
                                   ALU.subtract).then_inc(low_ready, 1)

            def body(i, par, last):
                for e in range(NE):
                    low_out(i * 2 + par, e)
                    if norms and last and par:
                        if e == 1:
                            norms.norm_root(pool, 0)
                        if e == 3:
                            norms.add_resid(pool, 0)
                        if e == 5:
                            norms.rms_root(pool, 0)
                    if e == at["in_root"] and not (last and par):
                        in_ready(i * 2 + par + 1)
                    if after_attention and not last:
                        if e == at["gather"]:
                            gather(i + 1, par)
                        if e == at["out_root"]:
                            root(i * 2 + par + 2, 1, y_var_ready, y_rstd_ready)
                        for n, step in enumerate(("gamma", "beta", "add")):
                            if e == at[step]:
                                add_normed(i * 2 + par + 2, n)

            if after_attention:
                out_ready(0, 0)
            in_ready(0)
            if after_attention:
                out_ready(0, 1)
            with pool.Fori(0, LAST) as i:
                body(i, 0, False)
                body(i, 1, False)
            body(LAST, 0, True)
            body(LAST, 1, True)

        @block.scalar
        def _(act):
            def heads_out(c):
                act.wait_ge(heads_turned, c + 2)
                act.copy(headsT[:, :], psX[:, :]).then_inc(headsT_ready, 1)

            def xn_out(c, par):
                act.wait_ge(xn_turned, c + 2)
                act.copy(xnT[0][:, par], psX[:, :]).then_inc(xnT_ready, 1)

            def tanh(c):
                act.wait_ge(margin_ready, c + 1)
                act.activation(half_tanh[:, :, :], margin[:, :, :], ACT.Tanh).then_inc(tanh_ready, 1)

            def parts_out(c, par):
                act.wait_ge(parts_turned, c + 2)
                act.copy(partsT[:, par], psX[:, 0:CH // 2].bitcast(BF16)).then_inc(partsT_ready, 1)

            def gate(c, e):
                n = c * NE + e
                act.wait_ge(p_ready, n + 1)
                act.wait_ge(hidden_ready, n + 1)
                act.activation(silu[:, e % 2], psP[e % 2][:, :], ACT.Silu).then_inc(silu_ready, 1)

            def high_out(c, e):
                n = c * NE + e
                act.wait_ge(hidden_ready, n + 3)
                act.wait_ge(down_steps, n + 1)
                act.copy(hidden_high[:, e % 2], hidden[:, e % 2]).then_inc(high_ready, 1)

            def body(i, par, last):
                c = i * 2 + par
                for e in range(NE):
                    if e + 1 < NE:
                        gate(c, e + 1)
                    elif not (last and par):
                        gate(c + 1, 0)
                    high_out(c, e)
                    if norms and last and par:
                        if e == 3:
                            norms.squares(act, 0)
                        if e == 7:
                            norms.rms_norm(act, 0)
                    if not (last and par):
                        if e == at["xn_out"]:
                            xn_out(c + 1, 1 - par)
                        if e == at["tanh"]:
                            tanh(c + 1)
                        if e == at["parts_out"]:
                            parts_out(c + 1, 1 - par)
                    if after_attention and not last and e == at["heads_out"]:
                        heads_out(c + 2)
                act.wait_ge(down_steps, (c + 1) * NE + 2)
                act.wait_ge(o_turned, c + 1)
                act.copy(oT[:, :], psO[:, :]).then_inc(o_copied, 1)

            act.wait_ge(k.ffn_weights_loaded, k.ffn_weights_total)
            for w, (high, _) in WEIGHTS:
                act.copy(high[:], w[:]).then_inc(w_high_ready, 1)
            if after_attention:
                heads_out(0)
            xn_out(0, 0)
            tanh(0)
            parts_out(0, 0)
            if after_attention:
                heads_out(1)
            gate(0, 0)
            with act.Fori(0, LAST) as i:
                body(i, 0, False)
                body(i, 1, False)
            body(LAST, 0, True)
            body(LAST, 1, True)

        @block.vector
        def _(dve):
            dve.wait_ge(parts_zeroed, 1)
            dve.wait_ge(k.consts_loaded, k.consts_total)
            for b in range(B):
                dve.wait_ge(k.x_loaded[b], 16)
            OUT_PER, IN_PER = CT + NORM_STEPS, CT + NORM_STEPS + 13

            def take_stats(step, src):
                for t in range(CT):
                    step.did(dve.bn_stats(stats[:, t], src(t)))

            def take_moments(n, step, var):
                step.wait()
                gather_stats(dve, step, stats, moments, mean[:, n], var_eps[:, n]).then_inc(var, 1)

            def norm(c, n, src, out, root, done):
                dve.wait_ge(root, c + 1)
                for t in range(CT):
                    dve.tensor_scalar(out[:, t], src(t), mean[:, n, t:t + 1], rstd[:, n, t:t + 1],
                                      ALU.subtract, ALU.mult).then_inc(done, 1)

            def out_sum(c):
                dve.wait_ge(projected, c + 1)
                dve.tensor_tensor(y[:, :, :], psY[:, :].rearrange("p (t d) -> p t d", d=D), chunk(k.xn, c),
                                  ALU.add).then_inc(y_taken, 1)

            def out_stats(c, step):
                dve.wait_ge(y_taken, c + 2)
                take_stats(step, lambda t: y[:, t])

            def out_moments(c, step):
                take_moments(1, step, y_var_ready)
                step.end()

            def out_norm(c):
                dve.wait_ge(x_added, c + 1)
                norm(c, 1, lambda t: y[:, t], yn, y_rstd_ready, yn_ready)

            x_tile = lambda c: lambda t: k.x[:, ds((c * CT + t) * D, D)]

            def in_stats(c, step):
                if after_attention:
                    dve.wait_ge(x_added, c + 2)
                take_stats(step, x_tile(c))

            def in_norm(c):
                dve.wait_ge(xn_turned, c + 1)
                norm(c, 0, x_tile(c), xn, rstd_ready, xn_ready)

            def xn_low(c, par):
                dve.wait_ge(xnT_ready, c + 2)
                dve.tensor_tensor(xnT[1][:, par], psX[:, :], xnT[0][:, par].bitcast(F32), ALU.subtract).then_inc(xn_low_ready, 1)

            def compare_experts(c, step):
                dve.wait_ge(routed, c + 1)
                dve.tensor_copy(logit[:, :, :], psY[:, 0:CT * E].rearrange("p (t e) -> p t e", e=E)).then_inc(logit_taken, 1)
                dve.wait_ge(logit_taken, c + 2)
                of = logit[:, :, :].unsqueeze(3).broadcast_to([P, CT, E, E])
                other = logit[:, :, :].unsqueeze(2).broadcast_to([P, CT, E, E])
                step.did(dve.tensor_tensor(above[:, :, :, :], other, of, ALU.is_gt))
                step.did(dve.tensor_tensor(equal[:, :, :, :], other, of, ALU.is_equal))

            def rank_experts(c, step):
                before = k.before[:, :].rearrange("p (a b) -> p a b", a=E).unsqueeze(1).broadcast_to([P, CT, E, E])
                step.wait()
                step.did(dve.tensor_tensor(equal[:, :, :, :], equal[:, :, :, :], before, ALU.mult))
                step.wait()
                step.did(dve.tensor_tensor(above[:, :, :, :], above[:, :, :, :], equal[:, :, :, :], ALU.add))
                step.wait()
                step.did(dve.tensor_reduce(rank[:, :, :], above[:, :, :, :], AX_X, ALU.add))
                step.wait()

            def take_experts(c, step):
                step.did(dve.tensor_scalar(taken[:, :, :], rank[:, :, :], TOPK - 0.5, None, ALU.is_lt))
                step.wait()
                step.did(dve.tensor_tensor(taken_logit[:, :, :], logit[:, :, :], taken[:, :, :], ALU.mult))
                step.wait()
                step.did(dve.tensor_reduce(logit_sum[:, :], taken_logit[:, :, :], AX_X, ALU.add))
                step.wait()
                dve.scalar_tensor_tensor(out=margin[:, :, :], in0=logit_sum[:, :].unsqueeze(2).broadcast_to([P, CT, E]),
                                         scalar=-0.5, in1=logit[:, :, :], op0=ALU.mult, op1=ALU.add).then_inc(margin_ready, 1)

            def split_shares(c, step):
                dve.wait_ge(tanh_ready, c + 1)
                step.did(dve.tensor_scalar(share[:, :, :], half_tanh[:, :, :], 0.5, 0.5, ALU.mult, ALU.add))
                step.wait()
                step.did(dve.tensor_tensor(share[:, :, :], share[:, :, :], taken[:, :, :], ALU.mult))
                step.wait()
                dve.wait_ge(parts_turned, c + 1)
                step.did(dve.tensor_copy(parts[:, :, 0:E], share[:, :, :]))
                step.wait()
                step.did(dve.tensor_tensor(rest[:, :, :], share[:, :, :], parts[:, :, 0:E], ALU.subtract))
                step.wait()
                step.did(dve.tensor_copy(parts[:, :, E:2 * E], rest[:, :, :]))
                step.wait()
                dve.tensor_tensor(parts[:, :, 2 * E:3 * E], rest[:, :, :], parts[:, :, E:2 * E],
                                  ALU.subtract).then_inc(parts_ready, 1)

            def hide(c, e):
                n = c * NE + e
                dve.wait_ge(silu_ready, n + 1)
                src = silu[:, e % 2]
                if e < E:
                    dve.wait_ge(c_ready, c * E + e + 1)
                    dve.tensor_tensor(scaled[:, e % 2], silu[:, e % 2], psC[:, :], ALU.mult).then_inc(scaled_ready, 1)
                    dve.wait_ge(scaled_ready, c * E + e + 2)
                    src = scaled[:, e % 2]
                dve.wait_ge(g_ready, n + 1)
                dve.wait_ge(low_ready, n + 1)
                dve.tensor_tensor(hidden[:, e % 2], src, psG[e % 2][:, :], ALU.mult).then_inc(hidden_ready, 1)

            def finish(c):
                dve.wait_ge(o_turned, c + 2)
                dve.tensor_tensor(chunk(k.x, c), chunk(k.x, c), psY[:, :].rearrange("p (t d) -> p t d", d=D),
                                  ALU.add).then_inc(o_added, 1)

            def body(i, par, last):
                c = i * 2 + par
                step = Chain(dve, in_steps, IN_PER, c + 1)
                if after_attention:
                    out_step = Chain(dve, out_steps, OUT_PER, c + 2)
                for e in range(NE):
                    if norms and last and par:
                        if e == 0:
                            norms.take_stats(dve, 0)
                        if e == 2:
                            norms.norm(dve, 0)
                        if e == 4:
                            norms.mean_square(dve, 0)
                    if not (last and par):
                        if e == at["in_stats"]:
                            in_stats(c + 1, step)
                        if e == at["in_moments"]:
                            take_moments(0, step, var_ready)
                        if e == at["in_norm"]:
                            in_norm(c + 1)
                        if e == at["xn_low"]:
                            xn_low(c + 1, 1 - par)
                        if e == at["compare"]:
                            compare_experts(c + 1, step)
                        if e == at["rank"]:
                            rank_experts(c + 1, step)
                        if e == at["take"]:
                            take_experts(c + 1, step)
                        if e == at["shares"]:
                            split_shares(c + 1, step)
                            step.end()
                    if after_attention and not last:
                        if e == at["out_sum"]:
                            out_sum(c + 2)
                        if e == at["out_stats"]:
                            out_stats(c + 2, out_step)
                        if e == at["out_moments"]:
                            out_moments(c + 2, out_step)
                        if e == at["out_norm"]:
                            out_norm(c + 2)
                    if e + 2 < NE:
                        hide(c, e + 2)
                    elif not (last and par):
                        hide(c + 1, e + 2 - NE)
                finish(c)

            def make_out(c):
                step = Chain(dve, out_steps, OUT_PER, c)
                out_sum(c)
                out_stats(c, step)
                out_moments(c, step)
                out_norm(c)

            def weight_low(n):
                w, (high, low) = WEIGHTS[n]
                dve.wait_ge(w_high_ready, n + 1)
                dve.tensor_tensor(low[:], w[:], high[:].bitcast(F32), ALU.subtract).then_inc(w_low_ready, 1)

            for n in range(len(WEIGHTS) if after_attention else 1):
                weight_low(n)
            if after_attention:
                make_out(0)
            step = Chain(dve, in_steps, IN_PER, 0)
            in_stats(0, step)
            take_moments(0, step, var_ready)
            in_norm(0)
            xn_low(0, 0)
            if not after_attention:
                weight_low(1)
            compare_experts(0, step)
            rank_experts(0, step)
            take_experts(0, step)
            split_shares(0, step)
            step.end()
            if not after_attention:
                weight_low(2)
            if after_attention:
                make_out(1)
            hide(0, 0)
            hide(0, 1)
            with dve.Fori(0, LAST) as i:
                body(i, 0, False)
                body(i, 1, False)
            body(LAST, 0, True)
            body(LAST, 1, True)

        @block.tensor
        def _(pe):
            for s, n in ((xn_turned, 1), (parts_turned, 1), (logit_taken, 1), (hidden_ready, 2), (low_ready, 2), (down_steps, 2),
                         (scaled_ready, 1), (o_turned, 1), (o_copied, 1), (o_added, 2), (xnT_ready, 1), (partsT_ready, 1)):
                pe.sem_inc(s, n)
            if after_attention:
                for s in (heads_turned, y_taken, x_added, headsT_ready):
                    pe.sem_inc(s, 1)
            pe.wait_ge(k.ffn_weights_loaded, k.ffn_weights_total)
            pe.wait_ge(k.consts_loaded, k.consts_total)

            def product(out, w, x):
                for n, (a, b) in enumerate(((0, 0), (1, 0), (0, 1))):
                    mm = pe.matmul(out, w[a], x[b], start=(n == 0), stop=(n == 2))
                return mm

            def turn_heads(c):
                pe.wait_ge(heads_ready, c + 1)
                for t in range(CT):
                    mm = pe.transpose(psX[:, t * P:(t + 1) * P], heads[:, t], k.ident[:, :])
                mm.then_inc(heads_turned, 1)

            def project_heads(c):
                pe.wait_ge(headsT_ready, c + 2)
                for t in range(CT):
                    cols = slice(t * P, (t + 1) * P)
                    mm = pe.matmul(psY[:, cols], headsT[:, cols], k.w_out[:, :], start=True, stop=True)
                mm.then_inc(projected, 1)

            def turn_xn(c):
                pe.wait_ge(xn_ready, (c + 1) * CT)
                for t in range(CT):
                    mm = pe.transpose(psX[:, t * P:(t + 1) * P], xn[:, t], k.ident[:, :])
                mm.then_inc(xn_turned, 1)

            def route(c, par):
                pe.wait_ge(xn_low_ready, c + 1)
                pe.wait_ge(w_low_ready, 1)
                pe.wait_ge(o_added, c + 1)
                for t in range(CT):
                    mm = product(psY[:, t * E:(t + 1) * E], [x[:, par, t * P:(t + 1) * P] for x in xnT],
                                 [w[:, :] for w in w_router])
                mm.then_inc(routed, 1)

            def turn_parts(c):
                pe.wait_ge(parts_ready, c + 1)
                pe.wait_ge(xn_low_ready, c + 1)
                for t in range(CT):
                    mm = pe.transpose(psX[:, t * P // 2:(t + 1) * P // 2].bitcast(BF16), parts[:, t], k.ident_b[:, :])
                mm.then_inc(parts_turned, 1)

            def up(c, par, e):
                n = c * NE + e
                pe.wait_ge(hidden_ready, n + 1)
                x = [half[:, par] for half in xnT]
                product(psP[e % 2][:, :], [w[:, e, 0:I] for w in w1], x).then_inc(p_ready, 1)
                product(psG[e % 2][:, :], [w[:, e, I:2 * I] for w in w1], x).then_inc(g_ready, 1)

            def share_out(c, par, e):
                if e < E:
                    if e == 0:
                        pe.wait_ge(partsT_ready, c + 2)
                    pe.wait_ge(scaled_ready, c * E + e + 1)
                    pe.matmul(psC[:, :], k.spread[:, e], partsT[:, par], start=True, stop=True).then_inc(c_ready, 1)

            def down(c, e):
                n = c * NE + e
                pe.wait_ge(high_ready, n + 1)
                if e == 0:
                    pe.wait_ge(o_copied, c + 1)
                pe.matmul(psO[:, :], w2[0][:, e], hidden_high[:, e % 2], start=(e == 0), stop=False)
                pe.matmul(psO[:, :], w2[1][:, e], hidden_high[:, e % 2], start=False, stop=False)
                pe.wait_ge(low_ready, n + 3)
                pe.matmul(psO[:, :], w2[0][:, e], hidden_low[:, e % 2], start=False, stop=(e == NE - 1)).then_inc(down_steps, 1)

            def turn_out(c):
                pe.wait_ge(o_copied, c + 2)
                for t in range(CT):
                    mm = pe.transpose(psY[:, t * P:(t + 1) * P], oT[:, t * P:(t + 1) * P], k.ident[:, :])
                mm.then_inc(o_turned, 1)

            def body(i, par, last):
                c = i * 2 + par
                for e in range(NE):
                    down(c, e)
                    if e + 2 < NE:
                        share_out(c, par, e + 2)
                    elif not (last and par):
                        share_out(c + 1, 1 - par, e + 2 - NE)
                    if not (last and par):
                        if e == at["turn_xn"]:
                            turn_xn(c + 1)
                        if e == at["route"]:
                            route(c + 1, 1 - par)
                    if after_attention and not last:
                        if e == at["turn_heads"]:
                            turn_heads(c + 2)
                        if e == at["project_heads"]:
                            pe.wait_ge(logit_taken, c + 3)
                            project_heads(c + 2)
                    if not (last and par) and e == at["turn_parts"]:
                        turn_parts(c + 1)
                    if e + 3 < NE:
                        up(c, par, e + 3)
                    elif not (last and par):
                        up(c + 1, 1 - par, e + 3 - NE)
                if after_attention and not last:
                    pe.wait_ge(y_taken, c + 4)
                turn_out(c)

            if after_attention:
                turn_heads(0)
                project_heads(0)
                pe.wait_ge(y_taken, 2)
            turn_xn(0)
            route(0, 0)
            pe.wait_ge(w_low_ready, 2)
            up(0, 0, 0)
            up(0, 0, 1)
            turn_parts(0)
            share_out(0, 0, 0)
            if after_attention:
                pe.wait_ge(logit_taken, 2)
                turn_heads(1)
                project_heads(1)
                pe.wait_ge(y_taken, 3)
            share_out(0, 0, 1)
            pe.wait_ge(w_low_ready, len(WEIGHTS))
            up(0, 0, 2)
            with pe.Fori(0, LAST) as i:
                body(i, 0, False)
                body(i, 1, False)
            body(LAST, 0, True)
            body(LAST, 1, True)


SSM_UNITS = dict(
    take_stats=0, mix=1, norm=4, mean_square=5, add_out=10,
    norm_root=0, rms_root=5, add_resid=4,
    squares=6, rms_norm=8, take_z=30, gates=5, xT_out=11, channels_out=23, low_out=26, soften=31,
    skip=0, project_out=4, turn=6, convolve=8, lower=19, raise_z=21,
)


class BatchNorms:

    def __init__(self, nc, k, ctx):
        sb = lambda n, s: ctx.enter_context(nc.sbuf_tensor("norms_" + n, s, F32))
        self.k = k
        self.stats, self.moments = sb("stats", [P, TB, 6]), sb("moments", [P, TB, 8])
        self.resid, self.xr = sb("resid", [P, TB, D]), sb("xr", [P, TB, D])
        self.mean, self.var_eps, self.rstd = sb("mean", [P, TB]), sb("var_eps", [P, TB]), sb("rstd", [P, TB])
        self.square_sum, self.ms_eps, self.rrms = sb("square_sum", [P, TB]), sb("ms_eps", [P, TB]), sb("rrms", [P, TB])
        sem = lambda n: ctx.enter_context(nc.semaphore("norms_" + n))
        self.dve_steps, self.var_ready, self.rstd_ready = sem("dve_steps"), sem("var_ready"), sem("rstd_ready")
        self.resid_ready, self.resid_added, self.squared = sem("resid_ready"), sem("resid_added"), sem("squared")
        self.ms_ready, self.rrms_ready, self.xr_ready = sem("ms_ready"), sem("rrms_ready"), sem("xr_ready")
        self.turned = sem("turned")

    def batch(self, b):
        return self.k.x[:, ds(b * S, S)].rearrange("p (t d) -> p t d", d=D)

    def take_stats(self, dve, c):
        step = Chain(dve, self.dve_steps, TB + NORM_STEPS, c)
        for j in range(TB):
            step.did(dve.bn_stats(self.stats[:, j], self.k.x[:, ds((c * TB + j) * D, D)]))
        step.wait()
        gather_stats(dve, step, self.stats, self.moments, self.mean, self.var_eps[:, :]).then_inc(self.var_ready, 1)
        step.end()

    def norm(self, dve, c):
        dve.wait_ge(self.rstd_ready, c + 1)
        dve.wait_ge(self.resid_added, c)
        dve.wait_ge(self.xr_ready, c * TB)
        for j in range(TB):
            dve.tensor_scalar(self.resid[:, j], self.k.x[:, ds((c * TB + j) * D, D)], self.mean[:, j:j + 1],
                              self.rstd[:, j:j + 1], ALU.subtract, ALU.mult).then_inc(self.resid_ready, 1)

    def mean_square(self, dve, c):
        dve.wait_ge(self.squared, (c + 1) * TB)
        dve.tensor_scalar(self.ms_eps[:, :], self.square_sum[:, :], 1.0 / D, LN_EPS, ALU.mult, ALU.add).then_inc(self.ms_ready, 1)

    def norm_root(self, pool, c):
        pool.wait_ge(self.var_ready, c + 1)
        pool.tensor_tensor(self.rstd[:, :], self.var_eps[:, :], self.k.minus_half[:, 0:TB], ALU.pow).then_inc(self.rstd_ready, 1)

    def add_resid(self, pool, c):
        pool.wait_ge(self.resid_ready, (c + 1) * TB)
        pool.tensor_tensor(self.batch(c), self.batch(c), self.resid[:, :, :], ALU.add).then_inc(self.resid_added, 1)

    def rms_root(self, pool, c):
        pool.wait_ge(self.ms_ready, c + 1)
        pool.tensor_tensor(self.rrms[:, :], self.ms_eps[:, :], self.k.minus_half[:, 0:TB], ALU.pow).then_inc(self.rrms_ready, 1)

    def squares(self, act, c):
        act.wait_ge(self.turned, c)
        act.wait_ge(self.resid_ready, (c + 1) * TB)
        for j in range(TB):
            act.activation(self.xr[:, j], self.resid[:, j], ACT.Square, accum_out=self.square_sum[:, j:j + 1]).then_inc(self.squared, 1)

    def rms_norm(self, act, c):
        act.wait_ge(self.rrms_ready, c + 1)
        act.wait_ge(self.squared, (c + 1) * TB)
        for j in range(TB):
            act.mul(self.xr[:, j], self.resid[:, j], self.rrms[:, j:j + 1]).then_inc(self.xr_ready, 1)


def state_space(nc, k, norms):
    with ExitStack() as ctx:
        sb = lambda n, s, d=F32: ctx.enter_context(nc.sbuf_tensor("ssm_" + n, s, d))
        sem = lambda n: ctx.enter_context(nc.semaphore("ssm_" + n))
        RING, ROWS = 3, 4
        PARTS_OUT = 4
        FREE = ROWS * MT
        PAD = 4
        xT = sb("xT", [P, PAD + S])
        gate = sb("gate", [P, MT, S])
        xs = sb("xs", [P, 2, MT, S])
        low = sb("low", [MR + 2 * MN, S])
        z = sb("z", [P, MT, S])
        soft = sb("soft", [P, MT, S])
        delta = sb("delta", [P, MT, S])
        dx = sb("dx", [P, MT, S])
        b_all = sb("b_all", [P, ROWS, S])
        c_all = sb("c_all", [P, ROWS, S])
        decay = sb("decay", [P, RING, S])
        feed = sb("feed", [P, RING, S])
        state = sb("state", [P, RING, S])
        part = sb("part", [P, PARTS_OUT, S])
        conv_in = k.conv_w
        neg_a = sb("neg_a", [P, MT, MN])
        psY = ctx.enter_context(nc.psum_tensor("ssm_psY", [P, MT, S], F32))
        ps = [ctx.enter_context(nc.psum_tensor(f"ssm_ps{j}", [P, S], F32)) for j in range(2)]
        made_ready, exp_a = sem("made_ready"), sem("exp_a")
        turned, xT_ready = norms.turned, sem("xT_ready")
        skip_done, gate_ready = sem("skip_done"), sem("gate_ready")
        conv_done, xs_ready = sem("conv_done"), sem("xs_ready")
        low_done, low_ready = sem("low_done"), sem("low_ready")
        bc_stored = sem("bc_stored")
        z_done, z_ready, abs_ready, exp_ready, log_ready = sem("z_done"), sem("z_ready"), sem("abs_ready"), sem("exp_ready"), sem("log_ready")
        delta_ready, dx_ready = sem("delta_ready"), sem("dx_ready")
        b_loaded, c_loaded = ([sem(f"{r}_loaded{n}") for n in range(ROWS)] for r in "bc")
        decay_ready, feed_ready, state_ready, part_ready = sem("decay_ready"), sem("feed_ready"), sem("state_ready"), sem("part_ready")
        summed = sem("summed")
        skipped, y_ready, out_done = sem("skipped"), sem("y_ready"), sem("out_done")
        batch_done = sem("batch_done")
        block = ctx.enter_context(nc.Block())
        halves = [slice(h * HALF, (h + 1) * HALF) for h in range(2)]
        batch = norms.batch

        at = SSM_UNITS

        def over_batches(eng, body):
            body(0, 0, True, False)
            with eng.Fori(0, (B - 2) // 2) as i:
                body(i * 2 + 1, 1, False, False)
                body(i * 2 + 2, 0, False, False)
            body(B - 1, 1, False, True)

        def ring_free(b, u):
            return b * UNITS + max(u + 1, RING if u else UNITS % RING)

        @block.sync
        def _(sp):
            with sp.Fori(0, B) as b:
                sp.wait_ge(low_ready, b + 1)
                sp.dma_start(k.bc_rows[ds(b, 1)].rearrange("o r s -> (o r) s"), low[MR:, :]).then_inc(bc_stored, 16)
                sp.wait_ge(bc_stored, b * 16 + 16)
                for n in range(MN):
                    sp.wait_ge(feed_ready, b * UNITS + (n + 1) * MT)
                    sp.dma_start(b_all[:, n % ROWS], k.bc_rows[ds(b, 1), n, :].broadcast_to([P, S])).then_inc(b_loaded[n % ROWS], 16)
                    sp.wait_ge(part_ready, b * UNITS + (n + 1) * MT)
                    sp.dma_start(c_all[:, n % ROWS], k.bc_rows[ds(b, 1), MN + n, :].broadcast_to([P, S])).then_inc(c_loaded[n % ROWS], 16)

        @block.gpsimd
        def _(pool):
            pool.wait_ge(k.consts_loaded, k.consts_total)

            def body(b, par, first, last):
                for u in range(UNITS):
                    n, et, m = u // MT, u % MT, b * UNITS + u
                    if et == 0:
                        pool.wait_ge(c_loaded[n % ROWS], (b * (MN // ROWS) + n // ROWS + 1) * 16)
                    pool.wait_ge(state_ready, RING + m + 1)
                    pool.wait_ge(summed, m + 1)
                    pool.tensor_tensor(part[:, u % PARTS_OUT], state[:, u % RING], c_all[:, n % ROWS], ALU.mult).then_inc(part_ready, 1)
                    if last:
                        continue
                    if not first:
                        if u == at["norm_root"]:
                            norms.norm_root(pool, b + 1)
                        if u == at["rms_root"]:
                            norms.rms_root(pool, b + 1)
                        if u == at["add_resid"]:
                            norms.add_resid(pool, b + 1)

            norms.norm_root(pool, 1)
            norms.add_resid(pool, 1)
            norms.rms_root(pool, 1)
            over_batches(pool, body)

        @block.scalar
        def _(act):
            act.wait_ge(k.ssm_weights_loaded, k.ssm_weights_total)
            act.activation(neg_a[:, :, :], k.a_log[:, :, :], ACT.Exp).then_inc(exp_a, 1)
            act.wait_ge(made_ready, MC + 2)

            def xT_out(c):
                act.wait_ge(turned, c + 1)
                act.wait_ge(skip_done, c * MT)
                act.mul(xT[:, PAD:], ps[0][:, :], k.norm_w[:, 0:1]).then_inc(xT_ready, 1)

            def gates(b):
                act.wait_ge(y_ready, (b + 1) * MT)
                for et in range(MT):
                    act.wait_ge(skip_done, b * MT + et + 1)
                    act.activation(gate[:, et], ps[et][:, :], ACT.Silu).then_inc(gate_ready, 1)

            def channels_out(c, par):
                act.wait_ge(skipped, c * MT)
                for et in range(MT):
                    act.wait_ge(conv_done, c * MT + et + 1)
                    act.activation(xs[:, par, et], ps[1 - et][:, :], ACT.Silu, bias=k.conv_b[:, et:et + 1]).then_inc(xs_ready, 1)

            def low_out(c):
                act.wait_ge(low_done, c + 1)
                act.wait_ge(bc_stored, c * 16)
                act.copy(low[:, :], ps[1][0:MR + 2 * MN, :]).then_inc(low_ready, 1)

            def take_z(c):
                act.wait_ge(delta_ready, c * MT)
                act.wait_ge(batch_done, c)
                for et in range(MT):
                    act.wait_ge(z_done, c * MT + et + 1)
                    act.activation(soft[:, et], ps[et][:, :], ACT.Abs, bias=k.wd2_b[:, et:et + 1]).then_inc(abs_ready, 1)
                    act.activation(z[:, et], ps[et][:, :], ACT.Relu, bias=k.wd2_b[:, et:et + 1]).then_inc(z_ready, 1)

            def soften(c):
                act.wait_ge(abs_ready, (c + 1) * MT)
                act.activation(soft[:, :, :], soft[:, :, :], ACT.Exp, scale=-1.0).then_inc(exp_ready, 1)
                act.wait_ge(exp_ready, c + 1)
                act.activation(soft[:, :, :], soft[:, :, :], ACT.Ln, bias=1.0).then_inc(log_ready, 1)

            def body(b, par, first, last):
                for u in range(UNITS):
                    n, et, m = u // MT, u % MT, b * UNITS + u
                    if u < MT:
                        act.wait_ge(delta_ready, b * MT + et + 1)
                    act.wait_ge(state_ready, ring_free(b, u))
                    act.activation(decay[:, u % RING], delta[:, et], ACT.Exp, scale=neg_a[:, et, n:n + 1]).then_inc(decay_ready, 1)
                    if u == at["gates"]:
                        gates(b)
                    if last:
                        continue
                    if u == at["squares"] and not first:
                        norms.squares(act, b + 1)
                    if u == at["xT_out"]:
                        xT_out(b + 1)
                    if u == at["channels_out"]:
                        channels_out(b + 1, 1 - par)
                    if u == at["low_out"]:
                        low_out(b + 1)
                    if u == at["rms_norm"] and not first:
                        norms.rms_norm(act, b + 1)
                    if u == at["take_z"]:
                        take_z(b + 1)
                    if u == at["soften"]:
                        soften(b + 1)

            xT_out(0)
            norms.squares(act, 1)
            norms.rms_norm(act, 1)
            channels_out(0, 0)
            low_out(0)
            take_z(0)
            soften(0)
            over_batches(act, body)

        @block.vector
        def _(dve):
            for b in range(B):
                dve.wait_ge(k.x_loaded[b], 16)
            dve.wait_ge(k.ssm_weights_loaded, k.ssm_weights_total)
            for t in range(MC):
                dve.tensor_tensor(conv_in[:, t], k.in_w[:, :], k.conv_w[:, t], ALU.mult).then_inc(made_ready, 1)
            dve.memset(xT[:, 0:PAD], 0.0).then_inc(made_ready, 1)
            dve.wait_ge(exp_a, 1)
            dve.tensor_scalar(neg_a[:, :, :], neg_a[:, :, :], -1.0, None, ALU.mult).then_inc(made_ready, 1)

            def make_delta(c, par):
                dve.wait_ge(log_ready, c + 1)
                for et in range(MT):
                    dve.tensor_tensor(delta[:, et], z[:, et], soft[:, et], ALU.add).then_inc(delta_ready, 1)
                for et in range(MT):
                    dve.wait_ge(delta_ready, c * MT + et + 1)
                    dve.tensor_tensor(dx[:, et], delta[:, et], xs[:, par, et], ALU.mult).then_inc(dx_ready, 1)

            def mix(f, par):
                dve.wait_ge(summed, PARTS_OUT + (f + 1) * UNITS)
                for et in range(MT):
                    dve.scalar_tensor_tensor(out=z[:, et], in0=xs[:, par, et], scalar=k.w_d[:, et:et + 1], in1=psY[:, et],
                                             op0=ALU.mult, op1=ALU.add).then_inc(skipped, 1)
                for et in range(MT):
                    dve.wait_ge(skipped, (f + 1) * MT + et + 1)
                    dve.tensor_tensor(z[:, et], z[:, et], gate[:, et], ALU.mult).then_inc(y_ready, 1)

            def add_out(f):
                dve.wait_ge(out_done, f + 1)
                dve.wait_ge(norms.resid_added, f + 1)
                dve.tensor_tensor(batch(f), batch(f), ps[1][:, :].rearrange("p (t d) -> p t d", d=D), ALU.add).then_inc(batch_done, 1)

            def feed_unit(b, u):
                n, et = u // MT, u % MT
                if u < MT:
                    dve.wait_ge(dx_ready, b * MT + et + 1)
                if et == 0:
                    dve.wait_ge(b_loaded[n % ROWS], (b * (MN // ROWS) + n // ROWS + 1) * 16)
                dve.wait_ge(state_ready, ring_free(b, u))
                dve.tensor_tensor(feed[:, u % RING], dx[:, et], b_all[:, n % ROWS], ALU.mult).then_inc(feed_ready, 1)

            def body(b, par, first, last):
                feed_unit(b, 0)
                for u in range(UNITS):
                    et, m = u % MT, b * UNITS + u
                    if u + 1 < UNITS:
                        feed_unit(b, u + 1)
                    dve.wait_ge(feed_ready, FREE + m + 1)
                    dve.wait_ge(decay_ready, m + 1)
                    dve.wait_ge(part_ready, FREE + ring_free(b, u) - RING)
                    dve.tensor_tensor_scan(state[:, u % RING], decay[:, u % RING], feed[:, u % RING], 0.0, ALU.mult, ALU.add).then_inc(state_ready, 1)
                    if not first:
                        if u == at["mix"]:
                            mix(b - 1, 1 - par)
                        if u == at["add_out"]:
                            add_out(b - 1)
                    if last:
                        continue
                    if u == at["take_stats"] and not first:
                        norms.take_stats(dve, b + 1)
                    if u == at["norm"] and not first:
                        norms.norm(dve, b + 1)
                    if u == at["mean_square"] and not first:
                        norms.mean_square(dve, b + 1)
                if not last:
                    make_delta(b + 1, 1 - par)

            norms.take_stats(dve, 1)
            norms.norm(dve, 1)
            norms.mean_square(dve, 1)
            make_delta(0, 0)
            over_batches(dve, body)
            mix(B - 1, 1)
            add_out(B - 1)

        @block.tensor
        def _(pe):
            pe.wait_ge(made_ready, MC + 2)
            pe.wait_ge(k.consts_loaded, k.consts_total)
            pe.wait_ge(k.ssm_weights_loaded, k.ssm_weights_total)
            for s, n in ((state_ready, RING), (part_ready, FREE), (feed_ready, FREE), (summed, PARTS_OUT),
                         (batch_done, 1), (skipped, MT), (y_ready, MT)):
                pe.sem_inc(s, n)

            def product(out, rows, cols, w, src):
                for j in range(len(w)):
                    mm = pe.matmul(out[0:rows, cols], w[j], src(j, cols), start=(j == 0), stop=(j == len(w) - 1))
                return mm

            shift = lambda t: lambda j, cols: xT[:, PAD + t + j + cols.start:PAD + t + j + cols.stop]
            channels = [slice(et * P, (et + 1) * P) for et in range(MT)]

            def turn(c):
                pe.wait_ge(norms.xr_ready, (c + 1) * TB)
                for j in range(TB):
                    mm = pe.transpose(ps[0][:, j * P:(j + 1) * P], norms.xr[:, j], k.ident[:, :])
                mm.then_inc(turned, 1)

            def skip(b, et):
                pe.wait_ge(z_ready, (b + 1) * MT)
                for cols in halves:
                    mm = product(ps[et], P, cols, [k.skip_w[:, channels[et]]], shift(0))
                mm.then_inc(skip_done, 1)

            def convolve(c, et, h):
                if et == 0 and h == 0:
                    pe.wait_ge(xT_ready, c + 1)
                    pe.wait_ge(batch_done, c)
                mm = product(ps[1 - et], P, halves[h], [conv_in[:, t, channels[et]] for t in range(MC)], shift(1 - MC))
                if h == 1:
                    mm.then_inc(conv_done, 1)

            def lower(c, par, h):
                pe.wait_ge(xs_ready, (c + 1) * MT)
                mm = product(ps[1], MR + 2 * MN, halves[h], [k.w_low[:, et] for et in range(MT)],
                             lambda j, cols: xs[:, par, j, cols])
                if h == 1:
                    mm.then_inc(low_done, 1)

            def raise_z(c, et):
                pe.wait_ge(low_ready, c + 1)
                for cols in halves:
                    mm = product(ps[et], P, cols, [k.wd2[0:MR + 2 * MN, channels[et]]], lambda j, cols: low[:, cols])
                mm.then_inc(z_done, 1)

            def project_out(f, idle):
                pe.wait_ge(y_ready, (f + 2) * MT)
                if not idle:
                    pe.wait_ge(gate_ready, (f + 2) * MT)
                for j in range(TB):
                    cols = slice(j * P, (j + 1) * P)
                    for et in range(MT):
                        mm = pe.matmul(ps[1][:, cols], z[:, et, cols], k.out_w[:, et], start=(et == 0), stop=(et == MT - 1))
                mm.then_inc(out_done, 1)

            def body(b, par, first, last):
                for u in range(UNITS):
                    n, et, m = u // MT, u % MT, b * UNITS + u
                    if n == 0:
                        pe.wait_ge(skipped, b * MT + et + 1)
                    pe.wait_ge(part_ready, FREE + m + 1)
                    for cols in halves:
                        mm = pe.matmul(psY[:, et, cols], k.ident[:, :], part[:, u % PARTS_OUT, cols], start=(n == 0), stop=(n == MN - 1))
                    mm.then_inc(summed, 1)
                    if u - at["skip"] in range(MT):
                        skip(b, u - at["skip"])
                    if not first and u == at["project_out"]:
                        project_out(b - 1, False)
                    if last:
                        continue
                    if u == at["turn"]:
                        turn(b + 1)
                    if u - at["convolve"] in range(0, 4 * MT, 2):
                        convolve(b + 1, (u - at["convolve"]) // 4, (u - at["convolve"]) // 2 % 2)
                    if u - at["lower"] in range(2):
                        lower(b + 1, 1 - par, u - at["lower"])
                    if u - at["raise_z"] in range(MT):
                        raise_z(b + 1, u - at["raise_z"])

            turn(0)
            for et in range(MT):
                for h in range(2):
                    convolve(0, et, h)
            lower(0, 0, 0)
            lower(0, 0, 1)
            raise_z(0, 0)
            raise_z(0, 1)
            over_batches(pe, body)
            project_out(B - 1, True)
def build_program(nc, a, out):
    with ExitStack() as ctx:
        sb = lambda n, s, d=F32: ctx.enter_context(nc.sbuf_tensor(n, s, d))
        sem = lambda n: ctx.enter_context(nc.semaphore(n))
        k = Names()
        k.x = sb("x", [P, B * S])
        w_qkv = sb("w_qkv", [P, 3, D])
        k.w_q, k.w_k, k.w_v = (w_qkv[:, j] for j in range(3))
        k.w_out = sb("w_out", [P, D])
        k.b_out, k.gamma, k.beta = sb("b_out", [P, D]), sb("gamma", [P, D]), sb("beta", [P, D])
        k.ident = sb("ident", [P, P])
        k.minus_half = sb("minus_half", [P, B * TB])
        k.before = sb("before", [P, E * E])
        k.ident_b = sb("ident_b", [P, P], BF16)
        k.spread = sb("spread", [P, E, P], BF16)
        k.w_router = sb("w_router", [P, E])
        k.w1 = sb("w1", [P, NE, 2 * I])
        k.w2 = sb("w2", [P, NE, D])
        k.norm_w = sb("norm_w", [P, 1])
        k.skip_w, k.in_w = sb("skip_w", [P, ME]), sb("in_w", [P, ME])
        k.conv_w = sb("conv_w", [P, MC, ME])
        k.conv_b, k.wd2_b, k.w_d = sb("conv_b", [P, MT]), sb("wd2_b", [P, MT]), sb("w_d", [P, MT])
        k.w_low, k.wd2 = sb("w_low", [P, MT, MR + 2 * MN]), sb("wd2", [P, ME])
        k.a_log, k.out_w = sb("a_log", [P, MT, MN]), sb("out_w", [P, MT, D])
        k.bc_rows = nc.dram_tensor("bc_rows", [B, 2 * MN, S], F32, kind="Internal").ap()
        k.ssm_weights_loaded = sem("ssm_weights_loaded")
        k.q_terms = nc.dram_tensor("q_terms", [B, H, HD, NT, S], BF16, kind="Internal").ap()
        k.k_terms = nc.dram_tensor("k_terms", [B, H, HD, NT, S], BF16, kind="Internal").ap()
        k.x_loaded, k.consts_loaded = [sem(f"x_loaded{b}") for b in range(B)], sem("consts_loaded")
        k.attn_weights_loaded, k.ffn_weights_loaded = sem("attn_weights_loaded"), sem("ffn_weights_loaded")
        k.stored = sem("out_stored")
        k.spread_loaded = sem("spread_loaded")

        k.parts_stored = [sem("parts_stored0"), sem("parts_stored1")]
        k.zeroed, k.qk_loaded = sem("zeroed"), [sem("qk_loaded0"), sem("qk_loaded1")]

        def load_later_weights(sp):
            tiles = lambda name: a[name].rearrange("(t p) c -> p t c", p=P)
            sp.dma_start(k.spread_f[:, :], a["spread"]).then_inc(k.spread_loaded, 16)
            for dst, src in ((k.w_out[:, :], a["w_out"]), (k.w_router[:, :], a["w_router"]),
                             (k.w1[:, 0:E], a["fc1"].rearrange("e d f -> d e f")),
                             (k.w1[:, E:NE, 0:I], a["gate_w"].rearrange("d (s f) -> d s f", s=2)),
                             (k.w1[:, E:NE, I:2 * I], a["up_w"].rearrange("d (s f) -> d s f", s=2)),
                             (k.w2[:, 0:E], a["fc2"].rearrange("e i d -> i e d")),
                             (k.w2[:, E:NE], a["down_w"].rearrange("(s i) d -> i s d", s=2))):
                sp.dma_start(dst, src).then_inc(k.ffn_weights_loaded, 16)
            sp.wait_ge(k.zeroed, 3)
            for dst, src in ((k.norm_w[:, :], a["norm_w"]), (k.skip_w[:, :], a["skip_w"]), (k.in_w[:, :], a["in_w"]),
                             (k.conv_w[:, :, :], a["conv_w"].unsqueeze(0).broadcast_to([P, MC, ME])),
                             (k.w_low[:, :, 0:MR], tiles("wd1")), (k.wd2[0:MR, :], a["wd2"]),
                             (k.w_low[:, :, MR:MR + MN], tiles("wb")), (k.w_low[:, :, MR + MN:], tiles("wc")),
                             (k.a_log[:, :, :], tiles("A_log")), (k.out_w[:, :, :], tiles("out_w")),
                             (k.conv_b[:, :], a["conv_b"]), (k.wd2_b[:, :], a["wd2_b"]), (k.w_d[:, :], a["W_D"])):
                sp.dma_start(dst, src).then_inc(k.ssm_weights_loaded, 16)

        k.load_later_weights = load_later_weights
        k.consts_total, k.attn_weights_total, k.ffn_weights_total = 6 * 16, 16, 7 * 16
        k.ssm_weights_total = 13 * 16
        norms = BatchNorms(nc, k, ctx)
        with ExitStack() as attn:
            sa = lambda n: attn.enter_context(nc.sbuf_tensor(n, [P, B * S], F32))
            k.xn = sa("attn_in")
            k.v = sa("v")
            k.att = sa("att")
            k.spread_f = attn.enter_context(nc.sbuf_tensor("spread_f", [P, E * P], F32))
            with ExitStack() as heads:
                k.q_part, k.k_part = (heads.enter_context(nc.sbuf_tensor(n, [P, 2, PARTS, S], BF16)) for n in ("q_part", "k_part"))
                k.q_in = heads.enter_context(nc.sbuf_tensor("q_in", [P, 2, HG // 2, S], BF16))
                k.k_in = heads.enter_context(nc.sbuf_tensor("k_in", [P, 2, HG, S], BF16))
                with nc.Block() as block:
                    @block.sync
                    def _(sp):
                        for b in range(B):
                            src = a["x"][b * S:(b + 1) * S].rearrange("(t p) d -> p t d", p=P)
                            sp.dma_start(k.x[:, b * S:(b + 1) * S].rearrange("p (t d) -> p t d", d=D), src).then_inc(k.x_loaded[b], 16)

                    @block.gpsimd
                    def _(pool):
                        pool.memset(k.k_in[:, :, :, :], 0.0).then_inc(k.zeroed, 1)
                        pool.memset(k.wd2[:, :], 0.0).then_inc(k.zeroed, 1)

                    @block.vector
                    def _(dve):
                        dve.memset(k.q_in[:, :, :, :], 0.0).then_inc(k.zeroed, 1)

                    @block.scalar
                    def _(act):
                        act.dma_start(k.minus_half[:, :], a["minus_half"]).then_inc(k.consts_loaded, 16)
                        act.dma_start(k.ident[:, :], a["ident"]).then_inc(k.consts_loaded, 16)
                        act.dma_start(w_qkv[:, :, :], a["w_qkv"].rearrange("j d c -> d j c")).then_inc(k.attn_weights_loaded, 16)
                        for dst, name in ((k.b_out, "b_out"), (k.gamma, "gamma"), (k.beta, "beta"), (k.before, "before")):
                            act.dma_start(dst[:, :], a[name].broadcast_to([P, a[name].shape[1]])).then_inc(k.consts_loaded, 16)
                project_qkv(nc, k)
                attend(nc, k)
            feed_forward(nc, k, "ffn1", True, norms=norms)
        state_space(nc, k, norms)
        feed_forward(nc, k, "ffn2", False, out)


def layout(inp):
    import numpy as np
    g = {n.replace("L0_attn_a_", "a_").replace("L0_attn_b_", "b_").replace("L0_ffn_", "f_"): np.asarray(v) for n, v in inp.items()}
    r = {
        "x": g["a_x"].reshape(B * S, D),
        "w_qkv": g["a_w_qkv"].reshape(D, H, 3, HD).transpose(2, 0, 1, 3).reshape(3, D, D),
        "w_out": g["a_w_out"], "b_out": g["a_b_out"].reshape(1, D), "gamma": g["a_gamma"].reshape(1, D),
        "beta": g["a_beta"].reshape(1, D), "norm_w": g["b_norm_w"].reshape(D, 1), "skip_w": g["b_skip_w"].T,
        "in_w": g["b_in_w"].T, "conv_w": g["b_conv_w"].reshape(ME, MC).T, "conv_b": g["b_conv_b"].reshape(MT, P).T,
        "wd1": g["b_wd1"].T, "wd2": g["b_wd2"].T, "wd2_b": g["b_wd2_b"].reshape(MT, P).T,
        "wb": g["b_wb"].T, "wc": g["b_wc"].T, "A_log": g["b_A_log"], "W_D": g["b_W_D"].reshape(MT, P).T,
        "out_w": g["b_out_w"].T, "w_router": g["f_w_router"], "fc1": g["f_fc1_w"], "fc2": g["f_fc2_w"],
        "gate_w": g["f_gate_w"], "up_w": g["f_up_w"], "down_w": g["f_down_w"],
    }
    spread = np.zeros((P, E, P), np.float32)
    for e in range(E):
        for part in range(PARTS):
            spread[part * E + e, e, :] = 1
    r["ident"] = np.eye(P, dtype=np.float32)
    r["spread"] = spread.reshape(P, E * P)
    r["before"] = np.tril(np.ones((E, E), np.float32), -1).reshape(1, E * E)
    r["minus_half"] = np.full((P, B * TB), -0.5, np.float32)
    return {n: np.ascontiguousarray(v) for n, v in r.items()}


def kernel(**inputs):
    import numpy as np
    import concourse.bacc as bacc
    from concourse.bass_utils import run_bass_kernel_spmd as run

    nc = bacc.Bacc("TRN2", target_bir_lowering=False, num_devices=1)
    arrays = {f"in_{n}": v for n, v in layout(inputs).items()}
    a = {n[3:]: nc.dram_tensor(n, v.shape, mybir.dt.from_np(v.dtype), kind="ExternalInput").ap() for n, v in arrays.items()}
    out = nc.dram_tensor("out", (B * S, D), F32, kind="ExternalOutput").ap()
    build_program(nc, a, out)
    r = run(nc, [arrays], core_ids=[0])
    return np.asarray(r.results[0]["out"]).reshape(B, S, D)
```
